# Optimizing a Trainium2 kernel written in Bass

```python
import numpy as np
import jax
import jax.numpy as jnp

def _softmax(x, axis=-1):
    return jax.nn.softmax(x, axis=axis)

def _gelu(x):
    return jax.nn.gelu(x, approximate=True)

def _silu(x):
    return jax.nn.silu(x)

def _sigmoid(x):
    return jax.nn.sigmoid(x)

def _layernorm(x, axis=-1, eps=1e-05):
    m = jnp.mean(x, axis=axis, keepdims=True)
    v = jnp.var(x, axis=axis, keepdims=True)
    return (x - m) / jnp.sqrt(v + eps)

def _scatter_add(tgt, idx, src, axis=0):
    return tgt.at[idx].add(src)

def _segment_sum(src, seg, n):
    return jax.ops.segment_sum(src, seg, n)
kernel_name = 'mk_flamingo_gated_d4_seqx_r8_5b54b5'

def setup_inputs(seed: int=0):
    np.random.seed(seed)
    _w = jnp.asarray

    def _rec_inputs():
        import jax
        import jax.numpy as jnp
        _rk = jax.random.key(seed)
        x = 4.136e-05 + 0.9999 * jax.random.normal(jax.random.fold_in(_rk, 1), (32, 128, 128), jnp.float32)
        _lenS = 128 - jax.random.randint(jax.random.fold_in(_rk, 7), (32,), 0, max(1, 128 // 4) + 1, jnp.int32)
        _lenS2 = 128 - jax.random.randint(jax.random.fold_in(_rk, 8), (32,), 0, max(1, 128 // 4) + 1, jnp.int32)
        _ctx_2048P = jax.random.normal(jax.random.fold_in(_rk, 11), (32, 16, 256), jnp.float32)
        _ctx_2048c = jax.random.dirichlet(jax.random.fold_in(_rk, 511), 0.3 * jnp.ones((16,), jnp.float32), (32, 128))
        _ctx_2048t = jnp.einsum('bsk,bkd->bsd', _ctx_2048c, _ctx_2048P)
        _ctx_2048t = _ctx_2048t * jax.lax.rsqrt(jnp.mean(jnp.square(_ctx_2048t)) + 1e-12) * 0.953939
        ctx_2048 = -0.000392918 + 0.999932 * (_ctx_2048t + 0.3 * jax.random.normal(jax.random.fold_in(_rk, 611), (32, 128, 256), jnp.float32))
        itok_Bx1_68_817 = jax.random.randint(jax.random.fold_in(_rk, 12), (32, 1), 68, 818, jnp.int32)
        _validS = jnp.arange(128)[None, :] < _lenS[:, None]
        _validS2 = jnp.arange(128)[None, :] < _lenS2[:, None]
        _causal = jnp.tril(jnp.ones((128, 128), dtype=bool))
        mask_BxS2_ik0 = jnp.where(jnp.broadcast_to(_validS2[:, :], (32, 128)), 0, 1).astype(jnp.int32)
        mask_BxS2_if0 = jnp.where(jnp.ones((32, 128), dtype=bool), 4, 0).astype(jnp.int32)
        _g = jax.random.normal(jax.random.fold_in(_rk, 9001), (2, 4), jnp.float32)
        _g = jnp.sign(_g) * jnp.maximum(jnp.abs(_g), 1.0) + (_g == 0) * 1.0
        g_xattn = _g[0]
        g_ffn = _g[1]
        return (x, ctx_2048, itok_Bx1_68_817, mask_BxS2_ik0, mask_BxS2_if0, g_xattn, g_ffn)
    x, ctx_2048, itok_Bx1_68_817, mask_BxS2_ik0, mask_BxS2_if0, g_xattn, g_ffn = _rec_inputs()

    def _L0_xattn_setup():
        import jax, jax.numpy as jnp
        import numpy as np
        UNITS = 128
        NUM_HEADS = 16
        MASK_VALUE = -1000000000000.0

        def _split_heads(x, n):
            B, S, D = x.shape
            return x.reshape(B, S, n, D // n).transpose(0, 2, 1, 3)
        key = jax.random.key(seed)
        k1, k2, k3, k4 = jax.random.split(key, 4)
        B, S = (8, 128)
        memory = jax.random.normal(k1, (B, S, 2 * UNITS), dtype=jnp.float32)
        query = jax.random.normal(k2, (B, S, UNITS), dtype=jnp.float32)
        b = jax.random.normal(k3, (S,), dtype=jnp.float32)
        seq_len = jax.random.randint(k4, (B, 1), 0, S, dtype=jnp.int32)
        return {'memory': memory, 'query': query, 'b': b, 'seq_len': seq_len}
    _L0_xattn_all = _L0_xattn_setup()
    _L0_xattn_in = {k: v for k, v in _L0_xattn_all.items() if k in ('b',)}
    del _L0_xattn_all

    def _L0_ffn_setup():
        import jax, jax.numpy as jnp
        import numpy as np
        D_IN, D_HID = (128, 512)

        def _ternary(key, shape):
            return jax.random.randint(key, shape, -1, 2).astype(jnp.float32)

        def _tlin(x, w, s):
            return jnp.einsum('bsi,oi->bso', x, w) * s
        key = jax.random.key(seed)
        ks = jax.random.split(key, 12)
        inv = lambda fan: 1.0 / np.sqrt(fan).astype(np.float32)
        return {'x': jax.random.normal(ks[0], (4, 256, D_IN), dtype=jnp.float32), 'w1_w': _ternary(ks[1], (D_HID, D_IN)), 'w1_s': jax.random.uniform(ks[2], (D_HID,), dtype=jnp.float32) * inv(D_IN), 'w2_w': _ternary(ks[3], (D_HID, D_IN)), 'w2_s': jax.random.uniform(ks[4], (D_HID,), dtype=jnp.float32) * inv(D_IN), 'h1_w': _ternary(ks[5], (D_HID, D_HID)), 'h1_s': jax.random.uniform(ks[6], (D_HID,), dtype=jnp.float32) * inv(D_HID), 'h2_w': _ternary(ks[7], (D_HID, D_HID)), 'h2_s': jax.random.uniform(ks[8], (D_HID,), dtype=jnp.float32) * inv(D_HID), 'w3_w': _ternary(ks[9], (D_IN, D_HID)), 'w3_s': jax.random.uniform(ks[10], (D_IN,), dtype=jnp.float32) * inv(D_HID)}
    _L0_ffn_all = _L0_ffn_setup()
    _L0_ffn_in = {k: v for k, v in _L0_ffn_all.items() if k in ('w1_w', 'w1_s', 'w2_w', 'w2_s', 'h1_w', 'h1_s', 'h2_w', 'h2_s', 'w3_w', 'w3_s')}
    del _L0_ffn_all

    def _L1_xattn_setup():
        import jax, jax.numpy as jnp
        import numpy as np
        NUM_HEADS = 16
        key = jax.random.key(seed)
        ks = jax.random.split(key, 5)
        dim = 128
        B, N, N_c = (4, 128, 32)
        x = jax.random.normal(ks[0], (B, N, dim), dtype=jnp.float32)
        context = jax.random.normal(ks[1], (B, N_c, 2 * dim), dtype=jnp.float32)
        w_qkv = jax.random.normal(ks[2], (3 * dim, dim), dtype=jnp.float32) * 0.02
        w_proj = jax.random.normal(ks[3], (dim, dim), dtype=jnp.float32) * 0.02
        b_proj = jax.random.normal(ks[4], (dim,), dtype=jnp.float32) * 0.02
        return {'x': x, 'context': context, 'w_qkv': w_qkv, 'w_proj': w_proj, 'b_proj': b_proj}
    _L1_xattn_all = _L1_xattn_setup()
    _L1_xattn_in = {k: v for k, v in _L1_xattn_all.items() if k in ('w_qkv', 'w_proj', 'b_proj')}
    del _L1_xattn_all

    def _L1_ffn_setup():
        import jax, jax.numpy as jnp
        import numpy as np
        B, S, D = (2, 128, 128)
        L, H = (64, 16)
        HD = L // H
        F, E, K = (256, 8, 2)
        THETA = 10000.0
        EPS = 1e-05

        def _rmsnorm(x, g):
            return x * g * jax.lax.rsqrt(jnp.mean(x * x, axis=-1, keepdims=True) + EPS)

        def _rope(t, pos):
            inv_freq = 1.0 / THETA ** (jnp.arange(0, HD, 2, dtype=jnp.float32) / HD)
            ang = pos[:, None].astype(jnp.float32) * inv_freq[None, :]
            cos, sin = (jnp.cos(ang), jnp.sin(ang))
            t1, t2 = (t[..., 0::2], t[..., 1::2])
            r1 = t1 * cos - t2 * sin
            r2 = t1 * sin + t2 * cos
            return jnp.stack([r1, r2], axis=-1).reshape(t.shape)

        def _forward(x, g1, g2, w_down, wq, wk, wv, w_up, router_w, w1, w2, w3):
            b, s, _ = x.shape
            pos = jnp.arange(s)
            h = _rmsnorm(x, g1)
            c = h @ w_down
            split = lambda t: t.reshape(b, s, H, HD).transpose(0, 2, 1, 3)
            q = _rope(split(c @ wq), pos)
            k = _rope(split(c @ wk), pos)
            v = split(c @ wv)
            scores = jnp.einsum('bhqd,bhkd->bhqk', q, k) / jnp.sqrt(jnp.float32(HD))
            causal = jnp.tril(jnp.ones((s, s), bool))
            scores = jnp.where(causal, scores, -jnp.inf)
            attn = jax.nn.softmax(scores, axis=-1)
            o = jnp.einsum('bhqk,bhkd->bhqd', attn, v).transpose(0, 2, 1, 3).reshape(b, s, L)
            x = x + o @ w_up
            res = x
            t = _rmsnorm(x, g2).reshape(-1, D)
            probs = jax.nn.softmax(t @ router_w, axis=-1)
            vals, idx = jax.lax.top_k(probs, K)
            w = vals / jnp.sum(vals, axis=-1, keepdims=True)
            gate = jnp.sum(jax.nn.one_hot(idx, E, dtype=t.dtype) * w[..., None], axis=1)
            hid = jax.nn.silu(jnp.einsum('td,edf->tef', t, w1)) * jnp.einsum('td,edf->tef', t, w3)
            y_e = jnp.einsum('tef,efd->ted', hid, w2)
            y = jnp.einsum('ted,te->td', y_e, gate)
            return res + y.reshape(b, s, D)
        key = jax.random.key(seed)
        ks = jax.random.split(key, 12)
        g = lambda k, shape, scale: jax.random.normal(k, shape, dtype=jnp.float32) * scale
        return {'x': g(ks[0], (B, S, D), 1.0), 'g1': jnp.ones((D,), jnp.float32), 'g2': jnp.ones((D,), jnp.float32), 'w_down': g(ks[1], (D, L), 0.02), 'wq': g(ks[2], (L, L), 0.02), 'wk': g(ks[3], (L, L), 0.02), 'wv': g(ks[4], (L, L), 0.02), 'w_up': g(ks[5], (L, D), 0.02), 'router_w': g(ks[6], (D, E), 0.02), 'w1': g(ks[7], (E, D, F), 0.02), 'w3': g(ks[8], (E, D, F), 0.02), 'w2': g(ks[9], (E, F, D), 0.02)}
    _L1_ffn_all = _L1_ffn_setup()
    _L1_ffn_in = {k: v for k, v in _L1_ffn_all.items() if k in ('g1', 'g2', 'w_down', 'wq', 'wk', 'wv', 'w_up', 'router_w', 'w1', 'w2', 'w3')}
    del _L1_ffn_all

    def _L2_xattn_setup():
        import jax, jax.numpy as jnp
        import numpy as np
        UNITS = 128
        NUM_HEADS = 8

        def _split_heads(x, n):
            B, S, D = x.shape
            return x.reshape(B, S, n, D // n).transpose(0, 2, 1, 3)
        key = jax.random.key(seed)
        k1, k2, k3 = jax.random.split(key, 3)
        B, S = (8, 128)
        memory = jax.random.normal(k1, (B, S, 2 * UNITS), dtype=jnp.float32)
        query = jax.random.normal(k2, (B, S, UNITS), dtype=jnp.float32)
        seq_mask = jax.random.randint(k3, (B, S), 0, 2, dtype=jnp.int32)
        b = jnp.zeros((1,), dtype=jnp.float32)
        return {'memory': memory, 'query': query, 'seq_mask': seq_mask, 'b': b}
    _L2_xattn_all = _L2_xattn_setup()
    _L2_xattn_in = {k: v for k, v in _L2_xattn_all.items() if k in ('b',)}
    del _L2_xattn_all

    def _L2_ffn_setup():
        import jax, jax.numpy as jnp
        import numpy as np
        D = 128
        E = 8
        K = 2
        DF = 512
        B, S = (2, 256)
        EPS_LN = 1e-05
        EPS_TOPK = 1e-08

        def _xavier(key, shape, fan_in, fan_out, dtype=jnp.float32):
            bound = float(np.sqrt(6.0 / (fan_in + fan_out)))
            return jax.random.uniform(key, shape, dtype, -bound, bound)
        key = jax.random.key(seed)
        kx, kg, k1, k2 = jax.random.split(key, 4)
        return {'x': jax.random.normal(kx, (B, S, D), jnp.float32), 'gamma': jnp.ones((D,), jnp.float32), 'beta': jnp.zeros((D,), jnp.float32), 'Wg': _xavier(kg, (E, D), D, E), 'bg': jnp.zeros((E,), jnp.float32), 'W1': _xavier(k1, (E, DF, D), D, DF), 'b1': jnp.zeros((E, DF), jnp.float32), 'W2': _xavier(k2, (E, D, DF), DF, D), 'b2': jnp.zeros((E, D), jnp.float32)}
    _L2_ffn_all = _L2_ffn_setup()
    _L2_ffn_in = {k: v for k, v in _L2_ffn_all.items() if k in ('gamma', 'beta', 'Wg', 'bg', 'W1', 'b1', 'W2', 'b2')}
    del _L2_ffn_all

    def _L3_xattn_setup():
        import jax, jax.numpy as jnp
        import numpy as np
        B, L, P = (4, 512, 128)
        D_MODEL = 128
        D_GLOBAL = 256
        HEADDIM = 32
        EPSILON = 0.001
        RMS_EPS = 1e-05

        def rmsnorm(x, g, eps=RMS_EPS):
            var = jnp.mean(jnp.square(x), axis=-1, keepdims=True)
            return x * jax.lax.rsqrt(var + eps) * g

        def _hnet_depool(h, h_patch_full, patch_lens):
            h_patch = h_patch_full[..., :D_MODEL]
            bsz, plen = (h_patch.shape[0], h_patch.shape[1])
            seqlen = h.shape[1]
            logp = jnp.full((bsz, plen), -EPSILON, dtype=jnp.float32)
            bidx = jnp.cumsum(patch_lens, axis=1) - 1
            boundary_mask = jnp.zeros((bsz, seqlen), dtype=jnp.int32)
            boundary_mask = boundary_mask.at[jnp.arange(bsz)[:, None], bidx].set(1)
            dt = (-jnp.log(-jnp.expm1(logp))).astype(h_patch.dtype)
            x = h_patch / dt[..., None]
            n_heads = D_MODEL // HEADDIM
            A = -jnp.ones((n_heads,), dtype=jnp.float32)
            bcoef = jnp.exp(logp).astype(h_patch.dtype)
            x4 = x.reshape(bsz, plen, n_heads, HEADDIM)
            a = jnp.exp(dt[:, :, None] * A[None, None, :])
            u = (dt * bcoef)[:, :, None, None] * x4
            a_b = jnp.broadcast_to(a[..., None], u.shape)

            def comb(lft, rgt):
                aL, uL = lft
                aR, uR = rgt
                return (aL * aR, uL * aR + uR)
            _, s = jax.lax.associative_scan(comb, (a_b, u), axis=1)
            depool = s.reshape(bsz, plen, D_MODEL)
            plug = jnp.clip(jnp.cumsum(boundary_mask, axis=1) - 1, 0, plen - 1)
            depool_out = depool[jnp.arange(bsz)[:, None], plug]
            return depool_out + h
        key = jax.random.key(seed)
        k1, k2, k3, k4 = jax.random.split(key, 4)
        embeds = jax.random.normal(k1, (B, L, D_MODEL), dtype=jnp.float32)
        patch_embeds = jax.random.normal(k2, (B, P, D_GLOBAL), dtype=jnp.float32)
        patch_lens = jnp.full((B, P), L // P, dtype=jnp.int64)
        W_in = jax.random.normal(k3, (D_MODEL, D_MODEL), dtype=jnp.float32) * 0.02
        b_in = jnp.zeros((D_MODEL,), dtype=jnp.float32)
        g_res = jnp.ones((D_MODEL,), dtype=jnp.float32)
        g_init = jnp.ones((D_GLOBAL,), dtype=jnp.float32)
        return {'embeds': embeds, 'patch_embeds': patch_embeds, 'patch_lens': patch_lens, 'W_in': W_in, 'b_in': b_in, 'g_res': g_res, 'g_init': g_init}
    _L3_xattn_all = _L3_xattn_setup()
    _L3_xattn_in = {k: v for k, v in _L3_xattn_all.items() if k in ('W_in', 'b_in', 'g_res', 'g_init')}
    del _L3_xattn_all

    def _L3_ffn_setup():
        import jax, jax.numpy as jnp
        import numpy as np
        HIDDEN = 128
        INNER = 512

        def _weight_quant(w):
            scale = 1.0 / jnp.clip(jnp.mean(jnp.abs(w)), 1e-05)
            wq = jnp.clip(jnp.round(w * scale), -1.0, 1.0) / scale
            return w + jax.lax.stop_gradient(wq - w)

        def _act_quant(x):
            scale = 127.0 / jnp.clip(jnp.max(jnp.abs(x), axis=-1, keepdims=True), 1e-05)
            xq = jnp.clip(jnp.round(x * scale), -128.0, 127.0) / scale
            return x + jax.lax.stop_gradient(xq - x)

        def _bitlinear(x, w):
            return jnp.einsum('bsi,oi->bso', _act_quant(x), _weight_quant(w))
        key = jax.random.key(seed)
        k0, k1, k2, k3 = jax.random.split(key, 4)
        x = jax.random.normal(k0, (4, 256, HIDDEN), dtype=jnp.float32)
        w_gate = jax.random.normal(k1, (INNER, HIDDEN), dtype=jnp.float32) / np.sqrt(HIDDEN)
        w_up = jax.random.normal(k2, (INNER, HIDDEN), dtype=jnp.float32) / np.sqrt(HIDDEN)
        w_down = jax.random.normal(k3, (HIDDEN, INNER), dtype=jnp.float32) / np.sqrt(INNER)
        return {'x': x, 'w_gate': w_gate, 'w_up': w_up, 'w_down': w_down}
    _L3_ffn_all = _L3_ffn_setup()
    _L3_ffn_in = {k: v for k, v in _L3_ffn_all.items() if k in ('w_gate', 'w_up', 'w_down')}
    del _L3_ffn_all
    return {'x': x, 'ctx_2048': ctx_2048, 'itok_Bx1_68_817': itok_Bx1_68_817, 'mask_BxS2_ik0': mask_BxS2_ik0, 'mask_BxS2_if0': mask_BxS2_if0, 'g_xattn': g_xattn, 'g_ffn': g_ffn, 'L0_xattn_b': _L0_xattn_in['b'], 'L0_ffn_w1_w': _L0_ffn_in['w1_w'], 'L0_ffn_w1_s': _L0_ffn_in['w1_s'], 'L0_ffn_w2_w': _L0_ffn_in['w2_w'], 'L0_ffn_w2_s': _L0_ffn_in['w2_s'], 'L0_ffn_h1_w': _L0_ffn_in['h1_w'], 'L0_ffn_h1_s': _L0_ffn_in['h1_s'], 'L0_ffn_h2_w': _L0_ffn_in['h2_w'], 'L0_ffn_h2_s': _L0_ffn_in['h2_s'], 'L0_ffn_w3_w': _L0_ffn_in['w3_w'], 'L0_ffn_w3_s': _L0_ffn_in['w3_s'], 'L1_xattn_w_qkv': _L1_xattn_in['w_qkv'], 'L1_xattn_w_proj': _L1_xattn_in['w_proj'], 'L1_xattn_b_proj': _L1_xattn_in['b_proj'], 'L1_ffn_g1': _L1_ffn_in['g1'], 'L1_ffn_g2': _L1_ffn_in['g2'], 'L1_ffn_w_down': _L1_ffn_in['w_down'], 'L1_ffn_wq': _L1_ffn_in['wq'], 'L1_ffn_wk': _L1_ffn_in['wk'], 'L1_ffn_wv': _L1_ffn_in['wv'], 'L1_ffn_w_up': _L1_ffn_in['w_up'], 'L1_ffn_router_w': _L1_ffn_in['router_w'], 'L1_ffn_w1': _L1_ffn_in['w1'], 'L1_ffn_w2': _L1_ffn_in['w2'], 'L1_ffn_w3': _L1_ffn_in['w3'], 'L2_xattn_b': _L2_xattn_in['b'], 'L2_ffn_gamma': _L2_ffn_in['gamma'], 'L2_ffn_beta': _L2_ffn_in['beta'], 'L2_ffn_Wg': _L2_ffn_in['Wg'], 'L2_ffn_bg': _L2_ffn_in['bg'], 'L2_ffn_W1': _L2_ffn_in['W1'], 'L2_ffn_b1': _L2_ffn_in['b1'], 'L2_ffn_W2': _L2_ffn_in['W2'], 'L2_ffn_b2': _L2_ffn_in['b2'], 'L3_xattn_W_in': _L3_xattn_in['W_in'], 'L3_xattn_b_in': _L3_xattn_in['b_in'], 'L3_xattn_g_res': _L3_xattn_in['g_res'], 'L3_xattn_g_init': _L3_xattn_in['g_init'], 'L3_ffn_w_gate': _L3_ffn_in['w_gate'], 'L3_ffn_w_up': _L3_ffn_in['w_up'], 'L3_ffn_w_down': _L3_ffn_in['w_down']}

def reference(x, ctx_2048, itok_Bx1_68_817, mask_BxS2_ik0, mask_BxS2_if0, g_xattn, g_ffn, L0_xattn_b, L0_ffn_w1_w, L0_ffn_w1_s, L0_ffn_w2_w, L0_ffn_w2_s, L0_ffn_h1_w, L0_ffn_h1_s, L0_ffn_h2_w, L0_ffn_h2_s, L0_ffn_w3_w, L0_ffn_w3_s, L1_xattn_w_qkv, L1_xattn_w_proj, L1_xattn_b_proj, L1_ffn_g1, L1_ffn_g2, L1_ffn_w_down, L1_ffn_wq, L1_ffn_wk, L1_ffn_wv, L1_ffn_w_up, L1_ffn_router_w, L1_ffn_w1, L1_ffn_w2, L1_ffn_w3, L2_xattn_b, L2_ffn_gamma, L2_ffn_beta, L2_ffn_Wg, L2_ffn_bg, L2_ffn_W1, L2_ffn_b1, L2_ffn_W2, L2_ffn_b2, L3_xattn_W_in, L3_xattn_b_in, L3_xattn_g_res, L3_xattn_g_init, L3_ffn_w_gate, L3_ffn_w_up, L3_ffn_w_down):
    import jax
    import jax.numpy as jnp

    def _L0_xattn_ref(memory, query, b, seq_len):
        import jax, jax.numpy as jnp
        import numpy as np
        UNITS = 128
        NUM_HEADS = 16
        MASK_VALUE = -1000000000000.0

        def _split_heads(x, n):
            B, S, D = x.shape
            return x.reshape(B, S, n, D // n).transpose(0, 2, 1, 3)
        B, S, _ = query.shape
        dh = UNITS // NUM_HEADS
        k_mem, v_mem = jnp.split(memory, 2, axis=2)
        Q = _split_heads(query, NUM_HEADS) * dh ** (-0.5)
        Kh = _split_heads(k_mem, NUM_HEADS)
        Vh = _split_heads(v_mem, NUM_HEADS)
        logits = jnp.einsum('bhqd,bhkd->bhqk', Q, Kh) + b
        valid = (jnp.arange(S)[None, :] < seq_len[:, 0:1]).astype(jnp.float32)
        logits = logits + MASK_VALUE * (1.0 - valid)[:, None, None, :]
        weights = jax.nn.softmax(logits, axis=-1)
        out = jnp.einsum('bhqk,bhkd->bhqd', weights, Vh)
        return out.transpose(0, 2, 1, 3).reshape(B, S, UNITS)

    def _L0_ffn_ref(x, w1_w, w1_s, w2_w, w2_s, h1_w, h1_s, h2_w, h2_s, w3_w, w3_s):
        import jax, jax.numpy as jnp
        import numpy as np
        D_IN, D_HID = (128, 512)

        def _ternary(key, shape):
            return jax.random.randint(key, shape, -1, 2).astype(jnp.float32)

        def _tlin(x, w, s):
            return jnp.einsum('bsi,oi->bso', x, w) * s
        h = jax.nn.silu(_tlin(x, w1_w, w1_s)) * _tlin(x, w2_w, w2_s)
        h = jax.nn.gelu(_tlin(h, h1_w, h1_s), approximate=False)
        h = jax.nn.gelu(_tlin(h, h2_w, h2_s), approximate=False)
        return _tlin(h, w3_w, w3_s)

    def _L1_xattn_ref(x, context, w_qkv, w_proj, b_proj):
        import jax, jax.numpy as jnp
        import numpy as np
        NUM_HEADS = 16
        B, N, C = x.shape
        H = NUM_HEADS
        D = C // H
        scale = D ** (-0.5)
        qkv = (x @ w_qkv.T).reshape(B, N, 3, H, D).transpose(2, 0, 3, 1, 4)
        q, k, v = (qkv[0], qkv[1], qkv[2])
        N_c = context.shape[1]
        kv = context.reshape(B, N_c, 2, H, D).transpose(2, 0, 3, 1, 4)
        extra_k, extra_v = (kv[0], kv[1])
        k = jnp.concatenate([extra_k, k], axis=2)
        v = jnp.concatenate([extra_v, v], axis=2)
        dtype = q.dtype
        attn = jnp.einsum('bhnd,bhmd->bhnm', q * scale, k).astype(jnp.float32)
        attn = jax.nn.softmax(attn, axis=-1).astype(dtype)
        out = jnp.einsum('bhnm,bhmd->bhnd', attn, v)
        out = out.transpose(0, 2, 1, 3).reshape(B, N, C)
        return out @ w_proj.T + b_proj

    def _L1_ffn_ref(x, g1, g2, w_down, wq, wk, wv, w_up, router_w, w1, w2, w3):
        import jax, jax.numpy as jnp
        import numpy as np
        B, S, D = (2, 128, 128)
        L, H = (64, 16)
        HD = L // H
        F, E, K = (256, 8, 2)
        THETA = 10000.0
        EPS = 1e-05

        def _rmsnorm(x, g):
            return x * g * jax.lax.rsqrt(jnp.mean(x * x, axis=-1, keepdims=True) + EPS)

        def _rope(t, pos):
            inv_freq = 1.0 / THETA ** (jnp.arange(0, HD, 2, dtype=jnp.float32) / HD)
            ang = pos[:, None].astype(jnp.float32) * inv_freq[None, :]
            cos, sin = (jnp.cos(ang), jnp.sin(ang))
            t1, t2 = (t[..., 0::2], t[..., 1::2])
            r1 = t1 * cos - t2 * sin
            r2 = t1 * sin + t2 * cos
            return jnp.stack([r1, r2], axis=-1).reshape(t.shape)

        def _forward(x, g1, g2, w_down, wq, wk, wv, w_up, router_w, w1, w2, w3):
            b, s, _ = x.shape
            pos = jnp.arange(s)
            h = _rmsnorm(x, g1)
            c = h @ w_down
            split = lambda t: t.reshape(b, s, H, HD).transpose(0, 2, 1, 3)
            q = _rope(split(c @ wq), pos)
            k = _rope(split(c @ wk), pos)
            v = split(c @ wv)
            scores = jnp.einsum('bhqd,bhkd->bhqk', q, k) / jnp.sqrt(jnp.float32(HD))
            causal = jnp.tril(jnp.ones((s, s), bool))
            scores = jnp.where(causal, scores, -jnp.inf)
            attn = jax.nn.softmax(scores, axis=-1)
            o = jnp.einsum('bhqk,bhkd->bhqd', attn, v).transpose(0, 2, 1, 3).reshape(b, s, L)
            x = x + o @ w_up
            res = x
            t = _rmsnorm(x, g2).reshape(-1, D)
            probs = jax.nn.softmax(t @ router_w, axis=-1)
            vals, idx = jax.lax.top_k(probs, K)
            w = vals / jnp.sum(vals, axis=-1, keepdims=True)
            gate = jnp.sum(jax.nn.one_hot(idx, E, dtype=t.dtype) * w[..., None], axis=1)
            hid = jax.nn.silu(jnp.einsum('td,edf->tef', t, w1)) * jnp.einsum('td,edf->tef', t, w3)
            y_e = jnp.einsum('tef,efd->ted', hid, w2)
            y = jnp.einsum('ted,te->td', y_e, gate)
            return res + y.reshape(b, s, D)
        return _forward(x, g1, g2, w_down, wq, wk, wv, w_up, router_w, w1, w2, w3)

    def _L2_xattn_ref(memory, query, seq_mask, b):
        import jax, jax.numpy as jnp
        import numpy as np
        UNITS = 128
        NUM_HEADS = 8

        def _split_heads(x, n):
            B, S, D = x.shape
            return x.reshape(B, S, n, D // n).transpose(0, 2, 1, 3)
        H = NUM_HEADS
        depth = UNITS // H
        Q = _split_heads(query, H) * depth ** (-0.5)
        k_mem, v_mem = jnp.split(memory, 2, axis=2)
        K = _split_heads(k_mem, H)
        V = _split_heads(v_mem, H)
        logits = jnp.einsum('bhqd,bhkd->bhqk', Q, K) + b[0]
        mask = seq_mask.astype(jnp.float32)[:, None, None, :]
        logits = logits + -1e+30 * (1.0 - mask)
        weights = jax.nn.softmax(logits, axis=-1)
        out = jnp.einsum('bhqk,bhkd->bhqd', weights, V)
        B, _, S, _ = out.shape
        return out.transpose(0, 2, 1, 3).reshape(B, S, UNITS)

    def _L2_ffn_ref(x, gamma, beta, Wg, bg, W1, b1, W2, b2):
        import jax, jax.numpy as jnp
        import numpy as np
        D = 128
        E = 8
        K = 2
        DF = 512
        B, S = (2, 256)
        EPS_LN = 1e-05
        EPS_TOPK = 1e-08

        def _xavier(key, shape, fan_in, fan_out, dtype=jnp.float32):
            bound = float(np.sqrt(6.0 / (fan_in + fan_out)))
            return jax.random.uniform(key, shape, dtype, -bound, bound)
        b, s, d = x.shape
        mu = jnp.mean(x, axis=-1, keepdims=True)
        var = jnp.mean((x - mu) ** 2, axis=-1, keepdims=True)
        xn = (x - mu) / jnp.sqrt(var + EPS_LN) * gamma + beta
        xf = xn.reshape(-1, d)
        logits = xf @ Wg.T + bg
        probs = jax.nn.softmax(logits, axis=-1)
        tp, ti = jax.lax.top_k(probs, K)
        tp = tp / (jnp.sum(tp, axis=-1, keepdims=True) + EPS_TOPK)
        w = jnp.sum(jax.nn.one_hot(ti, E, dtype=xf.dtype) * tp[..., None], axis=1)
        h = jax.nn.gelu(jnp.einsum('td,efd->tef', xf, W1) + b1, approximate=False)
        y = jnp.einsum('tef,edf->ted', h, W2) + b2
        out = jnp.einsum('ted,te->td', y, w)
        return x + out.reshape(b, s, d)

    def _L3_xattn_ref(embeds, patch_embeds, patch_lens, W_in, b_in, g_res, g_init):
        import jax, jax.numpy as jnp
        import numpy as np
        B, L, P = (4, 512, 128)
        D_MODEL = 128
        D_GLOBAL = 256
        HEADDIM = 32
        EPSILON = 0.001
        RMS_EPS = 1e-05

        def rmsnorm(x, g, eps=RMS_EPS):
            var = jnp.mean(jnp.square(x), axis=-1, keepdims=True)
            return x * jax.lax.rsqrt(var + eps) * g

        def _hnet_depool(h, h_patch_full, patch_lens):
            h_patch = h_patch_full[..., :D_MODEL]
            bsz, plen = (h_patch.shape[0], h_patch.shape[1])
            seqlen = h.shape[1]
            logp = jnp.full((bsz, plen), -EPSILON, dtype=jnp.float32)
            bidx = jnp.cumsum(patch_lens, axis=1) - 1
            boundary_mask = jnp.zeros((bsz, seqlen), dtype=jnp.int32)
            boundary_mask = boundary_mask.at[jnp.arange(bsz)[:, None], bidx].set(1)
            dt = (-jnp.log(-jnp.expm1(logp))).astype(h_patch.dtype)
            x = h_patch / dt[..., None]
            n_heads = D_MODEL // HEADDIM
            A = -jnp.ones((n_heads,), dtype=jnp.float32)
            bcoef = jnp.exp(logp).astype(h_patch.dtype)
            x4 = x.reshape(bsz, plen, n_heads, HEADDIM)
            a = jnp.exp(dt[:, :, None] * A[None, None, :])
            u = (dt * bcoef)[:, :, None, None] * x4
            a_b = jnp.broadcast_to(a[..., None], u.shape)

            def comb(lft, rgt):
                aL, uL = lft
                aR, uR = rgt
                return (aL * aR, uL * aR + uR)
            _, s = jax.lax.associative_scan(comb, (a_b, u), axis=1)
            depool = s.reshape(bsz, plen, D_MODEL)
            plug = jnp.clip(jnp.cumsum(boundary_mask, axis=1) - 1, 0, plen - 1)
            depool_out = depool[jnp.arange(bsz)[:, None], plug]
            return depool_out + h
        h = rmsnorm(embeds, g_res)
        h = jnp.einsum('bld,ed->ble', h, W_in) + b_in
        h_patch = rmsnorm(patch_embeds, g_init)
        return _hnet_depool(h, h_patch, patch_lens)

    def _L3_ffn_ref(x, w_gate, w_up, w_down):
        import jax, jax.numpy as jnp
        import numpy as np
        HIDDEN = 128
        INNER = 512

        def _weight_quant(w):
            scale = 1.0 / jnp.clip(jnp.mean(jnp.abs(w)), 1e-05)
            wq = jnp.clip(jnp.round(w * scale), -1.0, 1.0) / scale
            return w + jax.lax.stop_gradient(wq - w)

        def _act_quant(x):
            scale = 127.0 / jnp.clip(jnp.max(jnp.abs(x), axis=-1, keepdims=True), 1e-05)
            xq = jnp.clip(jnp.round(x * scale), -128.0, 127.0) / scale
            return x + jax.lax.stop_gradient(xq - x)

        def _bitlinear(x, w):
            return jnp.einsum('bsi,oi->bso', _act_quant(x), _weight_quant(w))
        gate = jax.nn.silu(_bitlinear(x, w_gate))
        up = _bitlinear(x, w_up)
        return _bitlinear(gate * up, w_down)
    x = x + jnp.tanh(g_xattn[0]) * _L0_xattn_ref(ctx_2048, _layernorm(x, axis=-1), L0_xattn_b, itok_Bx1_68_817)
    x = x + jnp.tanh(g_ffn[0]) * _L0_ffn_ref(_layernorm(x, axis=-1), L0_ffn_w1_w, L0_ffn_w1_s, L0_ffn_w2_w, L0_ffn_w2_s, L0_ffn_h1_w, L0_ffn_h1_s, L0_ffn_h2_w, L0_ffn_h2_s, L0_ffn_w3_w, L0_ffn_w3_s)
    x = x + jnp.tanh(g_xattn[1]) * _L1_xattn_ref(_layernorm(x, axis=-1), ctx_2048, L1_xattn_w_qkv, L1_xattn_w_proj, L1_xattn_b_proj)
    x = x + jnp.tanh(g_ffn[1]) * _L1_ffn_ref(_layernorm(x, axis=-1), L1_ffn_g1, L1_ffn_g2, L1_ffn_w_down, L1_ffn_wq, L1_ffn_wk, L1_ffn_wv, L1_ffn_w_up, L1_ffn_router_w, L1_ffn_w1, L1_ffn_w2, L1_ffn_w3)
    x = x + jnp.tanh(g_xattn[2]) * _L2_xattn_ref(ctx_2048, _layernorm(x, axis=-1), mask_BxS2_ik0, L2_xattn_b)
    x = x + jnp.tanh(g_ffn[2]) * _L2_ffn_ref(_layernorm(x, axis=-1), L2_ffn_gamma, L2_ffn_beta, L2_ffn_Wg, L2_ffn_bg, L2_ffn_W1, L2_ffn_b1, L2_ffn_W2, L2_ffn_b2)
    x = x + jnp.tanh(g_xattn[3]) * _L3_xattn_ref(_layernorm(x, axis=-1), ctx_2048, mask_BxS2_if0, L3_xattn_W_in, L3_xattn_b_in, L3_xattn_g_res, L3_xattn_g_init)
    x = x + jnp.tanh(g_ffn[3]) * _L3_ffn_ref(_layernorm(x, axis=-1), L3_ffn_w_gate, L3_ffn_w_up, L3_ffn_w_down)
    return x

_drawn_inputs = setup_inputs


def setup_inputs(seed=0):
    import zlib

    import numpy as np

    out = dict(_drawn_inputs(seed))
    spreads = {'L1_ffn_g1': (1.0, 0.2),
     'L1_ffn_g2': (1.0, 0.2),
     'L2_ffn_gamma': (1.0, 0.2),
     'L2_ffn_beta': (0.0, 0.1),
     'L2_ffn_bg': (0.0, 0.1),
     'L2_ffn_b1': (0.0, 0.1),
     'L2_ffn_b2': (0.0, 0.1),
     'L3_xattn_b_in': (0.0, 0.1),
     'L3_xattn_g_res': (1.0, 0.2),
     'L3_xattn_g_init': (1.0, 0.2)}
    factors = {}
    for name, (base, spread) in spreads.items():
        noise = np.random.default_rng([zlib.crc32(name.encode()), seed]).standard_normal(out[name].shape)
        drawn = base * np.exp(spread * noise) if base else spread * noise
        out[name] = jnp.asarray(drawn.astype(out[name].dtype))
    for name, factor in factors.items():
        out[name] = (out[name] * factor).astype(out[name].dtype)
    return out
```

```python
from contextlib import ExitStack

import numpy as np

import concourse.bass as bass
from concourse import mybir

F32 = mybir.dt.float32
BF16 = mybir.dt.bfloat16
I32 = mybir.dt.int32
ALU = mybir.AluOpType
ACT = mybir.ActivationFunctionType
AX = mybir.AxisListType

B, S, D = 32, 128, 128
NP = B // 2
NG = B // 4
LAG = 2
EPS = 1e-5

CST = {}


def const_block():
    f = np.float32
    j = np.arange(128)[:, None]
    t = np.arange(128)[None, :]
    parts = []

    def put(name, a):
        CST[name] = (sum(p.shape[1] for p in parts), a.shape[1])
        parts.append(np.ascontiguousarray(a, f))

    put("ident", (j == t).astype(f))
    put("tri", (j <= t).astype(f))
    logp = f(-0.001)
    dt = f(-np.log(-np.expm1(logp)))
    a = f(np.exp(-dt))
    put("toep", np.where(t >= j, np.power(np.float64(a), np.maximum(t - j, 0)), 0.0))
    put("iota_t", np.broadcast_to(t, (128, 128)))
    put("iota_p", j.astype(f))
    put("cneg", np.where(t > j, -1e30, 0.0))
    put("cnegT", np.where(j > t, -1e30, 0.0))
    put("selb", (np.arange(128)[:, None] % 32 == np.arange(32)[None, :]).astype(f))
    inv = (f(1.0) / np.power(f(10000.0), np.arange(0, 4, 2, dtype=f) / f(4))).astype(f)
    ang = np.arange(128, dtype=f)[None, :] * inv[(np.arange(128) % 4) // 2][:, None]
    half = np.where(np.arange(128) < 64, 0.5, 1.0).astype(f)[:, None]
    sign = np.where(np.arange(128) % 2 == 0, -1.0, 1.0).astype(f)[:, None]
    put("cos", np.cos(ang).astype(f) * half)
    put("sin", np.sin(ang).astype(f) * sign * half)
    i8 = np.arange(64)
    put("low", np.broadcast_to((i8 % 8 < i8 // 8).astype(f)[None, :], (128, 64)))
    put("ones", np.ones((128, 128), f))
    put("half", np.full((128, 32), -0.5, f))
    return np.concatenate(parts, axis=1), float(f(dt * f(np.exp(logp))) / dt)


class Queues:

    def __init__(self, nc, ctx):
        self.nc = nc
        self.names = ["pe", "dve", "act", "pool", "sp"]
        self.list = {n: [] for n in self.names}
        self.count = {n: 0 for n in self.names}
        self.sem = {n: ctx.enter_context(nc.semaphore("done_" + n)) for n in self.names}
        self.dsem = {}
        self.dcount = {}
        self.ctx = ctx

    def put(self, eng, fn, waits, inc=True):
        self.list[eng].append((fn, tuple(w for w in waits if w is not None), (self.sem[eng], 1) if inc else None))
        if inc:
            self.count[eng] += 1
        return (self.sem[eng], self.count[eng])

    def dma(self, name, out, in_, waits=(), eng="sp", **kw):
        if name not in self.dsem:
            self.dsem[name] = self.ctx.enter_context(self.nc.semaphore("dma_" + name))
            self.dcount[name] = 0
        self.dcount[name] += 16
        self.list[eng].append((lambda e: e.dma_start(out, in_, **kw), tuple(w for w in waits if w is not None),
                               (self.dsem[name], 16)))
        return (self.dsem[name], self.dcount[name])

    def emit(self, eng, handle):
        seen = {}
        for fn, waits, inc in self.list[eng]:
            for s, v in waits:
                if seen.get(s.name, 0) < v:
                    handle.wait_ge(s, v)
                    seen[s.name] = v
            ins = fn(handle)
            if ins is not None and inc is not None:
                ins.then_inc(*inc)


def build(nc, io, out, cu, stop=99):
    ctx = ExitStack()
    with ctx:
        Q = Queues(nc, ctx)

        def sb(name, shape, dt=F32):
            return ctx.enter_context(nc.sbuf_tensor(name, shape, dt))

        def dve(fn, *w, inc=True):
            return Q.put("dve", fn, w, inc)

        def act(fn, *w):
            return Q.put("act", fn, w)

        def pool(fn, *w):
            return Q.put("pool", fn, (*w, (Q.sem["pool"], Q.count["pool"])))

        def pe(fn, *w, inc=False):
            return Q.put("pe", fn, w, inc)

        PSB = [ctx.enter_context(nc.psum_tensor(f"psb{i}", [128, 512], F32)) for i in (0, 1)]
        PSD = [ctx.enter_context(nc.psum_tensor(f"psd{i}", [128, 1024], F32)) for i in (0, 1)]
        PSB += [PSD[0][:, 0:512], PSD[0][:, 512:1024], PSD[1][:, 0:512], PSD[1][:, 512:1024]]
        PSB += [ctx.enter_context(nc.psum_tensor(f"psb{i}", [128, 512], F32)) for i in (6, 7)]
        PSB = [b[:, :] for b in PSB]
        bank_free = [None] * 8

        ncst = sum(w for _, w in CST.values())
        cst = sb("cst", [128, ncst])

        def C(name):
            o, w = CST[name]
            return cst[:, o:o + w]

        X = sb("X", [128, B, D])
        U = sb("U", [128, B, D])
        WB = sb("WB", [128, 6144])
        WS = sb("WS", [128, 1216])
        Q8 = sb("Q8", [128, 3, 4096], BF16)
        K8 = sb("K8", [128, 3, 4096], BF16)
        KS = sb("KS", [128, 3, 4096], BF16)
        HB = sb("HB", [128, 8, 512])
        AT = sb("AT", [128, 2, 512])
        TT = K8[:, :, :].rearrange("p a b -> p (a b)").bitcast(F32)
        tg = sb("tg", [128, 8])
        graw = sb("graw", [128, 8])
        cols = sb("cols", [128, 64])
        rows = sb("rows", [128, 2, 128])
        identb = sb("identb", [128, 128], BF16)
        cnegb = sb("cnegb", [128, 2, 128], BF16)
        selbb = sb("selbb", [96, 32], BF16)
        trib = sb("trib", [128, 128], BF16)
        bias = sb("bias", [128, 2, 32])
        biasc = sb("biasc", [128, 2, 96], BF16)
        biasT = sb("biasT", [96, 2, 128], BF16)
        btmp = sb("btmp", [128, 32])
        ints = sb("ints", [128, 3, 32], I32)
        st = sb("st", [128, 2, 4, 6])
        mv = sb("mv", [128, 2, 4, 2])
        rs = sb("rs", [128, 2, 4, 2])
        xn = sb("xn", [128, 2, 512])
        xT = sb("xT", [128, 2, 512])
        sp32 = sb("sp32", [128, 2, 256])
        r32 = sb("r32", [128, 256])
        comp = sb("comp", [128, 4, 3 * 256], BF16)
        vraw = sb("vraw", [128, 3, 256])
        VA = sb("VA", [128, 4, 2 * 144])
        VS = sb("VS", [128, 4, 2 * 144])
        mneg = sb("mneg", [128, 4, 16])
        mres = sb("mres", [128, 16])
        mcb = sb("mcb", [128, 2, 48], BF16)
        mT = sb("mT", [48, 2, 128], BF16)
        rec = sb("rec", [128, 2, 16])
        otmp = sb("otmp", [128, 2, 128])
        oT = sb("oT", [128, 2, 128])
        LG = sb("LG", [128, B, 8])
        GT = sb("GT", [128, B, 8])
        PT = HB[:, :, :].rearrange("p a b -> p (a b)").rearrange("p (n c) -> p n c", c=1024)

        def scratch(name):
            return nc.dram_tensor(name, [3, 128, B * S], BF16, kind="Internal").ap()

        sc_k = scratch("sc_k")
        sc_q = [scratch(f"sc_q{i}") for i in range(4)]
        sc_s = [scratch(f"sc_s{i}") for i in range(2)]

        t_cst = Q.dma("cst", cst[:, :], io["cst"])
        t_x = [Q.dma(f"x{i}", X[:, 16 * i:16 * i + 16, :], io["x"][16 * i:16 * i + 16].rearrange("b t d -> t b d"))
               for i in range(2)]
        t_g = Q.dma("g", graw[:, 0:4], io["g_xattn"].rearrange("(a n) -> a n", a=1).broadcast_to([128, 4]))
        t_g = Q.dma("g", graw[:, 4:8], io["g_ffn"].rearrange("(a n) -> a n", a=1).broadcast_to([128, 4]))
        t_i = Q.dma("ints", ints[:, 0, :], io["seq"].rearrange("b a -> a b").broadcast_to([128, 32]))
        t_i = Q.dma("ints", ints[:, 1, :], io["maskT"])
        t_i = Q.dma("ints", ints[:, 2, :], io["lensT"])

        col_at = {}

        def load_cols(name, n):
            at = sum(w for _, w in col_at.values())
            col_at[name] = (at, n)
            return Q.dma("cols", cols[:, at:at + n], io[name])

        for name, n in (("L0_xattn_b", 1), ("L2_b", 1), ("w1_s", 4), ("w2_s", 4), ("h1_s", 4), ("h2_s", 4),
                        ("g1", 1), ("g2", 1), ("gamma", 1), ("beta", 1), ("g_res", 1)):
            t_cols = load_cols(name, n)

        def col(name, i=0):
            return cols[:, col_at[name][0] + i:col_at[name][0] + i + 1]

        def row_bc(name, k, n=128):
            return io[name].rearrange("(a n) -> a n", a=1)[:, 0:n].broadcast_to([128, n])

        t_row0 = Q.dma("row0", rows[:, 0, :], row_bc("w3_s", 0))
        t_row1 = Q.dma("row1", rows[:, 1, :], row_bc("b_proj", 0))

        wb = {}
        at = 0
        t_wb = []
        for name, n in (("w1T", 512), ("w2T", 512), ("h1T", 2048), ("h2T", 2048), ("w3T", 512)):
            wb[name] = WB[:, at:at + n]
            t_wb.append(Q.dma("wb" + name, wb[name], io[name]))
            at += n
        wsm = {}
        at = 0
        t_ws = None
        for name, p, n in (("w_qkvT", 128, 384), ("w_projT", 128, 128), ("w_down", 128, 64), ("wqk", 64, 128),
                           ("wqk_sw", 64, 128), ("wv", 64, 64), ("w_up", 64, 128), ("router_w", 128, 8),
                           ("WgT", 128, 8), ("W_inT", 128, 128)):
            wsm[name] = WS[0:p, at:at + n]
            t_ws = Q.dma("ws", wsm[name], io[name])
            at += n

        t_idb = dve(lambda e: e.tensor_copy(identb[:, :], C("ident")), t_cst)
        dve(lambda e: e.tensor_copy(cnegb[:, 0, :], C("cneg")), t_cst)
        dve(lambda e: e.tensor_copy(cnegb[:, 1, :], C("cnegT")), t_cst)
        dve(lambda e: e.tensor_copy(trib[:, :], C("tri")), t_cst)
        t_cb = dve(lambda e: e.tensor_copy(selbb[:, :], C("selb")[0:96, :]), t_cst)
        t_tg = act(lambda e: e.activation(tg[:, :], graw[:, :], ACT.Tanh), t_g)

        t_z = []
        for tile in (Q8, K8, KS):
            t = pool(lambda e, tile=tile: e.memset(tile[:, :, :], 0.0))
            if tile is not Q8:
                t = pool(lambda e, tile=tile: e.memset(tile[96:128, :, :], 1.0), t)
            t_z.append(t)
        for tile in (VA, VS):
            t_ones = pool(lambda e, tile=tile: e.memset(tile[:, :, :], 1.0))

        t = dve(lambda e: e.tensor_copy(btmp[:, :], ints[:, 0, :]), t_i)
        t = dve(lambda e: e.tensor_scalar(btmp[:, :], btmp[:, :], C("iota_p"), -1.0, ALU.is_gt, ALU.add), t, t_cst)
        t = dve(lambda e: e.tensor_scalar(bias[:, 0, :], btmp[:, :], 1e12, col("L0_xattn_b"), ALU.mult, ALU.add), t, t_cols)
        t = dve(lambda e: e.tensor_copy(btmp[:, :], ints[:, 1, :]), t)
        t = dve(lambda e: e.tensor_scalar(btmp[:, :], btmp[:, :], -1.0, 1e30, ALU.add, ALU.mult), t)
        t_bias = dve(lambda e: e.tensor_scalar(bias[:, 1, :], btmp[:, :], col("L2_b"), None, ALU.add), t, t_cols)
        t = t_bias
        for i in range(2):
            b3 = biasc[:, i, :].rearrange("p (c b) -> p c b", c=3)
            t = dve(lambda e, i=i, b3=b3: e.tensor_copy(b3[:, 0, :], bias[:, i, :]), t)
            t = dve(lambda e, i=i, b3=b3: e.tensor_tensor(btmp[:, :], bias[:, i, :], b3[:, 0, :], ALU.subtract), t)
            t = dve(lambda e, i=i, b3=b3: e.tensor_copy(b3[:, 1, :], btmp[:, :]), t)
            t = dve(lambda e, i=i, b3=b3: e.tensor_tensor(b3[:, 2, :], btmp[:, :], b3[:, 1, :], ALU.subtract), t)
            tp = pe(lambda e, i=i: e.transpose(PSB[7].bitcast(BF16)[0:96, 128 * i:128 * i + 128], biasc[:, i, :], identb[:, :]),
                    t, t_idb, bank_free[7], inc=True)
            t = dve(lambda e, i=i: e.tensor_copy(biasT[:, i, :], PSB[7].bitcast(BF16)[0:96, 128 * i:128 * i + 128]), tp)
            bank_free[7] = t
        t_biasT = t

        st_free = [None, None]
        turn = [0]

        def norm(src, n, waits, outs, eps=EPS, rms=False, width=128):
            k = turn[0] % 2
            turn[0] += 1
            for j in range(n):
                t = dve(lambda e, j=j: e.bn_stats(st[:, k, j, :], src[:, j, :]), *waits, st_free[k])
            for j in range(n):
                t = dve(lambda e, j=j: e.bn_aggr(mv[:, k, j, :], st[:, k, j, :]), t)
            m, v = mv[:, k, 0:n, 0:1], mv[:, k, 0:n, 1:2]
            r0, r1 = rs[:, k, 0:n, 0:1], rs[:, k, 0:n, 1:2]
            if rms:
                t = pool(lambda e: e.tensor_tensor(r0, m, m, ALU.mult), t)
                t = pool(lambda e: e.tensor_tensor(r0, r0, v, ALU.add), t)
                t = pool(lambda e: e.tensor_scalar(r0, r0, eps, None, ALU.add), t)
            else:
                t = pool(lambda e: e.tensor_scalar(r0, v, eps, None, ALU.add), t)
            t = pool(lambda e: e.tensor_tensor(r1, r0, C("half")[:, 0:n].unsqueeze(2), ALU.pow), t, t_cst)
            for j in range(n):
                if rms:
                    t2 = dve(lambda e, j=j: e.tensor_scalar(outs(j), src[:, j, 0:width], rs[:, k, j, 1:2], None, ALU.mult), t)
                else:
                    t2 = dve(lambda e, j=j: e.tensor_scalar(outs(j), src[:, j, :], mv[:, k, j, 0:1], rs[:, k, j, 1:2],
                                                            ALU.subtract, ALU.mult), t)
            st_free[k] = t2
            return t2

        xn_free = [None, None]
        xT_free = [None, None]

        def turned(k, n, bank, t, scale=None, bcol=None, dst=None, dst_free=None):
            dst = xT[:, k, 0:128 * n] if dst is None else dst
            for j in range(n):
                tp = pe(lambda e, j=j: e.transpose(PSB[bank][:, 128 * j:128 * j + 128], xn[:, k, 128 * j:128 * j + 128],
                                                   C("ident")), t, bank_free[bank], t_cst, inc=(j == n - 1))
            xn_free[k] = tp
            s = 1.0 if scale is None else scale
            bz = 0.0 if bcol is None else bcol
            f = ACT.Identity if bcol is not None else ACT.Copy
            ta = act(lambda e: e.activation(dst, PSB[bank][:, 0:128 * n], f, bias=bz, scale=s), tp, xT_free[k], dst_free, t_cols)
            bank_free[bank] = ta
            return ta

        r32_free = [None]

        def split(src, dst, t, free):
            t = pool(lambda e: e.tensor_copy(dst[:, 0, :], src), t, free)
            t = pool(lambda e: e.tensor_tensor(r32[:, :], src, dst[:, 0, :], ALU.subtract), t, r32_free[0])
            t_src = t
            t = pool(lambda e: e.tensor_copy(dst[:, 1, :], r32[:, :]), t)
            t = pool(lambda e: e.tensor_tensor(dst[:, 2, :], r32[:, :], dst[:, 1, :], ALU.subtract), t)
            r32_free[0] = t
            return t_src, t

        comp_free = [None] * 4
        comp_turn = [0]

        def split_out(src, t, sc, p, name):
            k = comp_turn[0] % 4
            comp_turn[0] += 1
            dst = comp[:, k, :].rearrange("p (c t) -> p c t", c=3)
            t_src, t = split(src, dst, t, comp_free[k])
            td = Q.dma(f"comp{k}", sc[:, :, 256 * p:256 * p + 256].rearrange("c p t -> p c t"), dst, (t,))
            comp_free[k] = td
            return t_src, td

        QO = (0, 1, 2, 0, 1, 0)
        KO = (0, 0, 0, 1, 1, 2)

        def load_rows(tile, name, sc, order, p, dh, H, waits):
            dst = tile[:, p % 3, 0:H * 256].rearrange("r (h t) -> r h t", h=H)
            for i, c in enumerate(order):
                src = sc[c, :, 256 * p:256 * p + 256].rearrange("(h d) t -> d h t", d=dh)
                t = Q.dma(f"{name}{p % 3}", dst[i * dh:i * dh + dh, :, :], src, waits)
            return t

        sp_free = [None, None]
        k_in = {}
        for p in range(NP):
            k = p % 2
            tl = Q.dma(f"kin{k}", sp32[:, k, :], io["kT"][:, 256 * p:256 * p + 256], (sp_free[k],))
            sp_free[k], k_in[p] = split_out(sp32[:, k, :], tl, sc_k, p, "k")

        x_tok = {b: t_x[b // 16] for b in range(B)}
        u_tok = {}

        q8_free = [t_z[0]] * 3
        k8_free = [t_z[1]] * 3
        ks_free = [t_z[2]] * 3
        va_free = [t_ones] * 4
        vs_free = [t_ones] * 4
        vr_free = [None] * 3
        pt_free = [None] * 4
        mn_free = [None] * 4
        mcb_free = [None] * 2
        mres_free = [None]
        mT_free = [None] * 2
        rec_free = [None] * 2
        later = []

        def attention(H, dh, vd, ctx_kb, self_kb, prep, finish, bias_i=None, causal=False, vdh=None):
            vdh = vd
            nkb = len(ctx_kb) + len(self_kb)
            tiles = [K8] * len(ctx_kb) + [KS] * len(self_kb)
            vts = [VA] * len(ctx_kb) + [VS] * len(self_kb)
            RQ = 96
            per_s = 4 // nkb
            n_s = H // per_s
            prepped = {}
            ready_m = {}
            chain = {}
            pv_wait = []
            nst = [0]
            last_st = {}

            def vh(vt, p, b2):
                return vt[:, p % 4, 0:2 * H * (vdh + 1)].rearrange("p (b h d) -> p b h d", b=2, h=H)[:, b2]

            def head(tile, p, b2, h, rows_):
                return tile[0:rows_, p % 3, 256 * h + 128 * b2:256 * h + 128 * b2 + 128]

            def s_unit(b, i):
                p, b2 = divmod(b, 2)
                bank = i % 2
                w = [bank_free[bank], *prepped[p]["qk"]]
                extra = bias_i is not None or causal
                for hh in range(per_s):
                    h = i * per_s + hh
                    for kb in range(nkb):
                        o = PSB[bank][:, 128 * (hh * nkb + kb):128 * (hh * nkb + kb) + 128]
                        last = hh == per_s - 1 and kb == nkb - 1
                        t = pe(lambda e, o=o, h=h, kb=kb, st_=(hh == 0 and kb == 0), sp_=not extra: e.matmul(
                            o, head(Q8, p, b2, h, RQ), head(tiles[kb], p, b2, h, RQ), start=st_, stop=sp_,
                            skip_group_check=True), *w, inc=last and not extra)
                        w = []
                if bias_i is not None:
                    t = pe(lambda e: e.matmul(PSB[bank].rearrange("p (h k) -> p h k", h=4), selbb[:, b:b + 1].broadcast_to([96, 128]),
                                              biasT[:, bias_i, :].unsqueeze(1).broadcast_to([96, 4, 128]), start=False, stop=True,
                                              skip_group_check=True), t_biasT, t_cb, inc=True)
                if causal:
                    t = pe(lambda e: e.matmul(PSB[bank].rearrange("p (h k) -> p h k", h=4), identb[:, :],
                                              cnegb[:, 0, :].unsqueeze(1).broadcast_to([128, 4, 128]), start=False, stop=True,
                                              skip_group_check=True), t_cb, inc=True)
                tr = dve(lambda e: e.tensor_reduce(mneg[:, b % 4, i * per_s:(i + 1) * per_s],
                                                   PSB[bank].rearrange("p (h k) -> p h k", h=per_s), AX.X, ALU.max, negate=True),
                         t, mn_free[b % 4])
                bank_free[bank] = tr
                if i == n_s - 1:
                    chain[b] = tr
                    k = b % 2
                    c3 = mcb[:, k, 0:3 * H].rearrange("p (c h) -> p c h", c=3)
                    mn = mneg[:, b % 4, 0:H]
                    t1 = pool(lambda e: e.tensor_copy(c3[:, 0, :], mn), tr, mcb_free[k])
                    t1 = pool(lambda e: e.tensor_tensor(mres[:, 0:H], mn, c3[:, 0, :], ALU.subtract), t1, mres_free[0])
                    mn_free[b % 4] = t1
                    t1 = pool(lambda e: e.tensor_copy(c3[:, 1, :], mres[:, 0:H]), t1)
                    t1 = pool(lambda e: e.tensor_tensor(c3[:, 2, :], mres[:, 0:H], c3[:, 1, :], ALU.subtract), t1)
                    mres_free[0] = t1
                    chain[b] = t1

            def m_turn(b):
                p, b2 = divmod(b, 2)
                k = b % 2
                o = PSB[7].bitcast(BF16)[0:3 * H, 0:128]
                t = pe(lambda e: e.transpose(o, mcb[:, k, 0:3 * H], identb[:, :]), chain[b], t_idb, bank_free[7], inc=True)
                mcb_free[k] = t
                t = act(lambda e: e.activation(mT[0:3 * H, k, :], o, ACT.Copy), t, mT_free[k])
                bank_free[7] = t
                dst = Q8[96:99, p % 3, 0:H * 256].rearrange("c (h t) -> c h t", h=H)[:, :, 128 * b2:128 * b2 + 128]
                for c in range(3):
                    t2 = Q.dma(f"m{k}", dst[c:c + 1], mT[c * H:c * H + H, k, :], (t, *prepped[p]["qk"]))
                mT_free[k] = t2
                ready_m[b] = t2

            def st_unit(b, i):
                p, b2 = divmod(b, 2)
                half, kb = divmod(i, nkb)
                n = nst[0]
                nst[0] += 1
                k = n % 2
                banks = (2 + 2 * k, 3 + 2 * k)
                w = [bank_free[banks[0]], bank_free[banks[1]], ready_m[b]]
                for hh in range(8):
                    h = 8 * half + hh
                    o = PSD[k][:, 128 * hh:128 * hh + 128]
                    t = pe(lambda e, o=o, h=h, hh=hh: e.matmul(o, head(tiles[kb], p, b2, h, 99), head(Q8, p, b2, h, 99),
                                                              start=(hh % 4 == 0), stop=not causal, skip_group_check=True),
                           *w, inc=(hh == 7 and not causal))
                    w = []
                if causal:
                    for j in range(2):
                        t = pe(lambda e, j=j: e.matmul(PSD[k][:, 512 * j:512 * j + 512].rearrange("p (h k) -> p h k", h=4), identb[:, :],
                                                       cnegb[:, 1, :].unsqueeze(1).broadcast_to([128, 4, 128]), start=False, stop=True,
                                                       skip_group_check=True), t_cb, inc=(j == 1))
                bz = 0.0 if bias_i is None else bias[:, bias_i, b:b + 1]
                slot = n % 4
                te = act(lambda e: e.activation(PT[:, slot, :], PSD[k][:, :], ACT.Exp, bias=bz), t, pt_free[slot], t_bias)
                bank_free[banks[0]] = bank_free[banks[1]] = te
                last_st[b] = t
                if b2 == 1 and i == n_st - 1:
                    q8_free[p % 3] = t
                    if ctx_kb:
                        k8_free[p % 3] = t
                    if self_kb:
                        ks_free[p % 3] = t
                return (b, half, kb, slot, te)

            n_st = (H // 8) * nkb
            got = {}

            def pv_unit(u):
                b, half, kb, slot, te = u
                got.setdefault((b, half), []).append((kb, slot, te))
                if kb != nkb - 1:
                    return
                p, b2 = divmod(b, 2)
                blocks = got.pop((b, half))
                w = [x[2] for x in blocks] + [*prepped[p]["v"]]
                if half == 0:
                    w.append(bank_free[6])
                for hh in range(8):
                    h = 8 * half + hh
                    o = PSB[6][:, h * (vdh + 1):(h + 1) * (vdh + 1)]
                    for kb_, slot_, _ in blocks:
                        t = pe(lambda e, o=o, h=h, hh=hh, kb_=kb_, slot_=slot_: e.matmul(
                            o, PT[:, slot_, 128 * hh:128 * hh + 128], vh(vts[kb_], p, b2)[:, h, :],
                            start=(h == 0 and kb_ == 0), stop=(kb_ == nkb - 1), skip_group_check=True), *w,
                            inc=(hh == 7 and kb_ == nkb - 1))
                        w = []
                for _, slot_, _ in blocks:
                    pt_free[slot_] = t
                if half == H // 8 - 1:
                    if b2 == 1:
                        if ctx_kb:
                            va_free[p % 4] = t
                        if self_kb:
                            vs_free[p % 4] = t
                    k = b % 2
                    o3 = PSB[6][:, 0:H * (vdh + 1)].rearrange("p (h d) -> p h d", h=H)
                    t = dve(lambda e: e.reciprocal(rec[:, k, 0:H], o3[:, :, vdh]), t, rec_free[k])
                    t = dve(lambda e: e.tensor_tensor(otmp[:, k, 0:H * vdh].rearrange("p (h d) -> p h d", h=H), o3[:, :, 0:vdh],
                                                      rec[:, k, 0:H].unsqueeze(2).broadcast_to([128, H, vdh]), ALU.mult), t)
                    bank_free[6] = t
                    finish(b, k, t)

            coming = {}
            for p in (0, 1):
                *first, last = prep(p)
                for f in first:
                    f()
                prepped[p] = last()
            for tstep in range(B + LAG):
                tasks = []
                if tstep < B:
                    tasks.append([lambda i=i: s_unit(tstep, i) for i in range(n_s)])
                if tstep >= LAG:
                    tasks.append([lambda i=i: ("st", st_unit(tstep - LAG, i)) for i in range(n_st)])
                order = sorted(((i + 0.5) / len(g), gi, f) for gi, g in enumerate(tasks) for i, f in enumerate(g))
                mids = {max(1, len(order) // 3): 0, max(2, 2 * len(order) // 3): 1}
                for i in range(len(order) + 1):
                    if i in mids:
                        m = mids[i]
                        run, later[:] = later[:], []
                        if m == 0 and 1 <= tstep <= B:
                            m_turn(tstep - 1)
                        for f in run:
                            f()
                        pp, half = divmod(tstep + 4, 2)
                        if pp < NP:
                            if half == 0 and m == 0:
                                coming[pp] = prep(pp)
                            if len(coming[pp]) > 1:
                                coming[pp].pop(0)()
                    if i < len(order):
                        r = order[i][2]()
                        if r is not None:
                            pv_wait.append(r[1])
                            if len(pv_wait) > 1:
                                pv_unit(pv_wait.pop(0))
                pp, half = divmod(tstep + 4, 2)
                if half == 1 and pp < NP:
                    for f in coming[pp][:-1]:
                        f()
                    prepped[pp] = coming.pop(pp)[-1]()
            while pv_wait:
                pv_unit(pv_wait.pop(0))
            while later:
                run, later[:] = later[:], []
                for f in run:
                    f()

        def load_v(p, H, dh):
            k = p % 3
            tv = Q.dma(f"vr{k}", vraw[:, k, :].rearrange("p (b d) -> p b d", b=2),
                       io["ctx_2048"][2 * p:2 * p + 2, :, 128:256].rearrange("b t d -> t b d"), (vr_free[k],))
            dst = VA[:, p % 4, 0:2 * H * (dh + 1)].rearrange("p (n d) -> p n d", d=dh + 1)
            t = pool(lambda e: e.tensor_copy(dst[:, :, 0:dh], vraw[:, k, :].rearrange("p (n d) -> p n d", d=dh)), tv, va_free[p % 4])
            vr_free[k] = t
            return t

        def prep_ctx(sc, dh, bi):
            H = 128 // dh

            def prep(p):
                k = p % 2
                got = {}

                def query():
                    t = norm(X[:, 2 * p:2 * p + 2, :], 2, (x_tok[2 * p], x_tok[2 * p + 1], xn_free[k]),
                             lambda j: xn[:, k, 128 * j:128 * j + 128])
                    got["n"] = t

                def query_T():
                    t = turned(k, 2, 7, got["n"], scale=float(np.float32(dh ** -0.5)))
                    xT_free[k], got["q"] = split_out(xT[:, k, 0:256], t, sc, p, "q")

                def loads():
                    tq = load_rows(Q8, "q8", sc[:, 0:128], QO, p, dh, H, (got["q"], q8_free[p % 3]))
                    tk = load_rows(K8, "k8", sc_k[:, 0:128], KO, p, dh, H, (k_in[p], k8_free[p % 3]))
                    return {"qk": [tq, tk], "v": [load_v(p, H, dh)]}
                return [query, query_T, loads]
            return prep

        def finish_add(gi):
            def finish(b, k, t):
                t = dve(lambda e: e.scalar_tensor_tensor(out=X[:, b, :], in0=otmp[:, k, :], scalar=tg[:, gi:gi + 1], in1=X[:, b, :],
                                                         op0=ALU.mult, op1=ALU.add), t, t_tg, x_tok[b])
                x_tok[b] = t
                rec_free[k] = t
            return finish

        ring = [0]

        def bank():
            ring[0] += 1
            return ring[0] % 8

        def group_T(g, src, waits, rms=False, scale=None, bcol=None, dst=None, dst_free=None):
            k = g % 2
            t = norm(src, 4, (*waits, xn_free[k]), lambda j: xn[:, k, 128 * j:128 * j + 128], rms=rms)
            return turned(k, 4, bank(), t, scale=scale, bcol=bcol, dst=dst, dst_free=dst_free)

        def xg(g):
            return [x_tok[4 * g + j] for j in range(4)]

        attention(16, 8, 8, [0], [], prep_ctx(sc_q[0], 8, 0), finish_add(0), bias_i=0)

        def ffn0():
            t_s3 = dve(lambda e: e.tensor_scalar(rows[:, 0, :], rows[:, 0, :], tg[:, 4:5], None, ALU.mult), t_row0, t_tg)
            xt = {0: group_T(0, X[:, 0:4, :], xg(0))}
            hb_free = [None, None]
            at_free = [None, None]
            hA, hB = HB[:, 0:4, :], HB[:, 4:8, :]
            t_last = [pt_free[0], pt_free[1], pt_free[2], pt_free[3]]

            def body(g):
                if g + 1 < NG:
                    xt[g + 1] = group_T(g + 1, X[:, 4 * g + 4:4 * g + 8, :], xg(g + 1))
                k = g % 2
                done = []
                for m in range(4):
                    ba, bb = bank(), bank()
                    ta = pe(lambda e, m=m, ba=ba: e.matmul(PSB[ba], wb["w1T"][:, 128 * m:128 * m + 128], xT[:, k, :], start=True, stop=True),
                            xt[g], bank_free[ba], *t_wb, inc=True)
                    tb = pe(lambda e, m=m, bb=bb: e.matmul(PSB[bb], wb["w2T"][:, 128 * m:128 * m + 128], xT[:, k, :], start=True, stop=True),
                            bank_free[bb], inc=True)
                    a = m % 2
                    t = act(lambda e, m=m, ba=ba, a=a: e.activation(AT[:, a, :], PSB[ba], ACT.Silu, scale=col("w1_s", m)), ta, at_free[a], t_cols)
                    bank_free[ba] = t
                    t = dve(lambda e, m=m, bb=bb, a=a: e.scalar_tensor_tensor(out=hA[:, m, :], in0=PSB[bb], scalar=col("w2_s", m), in1=AT[:, a, :],
                                                                             op0=ALU.mult, op1=ALU.mult), t, tb, hb_free[0], *t_last)
                    bank_free[bb] = at_free[a] = t
                    done.append(t)
                xT_free[k] = tb
                src, sk = hA, 0
                for wname, sname in (("h1T", "h1_s"), ("h2T", "h2_s")):
                    dst = hB if sk == 0 else hA
                    nxt = []
                    for m in range(4):
                        ba = bank()
                        for c in range(4):
                            t = pe(lambda e, m=m, c=c, ba=ba, src=src, wname=wname: e.matmul(
                                PSB[ba], wb[wname][:, 512 * c + 128 * m:512 * c + 128 * m + 128], src[:, c, :], start=(c == 0), stop=(c == 3)),
                                done[c], bank_free[ba], inc=(c == 3))
                        t = act(lambda e, m=m, ba=ba, dst=dst, sname=sname: e.activation(dst[:, m, :], PSB[ba], ACT.Gelu, scale=col(sname, m)),
                                t, hb_free[1 - sk], *t_last)
                        bank_free[ba] = t
                        nxt.append(t)
                    hb_free[sk] = (Q.sem["pe"], Q.count["pe"])
                    src, done, sk = dst, nxt, 1 - sk
                by = bank()
                for j in range(4):
                    for c in range(4):
                        t = pe(lambda e, j=j, c=c, src=src: e.matmul(PSB[by][:, 128 * j:128 * j + 128], src[:, c, 128 * j:128 * j + 128],
                                                                     wb["w3T"][:, 128 * c:128 * c + 128], start=(c == 0), stop=(c == 3)),
                               done[c], bank_free[by], inc=(c == 3 and j == 3))
                hb_free[sk] = t
                P4 = PSB[by].rearrange("p (b d) -> p b d", b=4)
                a = 0
                A4 = AT[:, a, :].rearrange("p (b d) -> p b d", b=4)
                t = dve(lambda e: e.tensor_tensor(A4, P4, rows[:, 0, :].unsqueeze(1).broadcast_to([128, 4, 128]), ALU.mult), t, t_s3, at_free[a])
                bank_free[by] = t
                t = dve(lambda e: e.tensor_tensor(X[:, 4 * g:4 * g + 4, :], X[:, 4 * g:4 * g + 4, :], A4, ALU.add), t, *xg(g))
                at_free[a] = t
                for j in range(4):
                    x_tok[4 * g + j] = t

            for g in range(NG):
                body(g)
            for i in range(4):
                pt_free[i] = hb_free[0]
            return hb_free, at_free

        if stop >= 2:
            ffn0()
        pe_after_ffn0 = (Q.sem["pe"], Q.count["pe"])

        def v_out(bank, p, H, dh, t):
            dst = VS[:, p % 4, 0:2 * H * (dh + 1)].rearrange("p (n d) -> p n d", d=dh + 1)
            t = act(lambda e: e.activation(dst[:, :, 0:dh], PSB[bank][:, 0:2 * H * dh].rearrange("p (n d) -> p n d", d=dh), ACT.Copy),
                    t, vs_free[p % 4])
            bank_free[bank] = t
            return t

        oT_free = [None] * 2

        def prep_x1(p):
            k = p % 2
            got = {}

            def n1():
                got["n"] = norm(X[:, 2 * p:2 * p + 2, :], 2, (x_tok[2 * p], x_tok[2 * p + 1], xn_free[k]),
                                lambda j: xn[:, k, 128 * j:128 * j + 128])

            def n2():
                got["T"] = turned(k, 2, 7, got["n"])

            def qk():
                w = wsm["w_qkvT"]
                pe(lambda e: e.matmul(PSB[7][:, 0:256], w[:, 0:128], xT[:, k, 0:256], start=True, stop=True), got["T"], t_ws, bank_free[7])
                t = pe(lambda e: e.matmul(PSB[7][:, 256:512], w[:, 128:256], xT[:, k, 0:256], start=True, stop=True), inc=True)
                ta = act(lambda e: e.activation(sp32[:, 0, :], PSB[7][:, 0:256], ACT.Copy, scale=float(np.float32(8 ** -0.5))), t, sp_free[0])
                tb = act(lambda e: e.activation(sp32[:, 1, :], PSB[7][:, 256:512], ACT.Copy), t, sp_free[1])
                bank_free[7] = tb
                sp_free[0], got["q"] = split_out(sp32[:, 0, :], ta, sc_q[1], p, "q")
                sp_free[1], got["k"] = split_out(sp32[:, 1, :], tb, sc_s[0], p, "s")

            def vv():
                for j in range(2):
                    t = pe(lambda e, j=j: e.matmul(PSB[7][:, 128 * j:128 * j + 128], xT[:, k, 128 * j:128 * j + 128],
                                                   wsm["w_qkvT"][:, 256:384], start=True, stop=True), got["T"], bank_free[7], inc=(j == 1))
                xT_free[k] = t
                got["v"] = v_out(7, p, 16, 8, t)

            def loads():
                tq = load_rows(Q8, "q8", sc_q[1], QO, p, 8, 16, (got["q"], q8_free[p % 3]))
                tk = load_rows(K8, "k8", sc_k, KO, p, 8, 16, (k_in[p], k8_free[p % 3]))
                t2 = load_rows(KS, "ks", sc_s[0], KO, p, 8, 16, (got["k"], ks_free[p % 3]))
                return {"qk": [tq, tk, t2], "v": [load_v(p, 16, 8), got["v"]]}
            return [n1, n2, qk, vv, loads]

        def finish_mm(n, wname, end):
            def finish(b, k, t):
                def turn():
                    tp = pe(lambda e: e.transpose(PSB[7][0:n, 0:128], otmp[:, k, 0:n], C("ident")), t, bank_free[7], inc=True)
                    rec_free[k] = tp
                    ta = act(lambda e: e.activation(oT[0:n, k, :], PSB[7][0:n, 0:128], ACT.Copy), tp, oT_free[k])
                    bank_free[7] = ta

                    def mul():
                        tm = pe(lambda e: e.matmul(PSB[7][:, 0:128], oT[0:n, k, :], wsm[wname], start=True, stop=True), ta, t_ws,
                                bank_free[7], inc=True)
                        oT_free[k] = tm
                        end(b, k, tm)
                    later.append(mul)
                later.append(turn)
            return finish

        ptmp_free = [None] * 2

        def end_x1(b, k, t):
            t = dve(lambda e: e.tensor_tensor(AT[:, 0, 128 * k:128 * k + 128], PSB[7][:, 0:128], rows[:, 1, :], ALU.add), t, t_row1,
                    ptmp_free[k])
            bank_free[7] = t
            t = dve(lambda e: e.scalar_tensor_tensor(out=X[:, b, :], in0=AT[:, 0, 128 * k:128 * k + 128], scalar=tg[:, 1:2], in1=X[:, b, :],
                                                     op0=ALU.mult, op1=ALU.add), t, x_tok[b], t_tg)
            x_tok[b] = ptmp_free[k] = t

        if stop >= 3:
            attention(16, 8, 8, [0], [0], prep_x1, finish_mm(128, "w_projT", end_x1))

        t_m = None

        def load_moe1(t):
            for name, at in (("m1", 0), ("m3", 2048), ("m2", 4096)):
                tt = Q.dma("wb2", WB[:, at:at + 2048], io[name], (t,))
            return tt

        def prep_f1(p):
            k = p % 2
            got = {}
            if p < 3:
                ks_free[p % 3] = pool(lambda e: e.memset(KS[0:64, p % 3, :], 0.0), ks_free[p % 3])

            def n1():
                t = norm(X[:, 2 * p:2 * p + 2, :], 2, (x_tok[2 * p], x_tok[2 * p + 1]), lambda j: U[:, 2 * p + j, :])
                u_tok[2 * p] = u_tok[2 * p + 1] = t
                t = norm(U[:, 2 * p:2 * p + 2, :], 2, (t, xn_free[k]), lambda j: xn[:, k, 128 * j:128 * j + 128], rms=True)
                got["T"] = turned(k, 2, 7, t, scale=col("g1"))

            def cc():
                t = pe(lambda e: e.matmul(PSB[7][0:64, 0:256], wsm["w_down"], xT[:, k, 0:256], start=True, stop=True), got["T"], t_ws,
                       bank_free[7], inc=True)
                xT_free[k] = t
                got["c"] = bank_free[7] = act(lambda e: e.activation(sp32[0:64, k, :], PSB[7][0:64, 0:256], ACT.Copy), t, sp_free[k])

            def qk():
                c = sp32[0:64, k, :]
                pe(lambda e: e.matmul(PSB[7][:, 0:256], wsm["wqk"], c, start=True, stop=True), got["c"], bank_free[7])
                t = pe(lambda e: e.matmul(PSB[7][:, 256:512], wsm["wqk_sw"], c, start=True, stop=True), inc=True)
                P = PSB[7].rearrange("p (a b t) -> p a b t", a=2, b=2)
                o = [AT[:, 0, 256 * i:256 * i + 256] for i in range(2)]
                o3 = [x.rearrange("p (b t) -> p b t", b=2) for x in o]
                t1 = dve(lambda e: e.tensor_tensor(o3[0], P[:, 0], C("cos").unsqueeze(1).broadcast_to([128, 2, 128]), ALU.mult), t, ptmp_free[0])
                t1 = dve(lambda e: e.tensor_tensor(o3[1], P[:, 1], C("sin").unsqueeze(1).broadcast_to([128, 2, 128]), ALU.mult), t)
                bank_free[7] = t1
                t1 = dve(lambda e: e.tensor_tensor(o[0], o[0], o[1], ALU.add), t1)
                ptmp_free[0], got["q"] = split_out(o[0], t1, sc_q[2], p, "q")

            def vv():
                for j in range(2):
                    t = pe(lambda e, j=j: e.matmul(PSB[7][:, 64 * j:64 * j + 64], sp32[0:64, k, 128 * j:128 * j + 128], wsm["wv"],
                                                   start=True, stop=True), bank_free[7], inc=(j == 1))
                sp_free[k] = t
                got["v"] = v_out(7, p, 16, 4, t)

            def loads():
                tq = load_rows(Q8, "q8", sc_q[2][:, 0:64], QO, p, 4, 16, (got["q"], q8_free[p % 3]))
                tk = load_rows(KS, "ks", sc_q[2][:, 64:128], KO, p, 4, 16, (got["q"], ks_free[p % 3]))
                return {"qk": [tq, tk], "v": [got["v"]]}
            return [n1, cc, qk, vv, loads]

        def end_f1(b, k, t):
            t = dve(lambda e: e.tensor_tensor(U[:, b, :], PSB[7][:, 0:128], U[:, b, :], ALU.add), t, u_tok[b])
            bank_free[7] = u_tok[b] = t

        def set_ones(d):
            for q in range(4):
                for vt, fr in ((VA, va_free), (VS, vs_free)):
                    fr[q] = pool(lambda e, vt=vt, q=q: e.memset(vt[:, q, :], 1.0), fr[q])

        def moe_front(g, rms, wname, scale, bcol, eps_row=None, first=None):
            dst = TT[:, 512 * g:512 * g + 512]
            t = group_T(g, U[:, 4 * g:4 * g + 4, :], [u_tok[4 * g + j] for j in range(4)], rms=rms, scale=scale, bcol=bcol,
                        dst=dst, dst_free=first)
            ba = bank()
            for j in range(4):
                tp = pe(lambda e, j=j: e.matmul(PSB[ba][:, 8 * j:8 * j + 8], TT[:, 512 * g + 128 * j:512 * g + 128 * j + 128], wsm[wname],
                                                start=True, stop=True), t, t_ws, bank_free[ba], inc=(j == 3))
            P = PSB[ba][:, 0:32].rearrange("p (b e) -> p b e", b=4)
            L = LG[:, 4 * g:4 * g + 4, :]
            if eps_row is None:
                tl = dve(lambda e: e.tensor_copy(L, P), tp)
            else:
                tl = dve(lambda e: e.tensor_tensor(L, P, eps_row.unsqueeze(1).broadcast_to([128, 4, 8]), ALU.add), tp, t_rows2)
            bank_free[ba] = tl
            return t, tl

        small = sb("small", [128, 3, 32])

        def gates(t, plus, w):
            big = [HB[:, 4 * i:4 * i + 4, :].rearrange("p a b -> p (a b)").rearrange("p (b i j) -> p b i j", b=32, i=8) for i in range(2)]
            bc = lambda x: x.unsqueeze(2).broadcast_to([128, 32, 8])
            t = dve(lambda e: e.tensor_reduce(small[:, 0, :], LG[:, :, :], AX.X, ALU.max), t)
            t = dve(lambda e: e.tensor_tensor(LG[:, :, :], LG[:, :, :], bc(small[:, 0, :]), ALU.subtract), t)
            t = act(lambda e: e.activation(LG[:, :, :], LG[:, :, :], ACT.Exp), t)
            t = dve(lambda e: e.tensor_reduce(small[:, 0, :], LG[:, :, :], AX.X, ALU.add), t)
            t = dve(lambda e: e.reciprocal(small[:, 1, :], small[:, 0, :]), t)
            t = dve(lambda e: e.tensor_tensor(LG[:, :, :], LG[:, :, :], bc(small[:, 1, :]), ALU.mult), t)
            pj = LG[:, :, :].unsqueeze(2).broadcast_to([128, 32, 8, 8])
            pi = LG[:, :, :].unsqueeze(3).broadcast_to([128, 32, 8, 8])
            low = C("low").rearrange("p (i j) -> p i j", i=8).unsqueeze(1).broadcast_to([128, 32, 8, 8])
            dve(lambda e: e.tensor_tensor(big[0], pj, pi, ALU.is_gt), t, *w)
            t = dve(lambda e: e.tensor_tensor(big[1], pj, pi, ALU.is_equal), t)
            t = dve(lambda e: e.tensor_tensor(big[1], big[1], low, ALU.mult), t)
            t = dve(lambda e: e.tensor_tensor(big[0], big[0], big[1], ALU.add), t)
            t = dve(lambda e: e.tensor_reduce(GT[:, :, :], big[0], AX.X, ALU.add), t)
            t = dve(lambda e: e.scalar_tensor_tensor(out=GT[:, :, :], in0=GT[:, :, :], scalar=1.5, in1=LG[:, :, :], op0=ALU.is_lt,
                                                     op1=ALU.mult), t)
            t = dve(lambda e: e.tensor_reduce(small[:, 0, :], GT[:, :, :], AX.X, ALU.add), t)
            if plus:
                t = dve(lambda e: e.tensor_scalar(small[:, 0, :], small[:, 0, :], plus, None, ALU.add), t)
            t = dve(lambda e: e.reciprocal(small[:, 1, :], small[:, 0, :]), t)
            return dve(lambda e: e.tensor_tensor(GT[:, :, :], GT[:, :, :], bc(small[:, 1, :]), ALU.mult), t)

        def moe_back(g, ex, hid, nc_, w2, t_hid, t_gate, hid_free):
            by = bank()
            for j in range(4):
                for c in range(nc_):
                    t = pe(lambda e, j=j, c=c: e.matmul(PSB[by][:, 128 * j:128 * j + 128], hid[c][:, 128 * j:128 * j + 128], w2(ex, c),
                                                        start=(c == 0), stop=(c == nc_ - 1)), *t_hid, bank_free[by],
                           inc=(c == nc_ - 1 and j == 3))
            hid_free(t)
            for j in range(4):
                b = 4 * g + j
                tu = dve(lambda e, j=j, b=b: e.scalar_tensor_tensor(out=U[:, b, :], in0=PSB[by][:, 128 * j:128 * j + 128],
                                                                    scalar=GT[:, b, ex:ex + 1], in1=U[:, b, :], op0=ALU.mult, op1=ALU.add),
                         t, t_gate, u_tok[b])
                u_tok[b] = tu
            bank_free[by] = tu

        def moe_end(g, gi):
            b = 4 * g
            t = dve(lambda e: e.scalar_tensor_tensor(out=X[:, b:b + 4, :], in0=U[:, b:b + 4, :], scalar=tg[:, gi:gi + 1], in1=X[:, b:b + 4, :],
                                                     op0=ALU.mult, op1=ALU.add), t_tg, *[u_tok[b + j] for j in range(4)], *xg(g))
            for j in range(4):
                x_tok[b + j] = u_tok[b + j] = t

        at_free = [None, None]
        chunk_free = [None] * 8

        if stop >= 4:
            t_m = load_moe1((Q.sem["pe"], pe_after_ffn0[1]))
            set_ones(4)
            attention(16, 4, 4, [], [0], prep_f1, finish_mm(64, "w_up", end_f1), causal=True)
            k8w = [x for x in k8_free]
            for g in range(NG):
                tt, tl = moe_front(g, True, "router_w", col("g2"), None, first=k8w[g % 3] if g else k8w[0])
            t_gate = gates(tl, None, pt_free)
            chunk_free = [t_gate] * 8
            at_free = [ptmp_free[0], ptmp_free[1]]

            def moe1(g):
                prev = None
                for ex in range(8):
                    hid, th = [], []
                    for c in range(2):
                        slot = (2 * ex + c) % 8
                        ba, bb = bank(), bank()
                        o = 256 * ex + 128 * c
                        ta = pe(lambda e, o=o, ba=ba: e.matmul(PSB[ba], WB[:, o:o + 128], TT[:, 512 * g:512 * g + 512], start=True, stop=True),
                                t_m, tt, bank_free[ba], inc=True)
                        tb = pe(lambda e, o=o, bb=bb: e.matmul(PSB[bb], WB[:, 2048 + o:2048 + o + 128], TT[:, 512 * g:512 * g + 512],
                                                               start=True, stop=True), bank_free[bb], inc=True)
                        t = act(lambda e, ba=ba, c=c: e.activation(AT[:, c, :], PSB[ba], ACT.Silu), ta, at_free[c])
                        bank_free[ba] = t
                        t = dve(lambda e, bb=bb, c=c, slot=slot: e.tensor_tensor(HB[:, slot, :], PSB[bb], AT[:, c, :], ALU.mult), t, tb,
                                chunk_free[slot])
                        bank_free[bb] = at_free[c] = t
                        hid.append(HB[:, slot, :])
                        th.append(t)
                    if prev:
                        moe_back(g, *prev)

                    def freed(tok, ex=ex):
                        for c in range(2):
                            chunk_free[(2 * ex + c) % 8] = tok
                    prev = (ex, hid, 2, lambda x, c: WB[:, 4096 + 256 * x + 128 * c:4096 + 256 * x + 128 * c + 128], th, t_gate, freed)
                moe_back(g, *prev)
                moe_end(g, 5)

            for g in range(NG):
                moe1(g)

        if stop >= 5:
            t_pe = (Q.sem["pe"], Q.count["pe"])
            t_ks = [Q.dma("w2", KS[:, :, :].rearrange("p a b -> p (a b)").bitcast(F32)[:, 0:4096], io["W2T"], tuple(ks_free))]
            t = pool(lambda e: e.memset(K8[96:128, :, :], 1.0), t_pe)
            k8_free = [t] * 3
            pt_free = [t_pe] * 4
            set_ones(16)
            attention(8, 16, 16, [0], [], prep_ctx(sc_q[3], 16, 2), finish_add(2), bias_i=1)

        rows2 = sb("rows2", [128, 8])
        b1 = sb("b1", [128, 32])
        b2 = sb("b2", [8, 128])
        gT = sb("gT", [8, 2, 512])
        if stop >= 6:
            t_rows2 = Q.dma("rows2", rows2[:, :], io["bg"].rearrange("(a n) -> a n", a=1).broadcast_to([128, 8]))
            t_b1 = Q.dma("b1", b1[:, :], io["b1"])
            t_b2 = Q.dma("b2", b2[:, :], io["b2"])
            W1 = Q8[:, :, :].rearrange("p a b -> p (a b)").bitcast(F32)
            W2 = KS[:, :, :].rearrange("p a b -> p (a b)").bitcast(F32)
            t_w1 = Q.dma("w1", W1[:, 0:4096], io["W1T"], tuple(q8_free))
            k8w = list(k8_free)
            for g in range(NG):
                t = norm(X[:, 4 * g:4 * g + 4, :], 4, xg(g), lambda j, g=g: U[:, 4 * g + j, :])
                for j in range(4):
                    u_tok[4 * g + j] = t
                tt, tl = moe_front(g, False, "WgT", col("gamma"), col("beta"), eps_row=rows2[:, :], first=t if g else k8w[0])
            t_gate = gates(tl, 1e-8, pt_free)
            chunk_free = [t_gate] * 8
            gT_free = [None] * 2

            def moe2(g):
                k = g % 2
                bt = bank()
                for j in range(4):
                    t = pe(lambda e, j=j: e.transpose(PSB[bt][0:8, 128 * j:128 * j + 128], GT[:, 4 * g + j, :], C("ident")), t_gate,
                           bank_free[bt], inc=(j == 3))
                t = act(lambda e: e.activation(gT[:, k, :], PSB[bt][0:8, :], ACT.Copy), t, gT_free[k])
                bank_free[bt] = t
                bc = bank()
                for j in range(4):
                    t2 = pe(lambda e, j=j: e.matmul(PSB[bc][:, 128 * j:128 * j + 128], gT[:, k, 128 * j:128 * j + 128], b2[:, :],
                                                    start=True, stop=True), t, t_b2, t_b1, bank_free[bc], inc=(j == 3))
                gT_free[k] = t2
                t = dve(lambda e: e.tensor_tensor(U[:, 4 * g:4 * g + 4, :], PSB[bc].rearrange("p (b d) -> p b d", b=4),
                                                  U[:, 4 * g:4 * g + 4, :], ALU.add), t2, *[u_tok[4 * g + j] for j in range(4)])
                bank_free[bc] = t
                for j in range(4):
                    u_tok[4 * g + j] = t
                prev = None
                for ex in range(8):
                    hid, th = [], []
                    for c in range(4):
                        slot = (4 * ex + c) % 8
                        ba = bank()
                        o = 512 * ex + 128 * c
                        ta = pe(lambda e, o=o, ba=ba: e.matmul(PSB[ba], W1[:, o:o + 128], TT[:, 512 * g:512 * g + 512], start=True, stop=True),
                                t_w1, tt, bank_free[ba], inc=True)
                        t = act(lambda e, ba=ba, slot=slot, i=4 * ex + c: e.activation(HB[:, slot, :], PSB[ba], ACT.Gelu, bias=b1[:, i:i + 1]),
                                ta, chunk_free[slot], t_b1, t_b2)
                        bank_free[ba] = t
                        hid.append(HB[:, slot, :])
                        th.append(t)
                    if prev:
                        moe_back(g, *prev)

                    def freed(tok, ex=ex):
                        for c in range(4):
                            chunk_free[(4 * ex + c) % 8] = tok
                    prev = (ex, hid, 4, lambda x, c: W2[:, 512 * x + 128 * c:512 * x + 128 * c + 128], th + t_ks, t_gate, freed)
                moe_back(g, *prev)
                moe_end(g, 6)

            for g in range(NG):
                moe2(g)

        if stop >= 7:
            t_pe = (Q.sem["pe"], Q.count["pe"])
            t_r0 = Q.dma("row0", rows[:, 0, :], row_bc("b_in", 0), (x_tok[0],))
            t_r1 = Q.dma("row1", rows[:, 1, :], row_bc("g_init", 1), (x_tok[0],))
            t_r1 = dve(lambda e: e.tensor_scalar(rows[:, 1, :], rows[:, 1, :], cu, None, ALU.mult), t_r1)
            bidx = small[:, 0, :]
            w = small[:, 1, :]
            t = dve(lambda e: e.tensor_copy(btmp[:, :], ints[:, 2, :]), t_i)
            b0 = bank()
            tp = pe(lambda e: e.matmul(PSB[b0][:, 0:32], C("tri"), btmp[:, :], start=True, stop=True), t, bank_free[b0], inc=True)
            t = dve(lambda e: e.tensor_scalar(bidx, PSB[b0][:, 0:32], -1.0, None, ALU.add), tp)
            bank_free[b0] = t
            t = dve(lambda e: e.tensor_scalar(w, bidx, 0.0, 128.0, ALU.is_lt, ALU.mult), t)
            t_bidx = dve(lambda e: e.tensor_tensor(bidx, bidx, w, ALU.add), t)
            EB = Q8[:, 0, 0:4096].rearrange("p (b t) -> p b t", b=32)
            onesb = Q8[:, 1, 0:1]
            bm = Q8[:, 1, 32:64]
            t_on = dve(lambda e: e.memset(onesb, 1.0), t_pe)
            b0 = bank()
            for b in range(B):
                t = dve(lambda e, b=b: e.tensor_scalar(EB[:, b, :], C("iota_t"), bidx[:, b:b + 1], None, ALU.is_equal), t_bidx, t_pe)
                tp = pe(lambda e, b=b: e.matmul(PSB[b0][:, b:b + 1], EB[:, b, :], onesb, start=True, stop=True), t, t_on, bank_free[b0],
                        inc=True)
            t_bm = dve(lambda e: e.tensor_scalar(bm, PSB[b0][:, 0:32], 1.0, None, ALU.min), tp)
            bank_free[b0] = t_bm
            CX = HB[:, 0:4, :].rearrange("p a b -> p (a b)").rearrange("p (n b d) -> p n b d", n=2, b=4)
            UP, DD = HB[:, 4, :], HB[:, 5, :]
            GM, UN = HB[:, 6, :], HB[:, 7, :]
            cx_free, up_free, dd_free, gm_free, un_free = [t_pe] * 2, [t_pe], [t_pe], [t_pe], [t_pe]

            def depool(g):
                k = g % 2
                tc = Q.dma(f"cx{k}", CX[:, k], io["ctx_2048"][4 * g:4 * g + 4].rearrange("b t d -> t b d"), (cx_free[k],))
                t = norm(CX[:, k], 4, (tc, up_free[0]), lambda j: UP[:, 128 * j:128 * j + 128], rms=True)
                cx_free[k] = t
                U4 = UP.rearrange("p (b d) -> p b d", b=4)
                t = dve(lambda e: e.tensor_tensor(U4, U4, rows[:, 1, :].unsqueeze(1).broadcast_to([128, 4, 128]), ALU.mult), t, t_r1)
                b0 = bank()
                t = pe(lambda e: e.matmul(PSB[b0], C("toep"), UP, start=True, stop=True), t, bank_free[b0], inc=True)
                up_free[0] = t
                t_dd = act(lambda e: e.activation(DD, PSB[b0], ACT.Copy), t, dd_free[0])
                bank_free[b0] = t_dd
                b1_ = bank()
                for j in range(4):
                    t = pe(lambda e, j=j: e.matmul(PSB[b1_][:, 128 * j:128 * j + 128], bm[:, 4 * g + j:4 * g + j + 1].broadcast_to([128, 128]),
                                                   trib[:, :], start=True, stop=True), t_bm, t_cb, bank_free[b1_], inc=(j == 3))
                t = dve(lambda e: e.tensor_scalar(GM, PSB[b1_], -1.0, 0.0, ALU.add, ALU.max), t, gm_free[0])
                bank_free[b1_] = t
                t_gm = dve(lambda e: e.tensor_scalar(GM, GM, 127.0, C("iota_p"), ALU.min, ALU.is_equal), t)
                t = norm(X[:, 4 * g:4 * g + 4, :], 4, (*xg(g), un_free[0]), lambda j: UN[:, 128 * j:128 * j + 128])
                t_h = group_T(g, UN.rearrange("p (b d) -> p b d", b=4), (t,), rms=True, scale=col("g_res"))
                un_free[0] = xn_free[k]
                b2_ = bank()
                for j in range(4):
                    o = slice(128 * j, 128 * j + 128)
                    pe(lambda e, o=o: e.matmul(PSB[b2_][:, o], GM[:, o], DD[:, o], start=True, stop=False), t_gm, t_dd, bank_free[b2_])
                    t = pe(lambda e, o=o: e.matmul(PSB[b2_][:, o], xT[:, k, o], wsm["W_inT"], start=False, stop=True), t_h, inc=(j == 3))
                dd_free[0] = gm_free[0] = xT_free[k] = t
                A4 = AT[:, 0, :].rearrange("p (b d) -> p b d", b=4)
                t = dve(lambda e: e.tensor_tensor(A4, PSB[b2_].rearrange("p (b d) -> p b d", b=4),
                                                  rows[:, 0, :].unsqueeze(1).broadcast_to([128, 4, 128]), ALU.add), t, t_r0)
                bank_free[b2_] = t
                t = dve(lambda e: e.scalar_tensor_tensor(out=X[:, 4 * g:4 * g + 4, :], in0=A4, scalar=tg[:, 3:4], in1=X[:, 4 * g:4 * g + 4, :],
                                                         op0=ALU.mult, op1=ALU.add), t, t_tg, *xg(g))
                for j in range(4):
                    x_tok[4 * g + j] = t

            for g in range(NG):
                depool(g)

        MAGIC = 12582912.0
        if stop >= 8:
            t_pe = (Q.sem["pe"], Q.count["pe"])
            t_dve = (Q.sem["dve"], Q.count["dve"])
            for i, name in enumerate(("qg", "qu", "qd")):
                t = Q.dma("wb3", WB[:, 512 * i:512 * i + 512], io[name], (t_pe,))
            W3 = WB[:, 0:1536].rearrange("p (n w) -> p n w", n=3)
            wt = WB[:, 1536:2304].bitcast(BF16).rearrange("p (n w) -> p n w", n=3)
            ws = small[:, 2, :]
            t = dve(lambda e: e.tensor_reduce(ws[:, 0:3], W3, AX.X, ALU.add, apply_absolute_value=True), t)
            b0 = bank()
            tp = pe(lambda e: e.matmul(PSB[b0][:, 0:3], C("ones"), ws[:, 0:3], start=True, stop=True), t, bank_free[b0], inc=True)
            t = dve(lambda e: e.tensor_scalar(ws[:, 4:7], PSB[b0][:, 0:3], 1.0 / 65536.0, 1e-5, ALU.mult, ALU.max), tp)
            bank_free[b0] = t
            t = dve(lambda e: e.reciprocal(ws[:, 8:11], ws[:, 4:7]), t)
            t_w = dve(lambda e: e.reciprocal(ws[:, 12:15], ws[:, 8:11]), t)
            for i in range(3):
                t = dve(lambda e, i=i: e.tensor_scalar(W3[:, i, :], W3[:, i, :], ws[:, 8 + i:9 + i], MAGIC, ALU.mult, ALU.add), t_w)
                t = dve(lambda e, i=i: e.tensor_scalar(W3[:, i, :], W3[:, i, :], -MAGIC, 1.0, ALU.add, ALU.min), t)
                t_wt = dve(lambda e, i=i: e.tensor_scalar(wt[:, i, :], W3[:, i, :], -1.0, None, ALU.max), t)
            qn = comp[:, 0:2, 0:512]
            qT = comp[:, 2:4, 0:512]
            q2 = Q8[:, 0, 0:2048].rearrange("p (k w) -> p k w", k=4)
            q2T = Q8[:, 1, 0:2048].rearrange("p (k w) -> p k w", k=4)
            sc = sb("sc", [128, 2, 4, 8])
            qn_free, qT_free, sc_free = [t_pe] * 2, [t_pe] * 2, [None] * 2
            h_free, q2_free, q2T_free, at2 = [t_pe] * 4, [t_pe] * 4, [t_pe] * 4, [t_dve] * 2

            def quant(src, am, inv, dst, tmp, t, w):
                t = dve(lambda e: e.tensor_scalar(am, am, 1e-5, None, ALU.max), t)
                t = dve(lambda e: e.reciprocal(inv, am), t)
                t_s = dve(lambda e: e.tensor_scalar(am, inv, 127.0, None, ALU.mult), t)
                t = dve(lambda e: e.tensor_scalar(tmp, src, am, MAGIC, ALU.mult, ALU.add), t_s)
                t = dve(lambda e: e.tensor_scalar(dst, tmp, -MAGIC, 127.0, ALU.add, ALU.min), t, *w)
                ti = dve(lambda e: e.reciprocal(inv, am), t_s)
                return t, ti

            def ffn3_in(g):
                k = g % 2
                t = norm(X[:, 4 * g:4 * g + 4, :], 4, (*xg(g), xn_free[k], sc_free[k]), lambda j: xn[:, k, 128 * j:128 * j + 128])
                am = sc[:, k, :, 0:1]
                t = dve(lambda e: e.tensor_reduce(am, xn[:, k, :].rearrange("p (b d) -> p b d", b=4), AX.X, ALU.max,
                                                  apply_absolute_value=True), t)
                for j in range(4):
                    xj = xn[:, k, 128 * j:128 * j + 128]
                    t, ti = quant(xj, sc[:, k, j, 0:1], sc[:, k, j, 1:2], qn[:, k, 128 * j:128 * j + 128], xj, t, (qn_free[k],))
                xn_free[k] = t
                for i in range(2):
                    ti = dve(lambda e, i=i: e.tensor_scalar(sc[:, k, :, 2 + i:3 + i], sc[:, k, :, 1:2], ws[:, 12 + i:13 + i], None, ALU.mult), ti)
                b0 = bank()
                for j in range(4):
                    tp = pe(lambda e, j=j: e.transpose(PSB[b0].bitcast(BF16)[:, 128 * j:128 * j + 128], qn[:, k, 128 * j:128 * j + 128],
                                                       identb[:, :]), t, bank_free[b0], inc=(j == 3))
                qn_free[k] = tp
                t = act(lambda e: e.activation(qT[:, k, :], PSB[b0].bitcast(BF16)[:, 0:512], ACT.Copy), tp, qT_free[k])
                bank_free[b0] = t
                return t, ti

            def ffn3_up(b, t_q, t_sc):
                g, j = divmod(b, 4)
                k, s4 = g % 2, b % 4
                ba, bb = bank(), bank()
                ta = pe(lambda e: e.matmul(PSB[ba], qT[:, k, 128 * j:128 * j + 128], wt[:, 0, :], start=True, stop=True), t_q, t_wt,
                        bank_free[ba], inc=True)
                tb = pe(lambda e: e.matmul(PSB[bb], qT[:, k, 128 * j:128 * j + 128], wt[:, 1, :], start=True, stop=True), bank_free[bb],
                        inc=True)
                if j == 3:
                    qT_free[k] = tb
                t = act(lambda e: e.activation(AT[:, b % 2, :], PSB[ba], ACT.Silu, scale=sc[:, k, j, 2:3]), ta, t_sc, at2[b % 2])
                bank_free[ba] = t
                t = dve(lambda e: e.scalar_tensor_tensor(out=HB[:, s4, :], in0=PSB[bb], scalar=sc[:, k, j, 3:4], in1=AT[:, b % 2, :],
                                                         op0=ALU.mult, op1=ALU.mult), t, tb, h_free[s4])
                bank_free[bb] = at2[b % 2] = t
                t = dve(lambda e: e.tensor_reduce(sc[:, k, j, 4:5], HB[:, s4, :], AX.X, ALU.max, apply_absolute_value=True), t)
                t, ti = quant(HB[:, s4, :], sc[:, k, j, 4:5], sc[:, k, j, 5:6], q2[:, s4, :], HB[:, s4, :], t, (q2_free[s4],))
                h_free[s4] = t
                ti = dve(lambda e: e.tensor_scalar(sc[:, k, j, 6:7], sc[:, k, j, 5:6], ws[:, 14:15], tg[:, 7:8], ALU.mult, ALU.mult), ti, t_tg)
                return t, ti

            def ffn3_down(b, t, ti):
                g, j = divmod(b, 4)
                k, s4 = g % 2, b % 4
                b0, b1_ = bank(), bank()
                for c in range(4):
                    tp = pe(lambda e, c=c: e.transpose(PSB[b0].bitcast(BF16)[:, 128 * c:128 * c + 128], q2[:, s4, 128 * c:128 * c + 128],
                                                       identb[:, :]), t, bank_free[b0], inc=(c == 3))
                q2_free[s4] = tp
                t = act(lambda e: e.activation(q2T[:, s4, :], PSB[b0].bitcast(BF16)[:, 0:512], ACT.Copy), tp, q2T_free[s4])
                bank_free[b0] = t
                for c in range(4):
                    t2 = pe(lambda e, c=c: e.matmul(PSB[b1_][:, 0:128], q2T[:, s4, 128 * c:128 * c + 128], wt[:, 2, 128 * c:128 * c + 128],
                                                    start=(c == 0), stop=(c == 3)), t, bank_free[b1_], inc=(c == 3))
                q2T_free[s4] = t2
                t = dve(lambda e: e.scalar_tensor_tensor(out=X[:, b, :], in0=PSB[b1_][:, 0:128], scalar=sc[:, k, j, 6:7], in1=X[:, b, :],
                                                         op0=ALU.mult, op1=ALU.add), t2, ti, x_tok[b])
                bank_free[b1_] = t
                x_tok[b] = t
                if j == 3:
                    sc_free[k] = t

            ins = {0: ffn3_in(0)}
            ups = {}
            for b in range(B + 2):
                if b % 4 == 2 and b // 4 + 1 < NG:
                    ins[b // 4 + 1] = ffn3_in(b // 4 + 1)
                if b < B:
                    ups[b] = ffn3_up(b, *ins[b // 4])
                if b >= 2:
                    ffn3_down(b - 2, *ups.pop(b - 2))

        t_o = Q.dma("out", out.rearrange("b t d -> t b d"), X[:, :, :], tuple(x_tok[b] for b in range(B)))
        Q.put("sp", lambda e: None, (t_o,), inc=False)

        blk = ctx.enter_context(nc.Block())
        blk.sync(lambda e: Q.emit("sp", e))
        blk.tensor(lambda e: Q.emit("pe", e))
        blk.vector(lambda e: Q.emit("dve", e))
        blk.scalar(lambda e: Q.emit("act", e))
        blk.gpsimd(lambda e: Q.emit("pool", e))


def layout(inputs):
    n = {k: np.asarray(v) for k, v in inputs.items()}
    c = np.ascontiguousarray

    def kT(w, k):
        return c(w.T.reshape(k, 128, w.shape[0]).transpose(1, 0, 2)).reshape(128, -1)

    def per_part(v):
        return c(v.reshape(-1, 128).T)

    a = {"x": c(n["x"]), "ctx_2048": c(n["ctx_2048"]), "seq": c(n["itok_Bx1_68_817"])}
    a["kT"] = c(n["ctx_2048"][:, :, :128].transpose(2, 0, 1)).reshape(128, B * S)
    a["maskT"] = c(n["mask_BxS2_ik0"].T)
    a["lensT"] = c(n["mask_BxS2_if0"].T)
    a["g_xattn"], a["g_ffn"] = c(n["g_xattn"]), c(n["g_ffn"])
    a["L0_xattn_b"] = per_part(n["L0_xattn_b"])
    a["L2_b"] = c(np.broadcast_to(n["L2_xattn_b"].reshape(1, 1), (128, 1)))
    for k in ("w1_s", "w2_s", "h1_s", "h2_s"):
        a[k] = per_part(n["L0_ffn_" + k])
    a["w3_s"] = c(n["L0_ffn_w3_s"])
    a["w1T"], a["w2T"] = kT(n["L0_ffn_w1_w"], 1), kT(n["L0_ffn_w2_w"], 1)
    a["h1T"], a["h2T"], a["w3T"] = kT(n["L0_ffn_h1_w"], 4), kT(n["L0_ffn_h2_w"], 4), kT(n["L0_ffn_w3_w"], 4)
    a["w_qkvT"], a["w_projT"] = c(n["L1_xattn_w_qkv"].T), c(n["L1_xattn_w_proj"].T)
    a["b_proj"] = c(n["L1_xattn_b_proj"])
    a["g1"], a["g2"] = per_part(n["L1_ffn_g1"]), per_part(n["L1_ffn_g2"])
    a["w_down"] = c(n["L1_ffn_w_down"])
    sw = np.arange(64) ^ 1
    a["wqk"] = c(np.concatenate([n["L1_ffn_wq"], n["L1_ffn_wk"]], 1))
    a["wqk_sw"] = c(np.concatenate([n["L1_ffn_wq"][:, sw], n["L1_ffn_wk"][:, sw]], 1))
    a["wv"], a["w_up"], a["router_w"] = c(n["L1_ffn_wv"]), c(n["L1_ffn_w_up"]), c(n["L1_ffn_router_w"])
    a["m1"] = c(n["L1_ffn_w1"].transpose(1, 0, 2)).reshape(128, 2048)
    a["m3"] = c(n["L1_ffn_w3"].transpose(1, 0, 2)).reshape(128, 2048)
    a["m2"] = c(n["L1_ffn_w2"].reshape(16, 128, 128).transpose(1, 0, 2)).reshape(128, 2048)
    a["gamma"], a["beta"] = per_part(n["L2_ffn_gamma"]), per_part(n["L2_ffn_beta"])
    a["WgT"], a["bg"] = c(n["L2_ffn_Wg"].T), c(n["L2_ffn_bg"])
    a["W1T"] = c(n["L2_ffn_W1"].transpose(2, 0, 1)).reshape(128, 4096)
    a["b1"] = per_part(n["L2_ffn_b1"])
    a["W2T"] = c(n["L2_ffn_W2"].transpose(0, 2, 1).reshape(32, 128, 128).transpose(1, 0, 2)).reshape(128, 4096)
    a["b2"] = c(n["L2_ffn_b2"])
    a["W_inT"], a["b_in"] = c(n["L3_xattn_W_in"].T), c(n["L3_xattn_b_in"])
    a["g_res"], a["g_init"] = per_part(n["L3_xattn_g_res"]), c(n["L3_xattn_g_init"])
    a["qg"], a["qu"], a["qd"] = kT(n["L3_ffn_w_gate"], 1), kT(n["L3_ffn_w_up"], 1), kT(n["L3_ffn_w_down"], 4)
    return a


def kernel(**inputs):
    import concourse.bacc as _bacc
    from concourse.bass_utils import run_bass_kernel_spmd as _run

    nc = _bacc.Bacc("TRN2", target_bir_lowering=False, num_devices=1)
    block, cu = const_block()
    arrays = {f"in_{k}": v for k, v in {**layout(inputs), "cst": block}.items()}
    io = {k[3:]: nc.dram_tensor(k, v.shape, mybir.dt.from_np(v.dtype), kind="ExternalInput").ap() for k, v in arrays.items()}
    out = nc.dram_tensor("out", (B, S, D), F32, kind="ExternalOutput").ap()
    build(nc, io, out, cu)
    r = _run(nc, [arrays], core_ids=[0])
    return r.results[0]["out"]
```

```python
from contextlib import ExitStack

import numpy as np

import concourse.bass as bass
from concourse import mybir

F32 = mybir.dt.float32
BF16 = mybir.dt.bfloat16
I32 = mybir.dt.int32
ALU = mybir.AluOpType
ACT = mybir.ActivationFunctionType
AX = mybir.AxisListType

B, S, D = 32, 128, 128
NP = B // 2
NG = B // 4
PVLAG = 2
EPS = 1e-5

COLS = (("L0_xattn_b", 1), ("L2_b", 1), ("w1_s", 4), ("w2_s", 4), ("h1_s", 4), ("h2_s", 4), ("w3_s", 1), ("g1", 1), ("g2", 1),
        ("gamma", 1), ("beta", 1), ("g_res", 1), ("b1", 32))
SMALL = (("w_qkvT", 128, 384), ("w_projT", 128, 128), ("w_down", 128, 64), ("wqk", 64, 128), ("wqk_sw", 64, 128), ("wv", 64, 64),
         ("w_up", 64, 128), ("router_w", 128, 8), ("WgT", 128, 8), ("W_inT", 128, 128))
CST = {}


def by_place(n, d):
    return np.arange(n * d).reshape(n, d).T.reshape(-1)


def const_block():
    f = np.float32
    j = np.arange(128)[:, None]
    t = np.arange(128)[None, :]
    parts = []

    def put(name, a):
        CST[name] = (sum(p.shape[1] for p in parts), a.shape[1])
        parts.append(np.ascontiguousarray(a, f))

    put("ident", (j == t).astype(f))
    put("tri", (j <= t).astype(f))
    logp = f(-0.001)
    dt = f(-np.log(-np.expm1(logp)))
    a = f(np.exp(-dt))
    put("toep", np.where(t >= j, np.power(np.float64(a), np.maximum(t - j, 0)), 0.0))
    put("iota_t", np.broadcast_to(t, (128, 128)))
    put("iota_p", j.astype(f))
    put("cneg", np.where(t > j, -1e30, 0.0))
    put("cnegT", np.where(j > t, -1e30, 0.0))
    put("selb", (np.arange(128)[:, None] % 32 == np.arange(32)[None, :]).astype(f))
    put("sel8", (np.arange(128)[:, None] % 8 == np.arange(8)[None, :]).astype(f))
    inv = (f(1.0) / np.power(f(10000.0), np.arange(0, 4, 2, dtype=f) / f(4))).astype(f)
    ang = np.arange(128, dtype=f)[None, :] * inv[(np.arange(128) % 4) // 2][:, None]
    half = np.where(np.arange(128) < 64, 0.5, 1.0).astype(f)[:, None]
    sign = np.where(np.arange(128) % 2 == 0, -1.0, 1.0).astype(f)[:, None]
    place = np.concatenate([by_place(16, 4), 64 + by_place(16, 4)])
    put("cos", (np.cos(ang).astype(f) * half)[place])
    put("sin", (np.sin(ang).astype(f) * sign * half)[place])
    i8 = np.arange(64)
    put("low", np.broadcast_to((i8 % 8 < i8 // 8).astype(f)[None, :], (128, 64)))
    put("ones", np.ones((128, 128), f))
    put("half", np.full((128, 32), -0.5, f))
    return np.concatenate(parts, axis=1), float(f(dt * f(np.exp(logp))) / dt)


class Queues:

    def __init__(self, nc, ctx):
        self.nc = nc
        self.names = ["pe", "dve", "act", "pool", "sp"]
        self.list = {n: [] for n in self.names}
        self.count = {n: 0 for n in self.names}
        self.sem = {n: ctx.enter_context(nc.semaphore("done_" + n)) for n in self.names}
        self.dsem = {}
        self.dcount = {}
        self.ctx = ctx

    def put(self, eng, fn, waits, inc=True):
        self.list[eng].append((fn, tuple(w for w in waits if w is not None), (self.sem[eng], 1) if inc else None))
        if inc:
            self.count[eng] += 1
        return (self.sem[eng], self.count[eng])

    def dma(self, name, out, in_, waits=(), eng="sp", **kw):
        if name not in self.dsem:
            self.dsem[name] = self.ctx.enter_context(self.nc.semaphore("dma_" + name))
            self.dcount[name] = 0
        self.dcount[name] += 16
        self.list[eng].append((lambda e: e.dma_start(out, in_, **kw), tuple(w for w in waits if w is not None),
                               (self.dsem[name], 16)))
        return (self.dsem[name], self.dcount[name])

    def emit(self, eng, handle):
        seen = {}
        for fn, waits, inc in self.list[eng]:
            for s, v in waits:
                if seen.get(s.name, 0) < v:
                    handle.wait_ge(s, v)
                    seen[s.name] = v
            ins = fn(handle)
            if ins is not None and inc is not None:
                ins.then_inc(*inc)


def build(nc, io, out, cu, stop=99):
    ctx = ExitStack()
    with ctx:
        Q = Queues(nc, ctx)

        def sb(name, shape, dt=F32):
            return ctx.enter_context(nc.sbuf_tensor(name, shape, dt))

        def dve(fn, *w, inc=True):
            return Q.put("dve", fn, w, inc)

        def act(fn, *w):
            return Q.put("act", fn, w)

        def pool(fn, *w):
            return Q.put("pool", fn, (*w, (Q.sem["pool"], Q.count["pool"])))

        def pe(fn, *w, inc=False):
            return Q.put("pe", fn, w, inc)

        PSB = [ctx.enter_context(nc.psum_tensor(f"psb{i}", [128, 512], F32)) for i in (0, 1)]
        PSD = [ctx.enter_context(nc.psum_tensor(f"psd{i}", [128, 1024], F32)) for i in (0, 1)]
        PSB += [PSD[0][:, 0:512], PSD[0][:, 512:1024], PSD[1][:, 0:512], PSD[1][:, 512:1024]]
        PSB += [ctx.enter_context(nc.psum_tensor(f"psb{i}", [128, 512], F32)) for i in (6, 7)]
        PSB = [b[:, :] for b in PSB]
        bank_free = [None] * 8

        ncst = sum(w for _, w in CST.values())
        cst = sb("cst", [128, ncst])

        def C(name):
            o, w = CST[name]
            return cst[:, o:o + w]

        X = sb("X", [128, B, D])
        U = sb("U", [128, B, D])
        WB = sb("WB", [128, 6144])
        WS = sb("WS", [128, 1216])
        Q8 = sb("Q8", [128, 3, 4096], BF16)
        K8 = sb("K8", [128, 3, 4096], BF16)
        KS = sb("KS", [128, 3, 4096], BF16)
        HB = sb("HB", [128, 8, 512])
        AT = sb("AT", [128, 2, 512])
        TT = K8[:, :, :].rearrange("p a b -> p (a b)").bitcast(F32)
        tg = sb("tg", [128, 8])
        graw = sb("graw", [128, 8])
        cols = sb("cols", [128, sum(w for _, w in COLS)])
        rows = sb("rows", [128, 2, 128])
        identb = sb("identb", [128, 128], BF16)
        cnegb = sb("cnegb", [128, 2, 128], BF16)
        selbb = sb("selbb", [96, 32], BF16)
        sel8b = sb("sel8b", [24, 8], BF16)
        trib = sb("trib", [128, 128], BF16)
        bias = sb("bias", [128, 2, 32])
        biasc = sb("biasc", [128, 2, 96], BF16)
        biasT = sb("biasT", [96, 2, 128], BF16)
        btmp = sb("btmp", [128, 32])
        ints = sb("ints", [128, 3, 32], I32)
        st = sb("st", [128, 4, 4, 6])
        mv = sb("mv", [128, 4, 4, 2])
        rs = sb("rs", [128, 4, 4, 2])
        xn = sb("xn", [128, 2, 512])
        xT = sb("xT", [128, 2, 512])
        sp32 = sb("sp32", [128, 2, 256])
        r32 = sb("r32", [128, 2, 256])
        comp = sb("comp", [128, 4, 3 * 256], BF16)
        vraw = sb("vraw", [128, 3, 256])
        VA = sb("VA", [128, 4, 2 * 144])
        VS = sb("VS", [128, 4, 2 * 144])
        mneg = sb("mneg", [128, 4, 16])
        mres = sb("mres", [128, 16])
        mcb = sb("mcb", [128, 4, 48], BF16)
        mT = sb("mT", [48, 4, 128], BF16)
        rec = sb("rec", [128, 2, 16])
        otmp = sb("otmp", [128, 2, 128])
        oT = sb("oT", [128, 2, 128])
        LG = sb("LG", [128, B, 8])
        GT = sb("GT", [128, B, 8])
        OE = sb("OE", [128, 2, 512])

        def scratch(name, n=128):
            return nc.dram_tensor(name, [NP, 6, n, 256], BF16, kind="Internal").ap()

        sc_k = scratch("sc_k")
        sc_q = [scratch(f"sc_q{i}") for i in range(4)]
        sc_s = scratch("sc_s")
        sc_f = [scratch(f"sc_f{i}", 64) for i in range(2)]

        sp_free = [None, None]
        k_in = {}
        k_raw = {}

        def k_load(p):
            k_raw[p] = Q.dma(f"kin{p % 2}", sp32[:, p % 2, :], io["kT"][:, 256 * p:256 * p + 256], (sp_free[p % 2],))

        cut = (0, 4, 16, 32)
        t_x = []

        def x_load(i):
            t = Q.dma(f"x{i}", X[:, cut[i]:cut[i + 1], :], io["x"][cut[i]:cut[i + 1]].rearrange("b t d -> t b d"))
            t_x.extend([t] * (cut[i + 1] - cut[i]))

        k_load(0)
        x_load(0)
        t_cst = Q.dma("cst", cst[:, :], io["cst"])
        k_load(1)
        t_i = Q.dma("ints", ints[:, 0, :], io["seq"].rearrange("b a -> a b").broadcast_to([128, 32]))
        t_i = Q.dma("ints", ints[:, 1, :], io["maskT"])
        t_i = Q.dma("ints", ints[:, 2, :], io["lensT"])
        x_load(1)
        x_load(2)
        t_g = Q.dma("g", graw[:, 0:4], io["g_xattn"].rearrange("(a n) -> a n", a=1).broadcast_to([128, 4]))
        t_g = Q.dma("g", graw[:, 4:8], io["g_ffn"].rearrange("(a n) -> a n", a=1).broadcast_to([128, 4]))

        col_at = {}
        for name, n in COLS:
            col_at[name] = sum(w for nm, w in COLS[:len(col_at)])
        t_cols = Q.dma("cols", cols[:, 0:sum(w for _, w in COLS)], io["cols"])

        def col(name, i=0):
            return cols[:, col_at[name] + i:col_at[name] + i + 1]

        def row_bc(name, k, n=128):
            return io[name].rearrange("(a n) -> a n", a=1)[:, 0:n].broadcast_to([128, n])

        t_row1 = Q.dma("row1", rows[:, 1, :], row_bc("b_proj", 0))

        wb = {}
        wsm = {}
        t_wb = []
        t_ws = None
        at = 0
        for name, n in (("w1T", 512), ("w2T", 512), ("h1T", 2048), ("h2T", 2048), ("w3T", 512)):
            wb[name] = WB[:, at:at + n]
            at += n
        at = 0
        for name, p, n in SMALL:
            wsm[name] = WS[0:p, at:at + n]
            at += n

        def load_weights():
            nonlocal t_ws
            for name in wb:
                t_wb.append(Q.dma("wb", wb[name], io[name]))
            for name, _, _ in SMALL:
                t_ws = Q.dma("ws", wsm[name], io[name])
            del t_wb[:-1]

        t_idb = dve(lambda e: e.tensor_copy(identb[:, :], C("ident")), t_cst)
        dve(lambda e: e.tensor_copy(cnegb[:, 0, :], C("cneg")), t_cst)
        dve(lambda e: e.tensor_copy(cnegb[:, 1, :], C("cnegT")), t_cst)
        dve(lambda e: e.tensor_copy(trib[:, :], C("tri")), t_cst)
        dve(lambda e: e.tensor_copy(sel8b[:, :], C("sel8")[0:24, :]), t_cst)
        t_cb = dve(lambda e: e.tensor_copy(selbb[:, :], C("selb")[0:96, :]), t_cst)
        t_tg = act(lambda e: e.activation(tg[:, :], graw[:, :], ACT.Tanh), t_g)

        def clear(put, tile, ones):
            t = []
            for p in range(3):
                t1 = put(lambda e, p=p: e.memset(tile[0:96, p, :], 0.0))
                if ones:
                    t1 = put(lambda e, p=p: e.memset(tile[96:128, p, :], 1.0))
                t.append(t1)
            return t

        t_z = [clear(dve, Q8, False), clear(dve, K8, True)]
        t_ones = pool(lambda e: e.memset(VA[:, :, :], 1.0))
        t_ones = pool(lambda e: e.memset(VS[:, :, :], 1.0))
        t_z.append([None] * 3)

        t = dve(lambda e: e.tensor_copy(btmp[:, :], ints[:, 0, :]), t_i)
        t = dve(lambda e: e.tensor_scalar(btmp[:, :], btmp[:, :], C("iota_p"), -1.0, ALU.is_gt, ALU.add), t, t_cst)
        t = dve(lambda e: e.tensor_scalar(bias[:, 0, :], btmp[:, :], 1e12, col("L0_xattn_b"), ALU.mult, ALU.add), t, t_cols)
        t = dve(lambda e: e.tensor_copy(btmp[:, :], ints[:, 1, :]), t)
        t = dve(lambda e: e.tensor_scalar(btmp[:, :], btmp[:, :], -1.0, 1e30, ALU.add, ALU.mult), t)
        t_bias = dve(lambda e: e.tensor_scalar(bias[:, 1, :], btmp[:, :], col("L2_b"), None, ALU.add), t, t_cols)
        t = t_bias
        for i in range(2):
            b3 = biasc[:, i, :].rearrange("p (c b) -> p c b", c=3)
            t = dve(lambda e, i=i, b3=b3: e.tensor_copy(b3[:, 0, :], bias[:, i, :]), t)
            t = dve(lambda e, i=i, b3=b3: e.tensor_tensor(btmp[:, :], bias[:, i, :], b3[:, 0, :], ALU.subtract), t)
            t = dve(lambda e, i=i, b3=b3: e.tensor_copy(b3[:, 1, :], btmp[:, :]), t)
            t = dve(lambda e, i=i, b3=b3: e.tensor_tensor(b3[:, 2, :], btmp[:, :], b3[:, 1, :], ALU.subtract), t)
            tp = pe(lambda e, i=i: e.transpose(PSB[7].bitcast(BF16)[0:96, 128 * i:128 * i + 128], biasc[:, i, :], identb[:, :]),
                    t, t_idb, bank_free[7], inc=True)
            t = dve(lambda e, i=i: e.tensor_copy(biasT[:, i, :], PSB[7].bitcast(BF16)[0:96, 128 * i:128 * i + 128]), tp)
            bank_free[7] = t
        t_biasT = t

        st_free = [None] * 4
        turn = [0]

        def norm_in(src, n, waits, eps=EPS, rms=False):
            k = turn[0] % 4
            turn[0] += 1
            for j in range(n):
                t = dve(lambda e, j=j: e.bn_stats(st[:, k, j, :], src[:, j, :]), *waits, st_free[k])
            for j in range(n):
                t = dve(lambda e, j=j: e.bn_aggr(mv[:, k, j, :], st[:, k, j, :]), t)
            m, v = mv[:, k, 0:n, 0:1], mv[:, k, 0:n, 1:2]
            r0, r1 = rs[:, k, 0:n, 0:1], rs[:, k, 0:n, 1:2]
            if rms:
                t = pool(lambda e: e.tensor_tensor(r0, m, m, ALU.mult), t)
                t = pool(lambda e: e.tensor_tensor(r0, r0, v, ALU.add), t)
                t = pool(lambda e: e.tensor_scalar(r0, r0, eps, None, ALU.add), t)
            else:
                t = pool(lambda e: e.tensor_scalar(r0, v, eps, None, ALU.add), t)
            t = pool(lambda e: e.tensor_tensor(r1, r0, C("half")[:, 0:n].unsqueeze(2), ALU.pow), t, t_cst)
            return src, n, k, t, rms

        def norm_out(state, outs, waits=(), width=128, view=lambda a: a):
            src, n, k, t, rms = state
            for j in range(n):
                if rms:
                    t2 = dve(lambda e, j=j: e.tensor_scalar(outs(j), view(src[:, j, 0:width]), rs[:, k, j, 1:2], None, ALU.mult), t, *waits)
                else:
                    t2 = dve(lambda e, j=j: e.tensor_scalar(outs(j), view(src[:, j, :]), mv[:, k, j, 0:1], rs[:, k, j, 1:2],
                                                            ALU.subtract, ALU.mult), t, *waits)
            st_free[k] = t2
            return t2

        def norm(src, n, waits, outs, rms=False):
            return norm_out(norm_in(src, n, waits, rms=rms), outs)

        xn_free = [None, None]
        xT_free = [None, None]

        def turned(k, n, bank, t, scale=None, bcol=None, dst=None, dst_free=None):
            dst = xT[:, k, 0:128 * n] if dst is None else dst
            for j in range(n):
                tp = pe(lambda e, j=j: e.transpose(PSB[bank][:, 128 * j:128 * j + 128], xn[:, k, 128 * j:128 * j + 128],
                                                   C("ident")), t, bank_free[bank], t_cst, inc=(j == n - 1))
            xn_free[k] = tp
            s = 1.0 if scale is None else scale
            bz = 0.0 if bcol is None else bcol
            f = ACT.Identity if bcol is not None else ACT.Copy
            ta = act(lambda e: e.activation(dst, PSB[bank][:, 0:128 * n], f, bias=bz, scale=s), tp, xT_free[k], dst_free, t_cols)
            bank_free[bank] = ta
            return ta

        r32_free = [None, None]

        def split(src, dst, t, free, which):
            eng = (pool, dve)[which]
            r = r32[:, which, :]
            t = eng(lambda e: e.tensor_copy(dst[:, 0, :], src), t, free)
            t = eng(lambda e: e.tensor_tensor(r, src, dst[:, 0, :], ALU.subtract), t, r32_free[which])
            t_src = t
            t = eng(lambda e: e.tensor_copy(dst[:, 1, :], r), t)
            t = eng(lambda e: e.tensor_tensor(dst[:, 2, :], r, dst[:, 1, :], ALU.subtract), t)
            r32_free[which] = t
            return t_src, t

        comp_free = [None] * 4
        comp_turn = [0]

        def split_out(src, t, dests, p, which=0):
            k = comp_turn[0] % 4
            comp_turn[0] += 1
            dst = comp[:, k, :].rearrange("p (c t) -> p c t", c=3)
            t_src, t = split(src, dst, t, comp_free[k], which)
            tds = []
            for kind, lo, n, sc in dests:
                for c, (at_, m) in enumerate(((0, 3), (3, 2), (5, 1))):
                    if kind == "q":
                        a = dst[lo:lo + n, 0:m, :]
                    else:
                        a = dst[lo:lo + n, c:c + 1, :].broadcast_to([n, m, 256])
                    td = Q.dma(f"comp{k}", sc[p, at_:at_ + m].rearrange("c p t -> p c t"), a, (t,))
            comp_free[k] = td
            return t_src, td

        def load_rows(tile, name, sc, at_, dh, H, p, waits):
            dst = place(tile, at_, H)
            if dh == 16:
                for par in range(2):
                    src = sc[p].rearrange("c (d h e) t -> (c d) h e t", d=8, e=2)[:, :, par, :]
                    t = Q.dma(f"{name}{at_}", dst[48 * par:48 * par + 48, :].rearrange("r (h t) -> r h t", h=8), src, waits)
                return t
            return Q.dma(f"{name}{at_}", dst[0:6 * dh, :], sc[p].rearrange("c (d h) t -> (c d) (h t)", d=dh), waits)

        def place(tile, at_, H):
            w = 256 * H
            return tile[:, at_ * w // 4096, at_ * w % 4096:at_ * w % 4096 + w]

        def k_split(p):
            sp_free[p % 2], k_in[p] = split_out(sp32[:, p % 2, :], k_raw[p], (("k", 0, 128, sc_k),), p, 1)
            if p + 2 < NP:
                k_load(p + 2)

        x_tok = dict(enumerate(t_x))
        u_tok = {}

        q8_free = t_z[0]
        k8_free = t_z[1]
        ks_free = t_z[2]
        va_free = [t_ones] * 4
        vs_free = [t_ones] * 4
        vr_free = [None] * 3
        pt_free = [None] * 8
        mn_free = [None] * 4
        mcb_free = [None] * 4
        mres_free = [None]
        mT_free = [None] * 4
        rec_free = [None] * 2
        oe_free = [None] * 2
        side = []
        slot_no = [0]
        misc_turn = [0]

        def soon(fn, delay, first=False):
            side.insert(0 if first else len(side), (slot_no[0] + delay, fn))

        def run_side(n):
            for _ in range(n):
                for i, (at_, fn) in enumerate(side):
                    if at_ <= slot_no[0]:
                        side.pop(i)
                        fn()
                        break

        def misc():
            misc_turn[0] += 1
            return 6 + misc_turn[0] % 2

        def attention(H, dh, vd, ctx_kb, self_kb, prep, finish, bias_i=None, causal=False):
            R = 48 // H
            LAG = 2 if H == 16 else 4
            nkb = len(ctx_kb) + len(self_kb)
            tiles = [K8] * len(ctx_kb) + [KS] * len(self_kb)
            vts = [VA] * len(ctx_kb) + [VS] * len(self_kb)
            RQ = 96
            per_s = 4 // nkb
            n_s = H // per_s
            n_st = (H // 4) * nkb
            prepped = {}
            ready_m = {}
            chain = {}
            pv_wait = []
            nst = [0]
            for bk in (4, 5):
                bank_free[bk] = dve(lambda e, bk=bk: e.memset(PSB[bk], 0.0), bank_free[bk])

            def vh(vt, p, b2):
                return vt[:, p % 4, 0:2 * H * (vd + 1)].rearrange("p (b h d) -> p b h d", b=2, h=H)[:, b2]

            def head(tile, p, b2, h, rows_):
                return place(tile, p % R, H)[0:rows_, 256 * h + 128 * b2:256 * h + 128 * b2 + 128]

            def s_unit(b, i):
                p, b2 = divmod(b, 2)
                bank = i % 2
                w = [bank_free[bank], *prepped[p]["qk"]]
                extra = bias_i is not None or causal
                for hh in range(per_s):
                    h = i * per_s + hh
                    for kb in range(nkb):
                        o = PSB[bank][:, 128 * (hh * nkb + kb):128 * (hh * nkb + kb) + 128]
                        last = hh == per_s - 1 and kb == nkb - 1
                        t = pe(lambda e, o=o, h=h, kb=kb, st_=(hh == 0 and kb == 0), sp_=not extra: e.matmul(
                            o, head(Q8, p, b2, h, RQ), head(tiles[kb], p, b2, h, RQ), start=st_, stop=sp_,
                            skip_group_check=True), *w, inc=last and not extra)
                        w = []
                if bias_i is not None:
                    t = pe(lambda e: e.matmul(PSB[bank].rearrange("p (h k) -> p h k", h=4), selbb[:, b:b + 1].broadcast_to([96, 128]),
                                              biasT[:, bias_i, :].unsqueeze(1).broadcast_to([96, 4, 128]), start=False, stop=True,
                                              skip_group_check=True), t_biasT, t_cb, inc=True)
                if causal:
                    t = pe(lambda e: e.matmul(PSB[bank].rearrange("p (h k) -> p h k", h=4), identb[:, :],
                                              cnegb[:, 0, :].unsqueeze(1).broadcast_to([128, 4, 128]), start=False, stop=True,
                                              skip_group_check=True), t_cb, inc=True)
                tr = dve(lambda e: e.tensor_reduce(mneg[:, b % 4, i * per_s:(i + 1) * per_s],
                                                   PSB[bank].rearrange("p (h k) -> p h k", h=per_s), AX.X, ALU.max, negate=True),
                         t, mn_free[b % 4])
                bank_free[bank] = tr
                if i == n_s - 1:
                    k = b % 4
                    c3 = mcb[:, k, 0:3 * H].rearrange("p (c h) -> p c h", c=3)
                    mn = mneg[:, b % 4, 0:H]
                    t1 = dve(lambda e: e.tensor_copy(c3[:, 0, :], mn), tr, mcb_free[k])
                    t1 = dve(lambda e: e.tensor_tensor(mres[:, 0:H], mn, c3[:, 0, :], ALU.subtract), t1, mres_free[0])
                    mn_free[b % 4] = t1
                    t1 = dve(lambda e: e.tensor_copy(c3[:, 1, :], mres[:, 0:H]), t1)
                    t1 = dve(lambda e: e.tensor_tensor(c3[:, 2, :], mres[:, 0:H], c3[:, 1, :], ALU.subtract), t1)
                    mres_free[0] = t1
                    chain[b] = t1
                    soon(lambda: m_turn(b), {2: 3, 4: 3, 8: 6}[n_st], True)

            def m_turn(b):
                p, b2 = divmod(b, 2)
                k = b % 4
                mb = misc()
                o = PSB[mb].bitcast(BF16)[0:3 * H, 0:128]
                t = pe(lambda e: e.transpose(o, mcb[:, k, 0:3 * H], identb[:, :]), chain[b], t_idb, bank_free[mb], inc=True)
                mcb_free[k] = t
                t = act(lambda e: e.activation(mT[0:3 * H, k, :], o, ACT.Copy), t, mT_free[k])
                bank_free[mb] = t
                dst = place(Q8, p % R, H)[96:99, :].rearrange("c (h t) -> c h t", h=H)[:, :, 128 * b2:128 * b2 + 128]
                for c in range(3):
                    t2 = Q.dma(f"m{k}", dst[c:c + 1], mT[c * H:c * H + H, k, :], (t, *prepped[p]["qk"]))
                mT_free[k] = t2
                ready_m[b] = t2

            def st_unit(b, i):
                p, b2 = divmod(b, 2)
                G, kb = divmod(i, nkb)
                n = nst[0]
                nst[0] += 1
                bk = 2 + n % 2
                w = [bank_free[bk], ready_m[b]]
                for hh in range(4):
                    h = 4 * G + hh
                    o = PSB[bk][:, 128 * hh:128 * hh + 128]
                    t = pe(lambda e, o=o, h=h, hh=hh: e.matmul(o, head(tiles[kb], p, b2, h, 99), head(Q8, p, b2, h, 99),
                                                              start=(hh == 0), stop=not causal, skip_group_check=True),
                           *w, inc=(hh == 3 and not causal))
                    w = []
                if causal:
                    t = pe(lambda e: e.matmul(PSB[bk].rearrange("p (h k) -> p h k", h=4), identb[:, :],
                                              cnegb[:, 1, :].unsqueeze(1).broadcast_to([128, 4, 128]), start=False, stop=True,
                                              skip_group_check=True), t_cb, inc=True)
                bz = 0.0 if bias_i is None else bias[:, bias_i, b:b + 1]
                slot = n % 8
                te = act(lambda e: e.activation(HB[:, slot, :], PSB[bk], ACT.Exp, bias=bz), t, pt_free[slot], t_bias)
                bank_free[bk] = te
                if b2 == 1 and i == n_st - 1:
                    q8_free[p % R] = t
                    if ctx_kb:
                        k8_free[p % R] = t
                    if self_kb:
                        ks_free[p % R] = t
                return (b, G, kb, slot, te)

            got = {}

            def pv_unit(u):
                b, G, kb, slot, te = u
                got.setdefault((b, G), []).append((kb, slot, te))
                if kb != nkb - 1:
                    return
                p, b2 = divmod(b, 2)
                k = b % 2
                bk = 4 + k
                blocks = got.pop((b, G))
                w = [x[2] for x in blocks] + [*prepped[p]["v"]]
                if G == 0:
                    w.append(bank_free[bk])
                for kb_, slot_, _ in blocks:
                    for hh in range(4):
                        h = 4 * G + hh
                        o = PSB[bk][32 * hh:32 * hh + vd + 1, 128 * G:128 * G + 128]
                        t = pe(lambda e, o=o, h=h, hh=hh, kb_=kb_, slot_=slot_: e.matmul(
                            o, vh(vts[kb_], p, b2)[:, h, :], HB[:, slot_, 128 * hh:128 * hh + 128],
                            start=(kb_ == 0), stop=(kb_ == nkb - 1), skip_group_check=True), *w, inc=(hh == 3))
                        w = []
                    pt_free[slot_] = t
                if G == H // 4 - 1:
                    if b2 == 1:
                        pv_done.add(p)
                        if ctx_kb:
                            va_free[p % 4] = t
                        if self_kb:
                            vs_free[p % 4] = t
                    te = act(lambda e: e.activation(OE[:, k, 0:32 * H], PSB[bk][:, 0:32 * H], ACT.Copy), t, oe_free[k])
                    bank_free[bk] = te
                    soon(lambda: pv_turn(b, te), 4 if H == 16 else 3, True)

            def pv_turn(b, te):
                k = b % 2
                mb = misc()
                for G in range(H // 4):
                    t = pe(lambda e, G=G: e.transpose(PSB[mb][:, 128 * G:128 * G + 128], OE[:, k, 128 * G:128 * G + 128], C("ident")),
                           te, bank_free[mb], inc=(G == H // 4 - 1))
                oe_free[k] = t
                o3 = PSB[mb][:, 0:32 * H].rearrange("p (h d) -> p h d", h=H)
                t = dve(lambda e: e.reciprocal(rec[:, k, 0:H], o3[:, :, vd]), t, rec_free[k])
                t = dve(lambda e: e.tensor_tensor(otmp[:, k, 0:H * vd].rearrange("p (h d) -> p h d", h=H), o3[:, :, 0:vd],
                                                  rec[:, k, 0:H].unsqueeze(2).broadcast_to([128, H, vd]), ALU.mult), t)
                bank_free[mb] = t
                finish(b, k, t)

            coming = {}
            pv_done = set()
            at_ = lambda p: p % R

            def stage(p):
                if len(coming.get(p, ())) > 1:
                    if coming[p][0].__name__ == "vv" and p >= 4 and p - 4 not in pv_done:
                        soon(lambda: stage(p), 1)
                    else:
                        coming[p].pop(0)()

            def copy(p):
                if p >= 4 and p - 4 not in pv_done:
                    soon(lambda: copy(p), 1)
                else:
                    prepped[p]["v"].append(prepped[p].pop("copy")())

            def loaded(p):
                for f in coming[p][:-1]:
                    f()
                prepped[p] = coming.pop(p)[-1]()
                if "copy" in prepped[p]:
                    soon(lambda: copy(p), n_s + n_st)

            load_step = {p: max(2 * (p - R) + 1 + LAG, 2 * p - 4) for p in range(NP)}
            ahead = [p for p in range(NP) if load_step[p] < 0]
            both = [prep(p, at_) for p in ahead]
            n = len(both[0]) - 1
            for i in range(n + 2 * len(both) - 2):
                for j, fs in enumerate(both):
                    if 0 <= i - 2 * j < n:
                        fs[i - 2 * j]()
            for p, fs in zip(ahead, both):
                coming[p] = fs[-1:]
                loaded(p)
            for tstep in range(B + LAG):
                tasks = []
                if tstep < B:
                    tasks.append([lambda i=i: s_unit(tstep, i) for i in range(n_s)])
                if tstep >= LAG:
                    tasks.append([lambda i=i: ("st", st_unit(tstep - LAG, i)) for i in range(n_st)])
                order = sorted(((i + 0.5) / len(g), gi, f) for gi, g in enumerate(tasks) for i, f in enumerate(g))
                for pp in range(NP):
                    if pp not in ahead and max(0, load_step[pp] - (2 if H == 16 else 4)) == tstep:
                        coming[pp] = prep(pp, at_)
                        gap = max(2, (n_s + n_st) // 5)
                        for i in range(len(coming[pp]) - 1):
                            soon(lambda pp=pp: stage(pp), 1 + i * gap)
                for _, _, f in order:
                    r = f()
                    if r is not None:
                        pv_wait.append(r[1])
                        if len(pv_wait) > PVLAG:
                            pv_unit(pv_wait.pop(0))
                    slot_no[0] += 1
                    run_side(2)
                for pp in range(NP):
                    if load_step[pp] == tstep:
                        loaded(pp)
            while pv_wait:
                slot_no[0] += 4
                run_side(4)
                pv_unit(pv_wait.pop(0))
            while side:
                slot_no[0] += 8
                run_side(1)

        def load_v(p):
            k = p % 3
            return Q.dma(f"vr{k}", vraw[:, k, :].rearrange("p (b d) -> p b d", b=2),
                         io["ctx_2048"][2 * p:2 * p + 2, :, 128:256].rearrange("b t d -> t b d"), (vr_free[k],))

        def copy_v(p, H, dh, tv):
            k = p % 3
            dst = VA[:, p % 4, 0:2 * H * (dh + 1)].rearrange("p (n d) -> p n d", d=dh + 1)
            t = dve(lambda e: e.tensor_copy(dst[:, :, 0:dh], vraw[:, k, :].rearrange("p (n d) -> p n d", d=dh)), tv, va_free[p % 4])
            vr_free[k] = t
            return t

        def heads_out(a):
            return a.rearrange("p (h d) -> p h d", h=16)

        def heads_in(a):
            return a.rearrange("p (d h) -> p h d", h=16)

        def prep_ctx(sc, dh, first):
            H = 128 // dh

            def prep(p, at_):
                k = p % 2
                got = {}

                def n1():
                    got["s"] = norm_in(X[:, 2 * p:2 * p + 2, :], 2, (x_tok[2 * p], x_tok[2 * p + 1]))

                def n2():
                    got["n"] = norm_out(got["s"], lambda j: heads_in(xn[:, k, 128 * j:128 * j + 128]), (xn_free[k],), view=heads_out)

                def qT():
                    got["T"] = turned(k, 2, misc(), got["n"], scale=float(np.float32(dh ** -0.5)))

                def parts():
                    xT_free[k], got["q"] = split_out(xT[:, k, 0:256], got["T"], (("q", 0, 128, sc),), p)

                def loads():
                    tk = load_rows(K8, "k8", sc_k, at_(p), dh, H, p, (k_in[p], k8_free[at_(p)]))
                    tq = load_rows(Q8, "q8", sc, at_(p), dh, H, p, (got["q"], q8_free[at_(p)]))
                    tv = load_v(p)
                    return {"qk": [tq, tk], "v": [], "copy": lambda: copy_v(p, H, dh, tv)}
                return [n1, n2, *([lambda: k_split(p)] if first else []), qT, parts, loads]
            return prep

        def finish_add(gi):
            def finish(b, k, t):
                t = dve(lambda e: e.scalar_tensor_tensor(out=X[:, b, :], in0=otmp[:, k, :], scalar=tg[:, gi:gi + 1], in1=X[:, b, :],
                                                         op0=ALU.mult, op1=ALU.add), t, t_tg, x_tok[b])
                x_tok[b] = t
                rec_free[k] = t
            return finish

        ring = [0, 8]

        def bank():
            ring[0] += 1
            return ring[0] % ring[1]

        def group_T(g, src, waits, rms=False, scale=None, bcol=None, dst=None, dst_free=None):
            k = g % 2
            t = norm(src, 4, (*waits, xn_free[k]), lambda j: xn[:, k, 128 * j:128 * j + 128], rms=rms)
            return turned(k, 4, bank(), t, scale=scale, bcol=bcol, dst=dst, dst_free=dst_free)

        def xg(g):
            return [x_tok[4 * g + j] for j in range(4)]

        soon(load_weights, 12)
        attention(16, 8, 8, [0], [], prep_ctx(sc_q[0], 8, True), finish_add(0), bias_i=0)

        def y_turn(src, t, free, g):
            bt = bank()
            for j in range(4):
                t = pe(lambda e, j=j: e.transpose(PSB[bt][:, 128 * j:128 * j + 128], src[:, 128 * j:128 * j + 128], C("ident")), t,
                       bank_free[bt], inc=(j == 3))
            free[g % 2] = t
            return bt, PSB[bt].rearrange("p (b d) -> p b d", b=4), t

        def ffn0():
            t_s3 = dve(lambda e: e.tensor_scalar(col("w3_s"), col("w3_s"), tg[:, 4:5], None, ALU.mult), t_cols, t_tg)
            KF = KS[:, :, :].rearrange("p a b -> p (a b)").bitcast(F32).rearrange("p (n t) -> p n t", t=512)
            space = [(HB[:, 0:4, :], HB[:, 4:8, :]), (KF[:, 0:4, :], KF[:, 4:8, :])]
            start_w = [tuple(pt_free), tuple(t_z[2])]
            at_free = [None, None]
            hA_free, hB_free = [None, None], [None, None]
            xt, nt, hid, yt = {}, {}, {}, {}

            def n_(g):
                k = g % 2
                nt[g] = norm(X[:, 4 * g:4 * g + 4, :], 4, (*xg(g), xn_free[k]), lambda j: xn[:, k, 128 * j:128 * j + 128])

            def t_(g):
                xt[g] = turned(g % 2, 4, bank(), nt[g])

            def up(g):
                k = g % 2
                hA = space[k][0]
                hid[g] = []
                for m in range(4):
                    ba, bb = bank(), bank()
                    ta = pe(lambda e, m=m, ba=ba: e.matmul(PSB[ba], wb["w1T"][:, 128 * m:128 * m + 128], xT[:, k, :], start=True, stop=True),
                            xt[g], bank_free[ba], *t_wb, inc=True)
                    tb = pe(lambda e, m=m, bb=bb: e.matmul(PSB[bb], wb["w2T"][:, 128 * m:128 * m + 128], xT[:, k, :], start=True, stop=True),
                            bank_free[bb], inc=True)
                    a = m % 2
                    t = act(lambda e, m=m, ba=ba, a=a: e.activation(AT[:, a, :], PSB[ba], ACT.Silu, scale=col("w1_s", m)), ta, at_free[a], t_cols)
                    bank_free[ba] = t
                    t = dve(lambda e, m=m, bb=bb, a=a: e.scalar_tensor_tensor(out=hA[:, m, :], in0=PSB[bb], scalar=col("w2_s", m), in1=AT[:, a, :],
                                                                             op0=ALU.mult, op1=ALU.mult), t, tb, hA_free[k], *start_w[k])
                    bank_free[bb] = at_free[a] = t
                    hid[g].append(t)
                xT_free[k] = tb

            def mix(g, back):
                k = g % 2
                src, dst = space[k][back], space[k][1 - back]
                wname, sname = ("h1T", "h1_s") if not back else ("h2T", "h2_s")
                done, hid[g] = hid[g], []
                free = (hB_free, hA_free)[back]
                for m in range(4):
                    ba = bank()
                    for c in range(4):
                        t = pe(lambda e, m=m, c=c, ba=ba: e.matmul(
                            PSB[ba], wb[wname][:, 512 * c + 128 * m:512 * c + 128 * m + 128], src[:, c, :], start=(c == 0), stop=(c == 3)),
                            done[c], bank_free[ba], inc=(c == 3))
                    t = act(lambda e, m=m, ba=ba: e.activation(dst[:, m, :], PSB[ba], ACT.Gelu, scale=col(sname, m)),
                            t, free[k], *start_w[k])
                    bank_free[ba] = t
                    hid[g].append(t)
                tp = (Q.sem["pe"], Q.count["pe"])
                (hA_free, hB_free)[back][k] = tp

            def down(g):
                k = g % 2
                hA = space[k][0]
                by = bank()
                for c in range(4):
                    t = pe(lambda e, c=c: e.matmul(PSB[by], wb["w3T"][:, 128 * c:128 * c + 128], hA[:, c, :], start=(c == 0), stop=(c == 3)),
                           hid[g][c], bank_free[by], inc=(c == 3))
                hA_free[k] = t
                t = act(lambda e: e.activation(OE[:, k, :], PSB[by], ACT.Copy, scale=col("w3_s")), t, oe_free[k], t_s3)
                bank_free[by] = t
                yt[g] = t

            def add(g):
                bt, P4, t = y_turn(OE[:, g % 2, :], yt[g], oe_free, g)
                t = dve(lambda e: e.tensor_tensor(X[:, 4 * g:4 * g + 4, :], X[:, 4 * g:4 * g + 4, :], P4, ALU.add), t, *xg(g))
                bank_free[bt] = t
                for j in range(4):
                    x_tok[4 * g + j] = t

            n_(0)
            n_(1)
            t_(0)
            t_(1)
            up(0)
            mix(0, 0)
            for g in range(NG):
                if g + 2 < NG:
                    n_(g + 2)
                if g + 1 < NG:
                    up(g + 1)
                if g:
                    add(g - 1)
                mix(g, 1)
                if g + 2 < NG:
                    t_(g + 2)
                if g + 1 < NG:
                    mix(g + 1, 0)
                down(g)
            add(NG - 1)
            t = (Q.sem["pe"], Q.count["pe"])
            for i in range(8):
                pt_free[i] = t
            ks_free[:] = clear(lambda fn: dve(fn, t), KS, True)

        if stop >= 2:
            ffn0()
        pe_after_ffn0 = (Q.sem["pe"], Q.count["pe"])

        def v_out(bank, p, H, dh, t):
            dst = VS[:, p % 4, 0:2 * H * (dh + 1)].rearrange("p (n d) -> p n d", d=dh + 1)
            t = act(lambda e: e.activation(dst[:, :, 0:dh], PSB[bank][:, 0:2 * H * dh].rearrange("p (n d) -> p n d", d=dh), ACT.Copy),
                    t, vs_free[p % 4])
            bank_free[bank] = t
            return t

        oT_free = [None] * 2

        def prep_x1(p, at_):
            k = p % 2
            got = {}

            def n1():
                got["s"] = norm_in(X[:, 2 * p:2 * p + 2, :], 2, (x_tok[2 * p], x_tok[2 * p + 1]))

            def n2():
                got["n"] = norm_out(got["s"], lambda j: xn[:, k, 128 * j:128 * j + 128], (xn_free[k],))

            def n3():
                got["T"] = turned(k, 2, misc(), got["n"])

            def qk():
                mb = misc()
                w = wsm["w_qkvT"]
                pe(lambda e: e.matmul(PSB[mb][:, 0:256], w[:, 0:128], xT[:, k, 0:256], start=True, stop=True), got["T"], t_ws, bank_free[mb])
                t = pe(lambda e: e.matmul(PSB[mb][:, 256:512], w[:, 128:256], xT[:, k, 0:256], start=True, stop=True), inc=True)
                got["ta"] = act(lambda e: e.activation(sp32[:, 0, :], PSB[mb][:, 0:256], ACT.Copy, scale=float(np.float32(8 ** -0.5))), t, sp_free[0])
                got["tb"] = act(lambda e: e.activation(sp32[:, 1, :], PSB[mb][:, 256:512], ACT.Copy), t, sp_free[1])
                bank_free[mb] = got["tb"]

            def parts():
                sp_free[0], got["q"] = split_out(sp32[:, 0, :], got["ta"], (("q", 0, 128, sc_q[1]),), p)
                sp_free[1], got["k"] = split_out(sp32[:, 1, :], got["tb"], (("k", 0, 128, sc_s),), p, 1)

            def vv():
                mb = misc()
                for j in range(2):
                    t = pe(lambda e, j=j: e.matmul(PSB[mb][:, 128 * j:128 * j + 128], xT[:, k, 128 * j:128 * j + 128],
                                                   wsm["w_qkvT"][:, 256:384], start=True, stop=True), got["T"], bank_free[mb], inc=(j == 1))
                xT_free[k] = t
                got["v"] = v_out(mb, p, 16, 8, t)

            def loads():
                tk = load_rows(K8, "k8", sc_k, at_(p), 8, 16, p, (k_in[p], k8_free[at_(p)]))
                tq = load_rows(Q8, "q8", sc_q[1], at_(p), 8, 16, p, (got["q"], q8_free[at_(p)]))
                t2 = load_rows(KS, "ks", sc_s, at_(p), 8, 16, p, (got["k"], ks_free[at_(p)]))
                tv = load_v(p)
                return {"qk": [tq, tk, t2], "v": [got["v"]], "copy": lambda: copy_v(p, 16, 8, tv)}
            return [n1, n2, n3, qk, parts, vv, loads]

        def finish_mm(n, wname, end):
            def finish(b, k, t):
                def turn():
                    mb = misc()
                    tp = pe(lambda e: e.transpose(PSB[mb][0:n, 0:128], otmp[:, k, 0:n], C("ident")), t, bank_free[mb], inc=True)
                    rec_free[k] = tp
                    ta = act(lambda e: e.activation(oT[0:n, k, :], PSB[mb][0:n, 0:128], ACT.Copy), tp, oT_free[k])
                    bank_free[mb] = ta

                    def mul():
                        mb = misc()
                        tm = pe(lambda e: e.matmul(PSB[mb][:, 0:128], oT[0:n, k, :], wsm[wname], start=True, stop=True), ta, t_ws,
                                bank_free[mb], inc=True)
                        oT_free[k] = tm
                        end(b, k, tm, mb)
                    soon(mul, 3, True)
                soon(turn, 4, True)
            return finish

        ptmp_free = [None] * 2

        def end_x1(b, k, t, mb):
            t = dve(lambda e: e.tensor_tensor(AT[:, 0, 128 * k:128 * k + 128], PSB[mb][:, 0:128], rows[:, 1, :], ALU.add), t, t_row1,
                    ptmp_free[k])
            bank_free[mb] = t
            t = dve(lambda e: e.scalar_tensor_tensor(out=X[:, b, :], in0=AT[:, 0, 128 * k:128 * k + 128], scalar=tg[:, 1:2], in1=X[:, b, :],
                                                     op0=ALU.mult, op1=ALU.add), t, x_tok[b], t_tg)
            x_tok[b] = ptmp_free[k] = t

        if stop >= 3:
            attention(16, 8, 8, [0], [0], prep_x1, finish_mm(128, "w_projT", end_x1))

        t_m = None

        def load_moe1(t):
            for name, at in (("m1", 0), ("m3", 2048), ("m2", 4096)):
                tt = Q.dma("wb2", WB[:, at:at + 2048], io[name], (t,))
            return tt

        def prep_f1(p, at_):
            k = p % 2
            got = {}
            if p < 3:
                ks_free[p % 3] = pool(lambda e: e.memset(KS[0:64, p % 3, :], 0.0), ks_free[p % 3])

            def n1():
                got["s"] = norm_in(X[:, 2 * p:2 * p + 2, :], 2, (x_tok[2 * p], x_tok[2 * p + 1]))

            def n2():
                t = norm_out(got["s"], lambda j: U[:, 2 * p + j, :])
                u_tok[2 * p] = u_tok[2 * p + 1] = t
                got["s"] = norm_in(U[:, 2 * p:2 * p + 2, :], 2, (t,), rms=True)

            def n3():
                got["n"] = norm_out(got["s"], lambda j: xn[:, k, 128 * j:128 * j + 128], (xn_free[k],))

            def n4():
                got["T"] = turned(k, 2, misc(), got["n"], scale=col("g1"))

            def cc():
                mb = misc()
                t = pe(lambda e: e.matmul(PSB[mb][0:64, 0:256], wsm["w_down"], xT[:, k, 0:256], start=True, stop=True), got["T"], t_ws,
                       bank_free[mb], inc=True)
                xT_free[k] = t
                got["c"] = bank_free[mb] = act(lambda e: e.activation(sp32[0:64, k, :], PSB[mb][0:64, 0:256], ACT.Copy), t, sp_free[k])

            def qk():
                mb = misc()
                c = sp32[0:64, k, :]
                pe(lambda e: e.matmul(PSB[mb][:, 0:256], wsm["wqk"], c, start=True, stop=True), got["c"], bank_free[mb])
                t = pe(lambda e: e.matmul(PSB[mb][:, 256:512], wsm["wqk_sw"], c, start=True, stop=True), inc=True)
                P = PSB[mb].rearrange("p (a b t) -> p a b t", a=2, b=2)
                o = [AT[:, 0, 256 * i:256 * i + 256] for i in range(2)]
                o3 = [x.rearrange("p (b t) -> p b t", b=2) for x in o]
                t1 = dve(lambda e: e.tensor_tensor(o3[0], P[:, 0], C("cos").unsqueeze(1).broadcast_to([128, 2, 128]), ALU.mult), t, ptmp_free[0])
                t1 = dve(lambda e: e.tensor_tensor(o3[1], P[:, 1], C("sin").unsqueeze(1).broadcast_to([128, 2, 128]), ALU.mult), t)
                bank_free[mb] = t1
                t1 = dve(lambda e: e.tensor_tensor(o[0], o[0], o[1], ALU.add), t1)
                got["r"] = t1

            def parts():
                ptmp_free[0], got["q"] = split_out(AT[:, 0, 0:256], got["r"], (("q", 0, 64, sc_f[0]), ("k", 64, 64, sc_f[1])), p)

            def vv():
                mb = misc()
                for j in range(2):
                    t = pe(lambda e, j=j: e.matmul(PSB[mb][:, 64 * j:64 * j + 64], sp32[0:64, k, 128 * j:128 * j + 128], wsm["wv"],
                                                   start=True, stop=True), bank_free[mb], inc=(j == 1))
                sp_free[k] = t
                got["v"] = v_out(mb, p, 16, 4, t)

            def loads():
                tq = load_rows(Q8, "q8", sc_f[0], at_(p), 4, 16, p, (got["q"], q8_free[at_(p)]))
                tk = load_rows(KS, "ks", sc_f[1], at_(p), 4, 16, p, (got["q"], ks_free[at_(p)]))
                return {"qk": [tq, tk], "v": [got["v"]]}
            return [n1, n2, n3, n4, cc, qk, parts, vv, loads]

        def end_f1(b, k, t, mb):
            t = dve(lambda e: e.tensor_tensor(U[:, b, :], PSB[mb][:, 0:128], U[:, b, :], ALU.add), t, u_tok[b])
            bank_free[mb] = u_tok[b] = t

        def set_ones(d, vt, fr):
            for q in range(4):
                fr[q] = pool(lambda e, q=q: e.memset(vt[:, q, :], 1.0), fr[q])

        small = sb("small", [128, 3, 32])
        gate_tok, tt_tok = {}, {}

        def chain(fns, gap):
            def go(i):
                fn, n = fns[i] if isinstance(fns[i], tuple) else (fns[i], gap)
                fn()
                if i + 1 < len(fns):
                    soon(lambda: go(i + 1), n)
            soon(lambda: go(0), 1)

        def front(g, dst, xf, rms, wname, scale, bcol, plus, w, layer_norm):
            got = {}
            bs = slice(4 * g, 4 * g + 4)
            u_in = lambda: [u_tok[4 * g + j] for j in range(4)]
            big = [AT[:, 1, 256 * i:256 * i + 256].rearrange("p (b i j) -> p b i j", b=4, i=8) for i in range(2)]
            L, T, s0, s1 = LG[:, bs, :], GT[:, bs, :], small[:, 0, bs], small[:, 1, bs]
            bc = lambda x: x.unsqueeze(2).broadcast_to([128, 4, 8])

            def n0():
                got["s"] = norm_in(X[:, bs, :], 4, xg(g))

            def n1():
                if layer_norm:
                    t = norm_out(got["s"], lambda j: U[:, 4 * g + j, :])
                    for j in range(4):
                        u_tok[4 * g + j] = t
                got["s"] = norm_in(U[:, bs, :], 4, u_in(), rms=rms)

            def n2():
                got["n"] = norm_out(got["s"], lambda j: xf[:, 128 * j:128 * j + 128], (fr["xf"], *w))

            def n3():
                mb = misc()
                for j in range(4):
                    t = pe(lambda e, j=j: e.transpose(PSB[mb][:, 128 * j:128 * j + 128], xf[:, 128 * j:128 * j + 128], C("ident")), got["n"],
                           bank_free[mb], inc=(j == 3))
                fr["xf"] = t
                f, bz = (ACT.Copy, 0.0) if bcol is None else (ACT.Identity, bcol)
                tt_tok[g] = bank_free[mb] = act(lambda e: e.activation(dst[:, 512 * g:512 * g + 512], PSB[mb], f, bias=bz, scale=scale), t, *w)

            def n4():
                mb = misc()
                for j in range(4):
                    t = pe(lambda e, j=j: e.matmul(PSB[mb][:, 8 * j:8 * j + 8], dst[:, 512 * g + 128 * j:512 * g + 128 * j + 128], wsm[wname],
                                                   start=True, stop=True), tt_tok[g], t_ws, bank_free[mb], inc=(j == 3))
                P = PSB[mb][:, 0:32].rearrange("p (b e) -> p b e", b=4)
                if plus is None:
                    t = dve(lambda e: e.tensor_copy(L, P), t, fr["gate"])
                else:
                    t = dve(lambda e: e.tensor_tensor(L, P, rows2[:, :].unsqueeze(1).broadcast_to([128, 4, 8]), ALU.add), t, t_rows2, fr["gate"])
                bank_free[mb] = t
                t = dve(lambda e: e.tensor_reduce(s0, L, AX.X, ALU.max), t)
                got["t"] = dve(lambda e: e.tensor_tensor(L, L, bc(s0), ALU.subtract), t)

            def n5():
                got["t"] = act(lambda e: e.activation(L, L, ACT.Exp), got["t"])

            def n6():
                t = dve(lambda e: e.tensor_reduce(s0, L, AX.X, ALU.add), got["t"])
                t = dve(lambda e: e.reciprocal(s1, s0), t)
                t = dve(lambda e: e.tensor_tensor(L, L, bc(s1), ALU.mult), t)
                pj = L.unsqueeze(2).broadcast_to([128, 4, 8, 8])
                pi = L.unsqueeze(3).broadcast_to([128, 4, 8, 8])
                low = C("low").rearrange("p (i j) -> p i j", i=8).unsqueeze(1).broadcast_to([128, 4, 8, 8])
                t = dve(lambda e: e.tensor_tensor(big[0], pj, pi, ALU.is_gt), t, *w)
                t = dve(lambda e: e.tensor_tensor(big[1], pj, pi, ALU.is_equal), t)
                t = dve(lambda e: e.tensor_tensor(big[1], big[1], low, ALU.mult), t)
                got["t"] = dve(lambda e: e.tensor_tensor(big[0], big[0], big[1], ALU.add), t)

            def n7():
                t = dve(lambda e: e.tensor_reduce(T, big[0], AX.X, ALU.add), got["t"])
                t = dve(lambda e: e.scalar_tensor_tensor(out=T, in0=T, scalar=1.5, in1=L, op0=ALU.is_lt, op1=ALU.mult), t)
                t = dve(lambda e: e.tensor_reduce(s0, T, AX.X, ALU.add), t)
                if plus:
                    t = dve(lambda e: e.tensor_scalar(s0, s0, plus, None, ALU.add), t)
                t = dve(lambda e: e.reciprocal(s1, s0), t)
                t = dve(lambda e: e.tensor_tensor(T, T, bc(s1), ALU.mult), t)
                t = dve(lambda e: e.tensor_copy(G3[:, bs, 0, :], T), t)
                r = gr[:, 4 * (g % 2):4 * (g % 2) + 4, :]
                t = dve(lambda e: e.tensor_tensor(r, T, G3[:, bs, 0, :], ALU.subtract), t)
                t = dve(lambda e: e.tensor_copy(G3[:, bs, 1, :], r), t)
                gate_tok[g] = dve(lambda e: e.tensor_tensor(G3[:, bs, 2, :], r, G3[:, bs, 1, :], ALU.subtract), t)

            return [*([n0] if layer_norm else []), n1, n2, n3, n4, n5, n6, n7]

        fr = {"xf": None, "gate": None}
        G3 = sb("G3", [128, 32, 3, 8], BF16)
        gS = comp[0:24, 0:2, 0:512]
        gr = sb("gr", [128, 8, 8])
        gs_tok = {}
        gS_free = [None, None]
        yt_free = [None, None]
        tmp_free = [None, None]
        tmp_turn = [0]

        def gate_rows(g):
            k = g % 2
            bt = bank()
            for j in range(4):
                t = pe(lambda e, j=j: e.transpose(PSB[bt].bitcast(BF16)[0:24, 128 * j:128 * j + 128],
                                                  G3[:, 4 * g + j].rearrange("p c e -> p (c e)"), identb[:, :]), gate_tok[g], bank_free[bt], inc=(j == 3))
            gs_tok[g] = bank_free[bt] = act(lambda e: e.activation(gS[:, k, :], PSB[bt].bitcast(BF16)[0:24, 0:512], ACT.Copy), t, gS_free[k])

        def moe_back(g, ex, hid, w2, t_hid, hid_free, y_tok):
            k = g % 2
            by, bg = bank(), bank()
            n = len(hid)
            for c in range(n):
                t = pe(lambda e, c=c: e.matmul(PSB[by], w2(ex, c), hid[c], start=(c == 0), stop=(c == n - 1)), t_hid[c], bank_free[by],
                       inc=(c == n - 1))
            hid_free(t)
            tg_ = pe(lambda e: e.matmul(PSB[bg], sel8b[:, ex:ex + 1].broadcast_to([24, 128]), gS[:, k, :], start=True, stop=True),
                     gs_tok[g], bank_free[bg], t_cb, inc=True)
            if ex == 7:
                gS_free[k] = tg_
            i = tmp_turn[0] % 2
            tmp_turn[0] += 1
            ta = act(lambda e: e.activation(OE[:, i, :], PSB[bg], ACT.Copy), tg_, tmp_free[i])
            bank_free[bg] = ta
            YT = xT[:, k, :]
            if y_tok is None:
                t = dve(lambda e: e.tensor_tensor(YT, PSB[by], OE[:, i, :], ALU.mult), t, ta, yt_free[k])
                bank_free[by] = tmp_free[i] = t
                return t
            t = dve(lambda e: e.tensor_tensor(OE[:, i, :], PSB[by], OE[:, i, :], ALU.mult), t, ta)
            bank_free[by] = t
            t = pool(lambda e: e.tensor_tensor(YT, YT, OE[:, i, :], ALU.add), t, y_tok)
            tmp_free[i] = t
            return t

        def moe_end(g, gi, t):
            b = 4 * g
            bt, P4, t = y_turn(xT[:, g % 2, :], t, yt_free, g)
            t = dve(lambda e: e.tensor_tensor(U[:, b:b + 4, :], P4, U[:, b:b + 4, :], ALU.add), t, *[u_tok[b + j] for j in range(4)])
            bank_free[bt] = t
            t = dve(lambda e: e.scalar_tensor_tensor(out=X[:, b:b + 4, :], in0=U[:, b:b + 4, :], scalar=tg[:, gi:gi + 1], in1=X[:, b:b + 4, :],
                                                     op0=ALU.mult, op1=ALU.add), t, t_tg, *xg(g))
            for j in range(4):
                x_tok[b + j] = u_tok[b + j] = t

        def tick():
            slot_no[0] += 1
            run_side(1)

        def moe(gi, up, w2, init, w, each=lambda n: None, done=lambda g: None):
            for i in range(2):
                yt_free[i] = tmp_free[i] = w
                gS_free[i] = w
            ring[1] = 6
            gate_rows(0)
            prev, end = None, None
            for n in range(8 * NG + 1):
                g, ex = divmod(n, 8)
                each(n)
                if n < 8 * NG:
                    cur = (g, ex, *up(g, ex))
                if end and (n % 8 == 2 or n == 8 * NG):
                    moe_end(end[0], gi, end[1])
                    done(end[0])
                    end = None
                if prev:
                    pg, pex, hid, th, freed = prev
                    if pex == 0:
                        y = init(pg) if init else None
                    y = moe_back(pg, pex, hid, w2, th, freed, y)
                    if pex == 7:
                        end = (pg, y)
                tick()
                tick()
                if n % 8 == 4 and g + 1 < NG:
                    gate_rows(g + 1)
                prev = cur
            moe_end(end[0], gi, end[1])
            done(end[0])
            while side:
                slot_no[0] += 1
                run_side(1)
            ring[1] = 8

        at_free = [None, None]
        chunk_free = [None] * 8

        if stop >= 4:
            t_m = load_moe1((Q.sem["pe"], pe_after_ffn0[1]))
            set_ones(4, VS, vs_free)
            w_f = list(k8_free)
            fr["xf"] = (Q.sem["dve"], Q.count["dve"])

            def front1(b):
                if b % 4 == 3:
                    chain(front(b // 4, TT, vraw[:, 0:2, :].rearrange("p a b -> p (a b)"), True, "router_w", col("g2"), None, None, w_f, False), 2)

            attention(16, 4, 4, [], [0], prep_f1, finish_mm(64, "w_up", lambda *a: (end_f1(*a), front1(a[0]))), causal=True)
            t = (Q.sem["dve"], Q.count["dve"])
            chunk_free = list(pt_free)
            at_free = [t, t]

            def up1(g, ex):
                hid, th = [], []
                for c in range(2):
                    slot = (2 * ex + c) % 8
                    ba, bb = bank(), bank()
                    o = 256 * ex + 128 * c
                    ta = pe(lambda e, o=o, ba=ba: e.matmul(PSB[ba], WB[:, o:o + 128], TT[:, 512 * g:512 * g + 512], start=True, stop=True),
                            t_m, tt_tok[g], bank_free[ba], inc=True)
                    tb = pe(lambda e, o=o, bb=bb: e.matmul(PSB[bb], WB[:, 2048 + o:2048 + o + 128], TT[:, 512 * g:512 * g + 512],
                                                           start=True, stop=True), bank_free[bb], inc=True)
                    t = act(lambda e, ba=ba, c=c: e.activation(AT[:, c, :], PSB[ba], ACT.Silu), ta, at_free[c])
                    bank_free[ba] = t
                    t = dve(lambda e, bb=bb, c=c, slot=slot: e.tensor_tensor(HB[:, slot, :], PSB[bb], AT[:, c, :], ALU.mult), t, tb,
                            chunk_free[slot])
                    bank_free[bb] = at_free[c] = t
                    hid.append(HB[:, slot, :])
                    th.append(t)

                def freed(tok):
                    for c in range(2):
                        chunk_free[(2 * ex + c) % 8] = tok
                return hid, th, freed

            moe(5, up1, lambda x, c: WB[:, 4096 + 256 * x + 128 * c:4096 + 256 * x + 128 * c + 128], None, gate_tok[NG - 1])

        rows2 = sb("rows2", [128, 8])
        b2 = sb("b2", [8, 128])
        KF = KS[:, :, :].rearrange("p a b -> p (a b)").bitcast(F32)
        QF = Q8[:, :, :].rearrange("p a b -> p (a b)").bitcast(F32)
        CF = K8[:, :, :].rearrange("p a b -> p (a b)").bitcast(F32)
        if stop >= 5:
            t_pe = (Q.sem["pe"], Q.count["pe"])
            t_dve = (Q.sem["dve"], Q.count["dve"])
            W2 = KF[:, 0:4096]
            t_ks = Q.dma("w2", W2, io["W2T"], tuple(ks_free))
            t_w1 = [Q.dma("w1a", KF[:, 4096:6144], io["W1T"][:, 0:2048], tuple(ks_free))]
            t_rows2 = Q.dma("rows2", rows2[:, :], io["bg"].rearrange("(a n) -> a n", a=1).broadcast_to([128, 8]))
            t_b2 = Q.dma("b2", b2[:, :], io["b2"])
            t = pool(lambda e: e.memset(K8[96:128, :, :], 1.0), t_pe)
            k8_free[:] = [t] * 6
            q8_free[:] = [t_pe] * 6
            pt_free[:] = [t_pe] * 8
            set_ones(16, VA, va_free)
            vr_free[:] = [t_pe] * 3
            sp_free[:] = [t_dve] * 2
            fr["xf"], fr["gate"] = t_pe, t_pe
            T2 = WB[:, 0:4096]

            def finish2(b, k, t):
                finish_add(2)(b, k, t)
                if b % 4 == 3:
                    chain(front(b // 4, T2, AT[:, 0, :], False, "WgT", col("gamma"), col("beta"), 1e-8, (t_pe, t_dve), True), 2)

            attention(8, 16, 16, [0], [], prep_ctx(sc_q[3], 16, False), finish2, bias_i=1)

        if stop >= 6:
            t_pe2 = (Q.sem["pe"], Q.count["pe"])
            t_w1.append(Q.dma("w1b", QF[:, 0:2048], io["W1T"][:, 2048:4096], (t_pe2,)))

            def W1(o):
                return KF[:, 4096 + o:4096 + o + 128] if o < 2048 else QF[:, o - 2048:o - 2048 + 128]

            t_gate = gate_tok[NG - 1]
            chunk_free = list(pt_free)
            gT = sp32[0:8, :, :].rearrange("p a b -> p (a b)")
            gT_free = [t_gate]

            def init2(g):
                bt, by = bank(), bank()
                for j in range(4):
                    t = pe(lambda e, j=j: e.transpose(PSB[bt][0:8, 128 * j:128 * j + 128], GT[:, 4 * g + j, :], C("ident")), gate_tok[g],
                           bank_free[bt], inc=(j == 3))
                t = act(lambda e: e.activation(gT, PSB[bt][0:8, :], ACT.Copy), t, gT_free[0])
                bank_free[bt] = t
                t = pe(lambda e: e.matmul(PSB[by], b2[:, :], gT, start=True, stop=True), t, t_b2, bank_free[by], inc=True)
                gT_free[0] = t
                t = act(lambda e: e.activation(xT[:, g % 2, :], PSB[by], ACT.Copy), t, yt_free[g % 2])
                bank_free[by] = t
                return t

            def up2(g, ex):
                hid, th = [], []
                for c in range(4):
                    slot = (4 * ex + c) % 8
                    ba = bank()
                    o = 512 * ex + 128 * c
                    ta = pe(lambda e, o=o, ba=ba: e.matmul(PSB[ba], W1(o), T2[:, 512 * g:512 * g + 512], start=True, stop=True),
                            t_w1[ex // 4], tt_tok[g], bank_free[ba], inc=True)
                    t = act(lambda e, ba=ba, slot=slot, i=4 * ex + c: e.activation(HB[:, slot, :], PSB[ba], ACT.Gelu, bias=col("b1", i)),
                            ta, chunk_free[slot], t_cols)
                    bank_free[ba] = t
                    hid.append(HB[:, slot, :])
                    th.append(t)
                    tick()

                def freed(tok):
                    for c in range(4):
                        chunk_free[(4 * ex + c) % 8] = tok
                return hid, th, freed

            Q.put("pe", lambda e: None, (t_ks,), False)

        MAGIC = 12582912.0
        bidx = sb("bidx", [128, 32])
        bm = sb("bm", [128, 32], BF16)
        onesb = sb("onesb", [128, 1], BF16)
        magic = sb("magic", [128, 1])
        sc = sb("sc", [128, 2, 4, 8])

        def layer3(w):
            W3 = CF[:, 0:1536].rearrange("p (n w) -> p n w", n=3)
            wt = CF[:, 1536:2304].bitcast(BF16).rearrange("p (n w) -> p n w", n=3)
            CX = CF[:, 2304:3328].rearrange("p (b d) -> p b d", b=4)
            UP, DD, GM = (CF[:, 3328 + 512 * i:3840 + 512 * i] for i in range(3))
            RR = [CF[:, 4864 + 512 * i:5376 + 512 * i] for i in range(2)]
            hT, xf = QF[:, 2048:2560], QF[:, 2560:3072]
            qn = QF[:, 3072:3328].bitcast(BF16)
            qT = QF[:, 3328:3840].bitcast(BF16).rearrange("p (k w) -> p k w", k=2)
            H = [QF[:, 4096 + 512 * i:4608 + 512 * i] for i in range(4)] + [WB[:, 4096 + 512 * i:4608 + 512 * i] for i in range(4)]
            q2 = VA[:, :, :].rearrange("p a b -> p (a b)").bitcast(BF16)[:, 0:2048].rearrange("p (k w) -> p k w", k=4)
            q2T = VS[:, :, :].rearrange("p a b -> p (a b)").bitcast(BF16)[:, 0:2048].rearrange("p (k w) -> p k w", k=4)
            EB = r32[:, :, :].rearrange("p a b -> p (a b)").bitcast(BF16)[:, 0:512].rearrange("p (k t) -> p k t", k=4)
            ws = small[:, 2, :]
            free = {n: w for n in ("cx", "up", "dd", "gm", "rr0", "rr1", "hT", "xf", "qn", "qT0", "qT1", "sil0", "sil1", "eb", "sc0", "sc1")}
            h_free, q2_free, q2T_free = [w] * 8, [w] * 4, [w] * 4
            tok = {}

            def b4(a):
                return a.rearrange("p (b d) -> p b d", b=4)

            def w0():
                for i, name in enumerate(("qg", "qu", "qd")):
                    tok["w"] = Q.dma("wb3", W3[:, i, :], io[name], (w,))
                tok["row0"] = Q.dma("row0", rows[:, 0, :], row_bc("b_in", 0), (w,))
                tok["row1"] = Q.dma("row1", rows[:, 1, :], row_bc("g_init", 1), (w,))
                tok["magic"] = dve(lambda e: e.memset(magic[:, :], -MAGIC))
                tok["ones"] = dve(lambda e: e.memset(onesb[:, :], 1.0))

            def m0():
                mb = misc()
                t = dve(lambda e: e.tensor_copy(btmp[:, :], ints[:, 2, :]), t_i)
                tp = pe(lambda e: e.matmul(PSB[mb][:, 0:32], C("tri"), btmp[:, :], start=True, stop=True), t, bank_free[mb], inc=True)
                t = dve(lambda e: e.tensor_scalar(bidx[:, :], PSB[mb][:, 0:32], -1.0, None, ALU.add), tp)
                bank_free[mb] = t
                t = dve(lambda e: e.tensor_scalar(btmp[:, :], bidx[:, :], 0.0, 128.0, ALU.is_lt, ALU.mult), t)
                tok["bidx"] = dve(lambda e: e.tensor_tensor(bidx[:, :], bidx[:, :], btmp[:, :], ALU.add), t)

            def w1():
                tok["w"] = dve(lambda e: e.tensor_reduce(ws[:, 0:3], W3, AX.X, ALU.add, apply_absolute_value=True), tok["w"])
                tok["row1"] = dve(lambda e: e.tensor_scalar(rows[:, 1, :], rows[:, 1, :], cu, None, ALU.mult), tok["row1"])

            def w2():
                mb = misc()
                tp = pe(lambda e: e.matmul(PSB[mb][:, 0:3], C("ones"), ws[:, 0:3], start=True, stop=True), tok["w"], bank_free[mb], inc=True)
                t = dve(lambda e: e.tensor_scalar(ws[:, 4:7], PSB[mb][:, 0:3], 1.0 / 65536.0, 1e-5, ALU.mult, ALU.max), tp)
                bank_free[mb] = t
                t = dve(lambda e: e.reciprocal(ws[:, 8:11], ws[:, 4:7]), t)
                tok["ws"] = dve(lambda e: e.reciprocal(ws[:, 12:15], ws[:, 8:11]), t)

            def w3(i):
                t = dve(lambda e: e.tensor_scalar(W3[:, i, :], W3[:, i, :], ws[:, 8 + i:9 + i], MAGIC, ALU.mult, ALU.add), tok["ws"])
                t = dve(lambda e: e.tensor_scalar(W3[:, i, :], W3[:, i, :], -MAGIC, 1.0, ALU.add, ALU.min), t)
                tok["wt"] = dve(lambda e: e.tensor_scalar(wt[:, i, :], W3[:, i, :], -1.0, None, ALU.max), t)

            setup = [w0, m0, w1, w2, lambda: w3(0), lambda: w3(1), lambda: w3(2)]

            def context(g):
                got = {}
                rr = f"rr{g % 2}"

                def c0():
                    got["c"] = Q.dma("cx", CX, io["ctx_2048"][4 * g:4 * g + 4].rearrange("b t d -> t b d"), (free["cx"],))

                def c1():
                    for j in range(4):
                        t = dve(lambda e, j=j: e.tensor_scalar(EB[:, j, :], C("iota_t"), bidx[:, 4 * g + j:4 * g + j + 1], None, ALU.is_equal),
                                tok["bidx"], free["eb"])
                    got["e"] = t

                def c2():
                    mb = misc()
                    for j in range(4):
                        t = pe(lambda e, j=j: e.matmul(PSB[mb][:, j:j + 1], EB[:, j, :], onesb[:, :], start=True, stop=True), got["e"],
                               tok["ones"], bank_free[mb], inc=(j == 3))
                    free["eb"] = t
                    got["bm"] = bank_free[mb] = dve(lambda e: e.tensor_scalar(bm[:, 4 * g:4 * g + 4], PSB[mb][:, 0:4], 1.0, None, ALU.min), t)

                def c3():
                    got["s"] = norm_in(CX, 4, (got["c"],), rms=True)

                def c4():
                    mb = misc()
                    for j in range(4):
                        t = pe(lambda e, j=j: e.matmul(PSB[mb][:, 128 * j:128 * j + 128], bm[:, 4 * g + j:4 * g + j + 1].broadcast_to([128, 128]),
                                                       trib[:, :], start=True, stop=True), got["bm"], t_cb, bank_free[mb], inc=(j == 3))
                    t = dve(lambda e: e.tensor_scalar(GM, PSB[mb], -1.0, 0.0, ALU.add, ALU.max), t, free["gm"])
                    bank_free[mb] = t
                    got["gm"] = dve(lambda e: e.tensor_scalar(GM, GM, 127.0, C("iota_p"), ALU.min, ALU.is_equal), t)

                def c5():
                    t = norm_out(got["s"], lambda j: UP[:, 128 * j:128 * j + 128], (free["up"],))
                    free["cx"] = t
                    got["u"] = dve(lambda e: e.tensor_tensor(b4(UP), b4(UP), rows[:, 1, :].unsqueeze(1).broadcast_to([128, 4, 128]), ALU.mult),
                                   t, tok["row1"])

                def c6():
                    mb = misc()
                    t = pe(lambda e: e.matmul(PSB[mb], C("toep"), UP, start=True, stop=True), got["u"], bank_free[mb], inc=True)
                    free["up"] = t
                    got["d"] = bank_free[mb] = act(lambda e: e.activation(DD, PSB[mb], ACT.Copy), t, free["dd"])

                def c7():
                    mb = misc()
                    for j in range(4):
                        o = slice(128 * j, 128 * j + 128)
                        t = pe(lambda e, o=o: e.matmul(PSB[mb][:, o], GM[:, o], DD[:, o], start=True, stop=True), got["gm"], got["d"],
                               bank_free[mb], inc=(j == 3))
                    free["dd"] = free["gm"] = t
                    tok["r", g] = bank_free[mb] = dve(lambda e: e.tensor_tensor(b4(RR[g % 2]), b4(PSB[mb]),
                                                                               rows[:, 0, :].unsqueeze(1).broadcast_to([128, 4, 128]), ALU.add),
                                                      t, free[rr], tok["row0"])

                return [c0, (c1, 4), c2, c3, c4, (c5, 6), (c6, 4), c7]

            def scale_of(am, inv, t):
                t = dve(lambda e: e.tensor_scalar(am, am, 1e-5, None, ALU.max), t)
                t = dve(lambda e: e.reciprocal(inv, am), t)
                t = dve(lambda e: e.tensor_scalar(am, inv, 127.0, None, ALU.mult), t)
                return t, dve(lambda e: e.reciprocal(inv, am), t)

            def own(g):
                k = g % 2
                bs = slice(4 * g, 4 * g + 4)
                got = {}
                qk, sk = f"qT{k}", f"sc{k}"
                S = sc[:, k]

                def x0():
                    got["s"] = norm_in(X[:, bs, :], 4, xg(g))

                def x1():
                    t = norm_out(got["s"], lambda j: xf[:, 128 * j:128 * j + 128], (free["xf"],))
                    got["s"] = norm_in(b4(xf), 4, (t,), rms=True)

                def x2():
                    got["x"] = norm_out(got["s"], lambda j: xf[:, 128 * j:128 * j + 128])

                def x3():
                    mb = misc()
                    for j in range(4):
                        t = pe(lambda e, j=j: e.transpose(PSB[mb][:, 128 * j:128 * j + 128], xf[:, 128 * j:128 * j + 128], C("ident")), got["x"],
                               bank_free[mb], inc=(j == 3))
                    free["xf"] = t
                    got["h"] = bank_free[mb] = act(lambda e: e.activation(hT, PSB[mb], ACT.Copy, scale=col("g_res")), t, free["hT"])

                def x4():
                    mb = misc()
                    for j in range(4):
                        o = slice(128 * j, 128 * j + 128)
                        t = pe(lambda e, o=o: e.matmul(PSB[mb][:, o], hT[:, o], wsm["W_inT"], start=True, stop=True), got["h"], t_ws,
                               bank_free[mb], inc=(j == 3))
                    free["hT"] = t
                    R = RR[k]
                    t = dve(lambda e: e.tensor_tensor(R, PSB[mb], R, ALU.add), t, tok["r", g])
                    bank_free[mb] = t
                    t = dve(lambda e: e.scalar_tensor_tensor(out=X[:, bs, :], in0=b4(R), scalar=tg[:, 3:4], in1=X[:, bs, :], op0=ALU.mult,
                                                             op1=ALU.add), t, t_tg, *xg(g))
                    free[f"rr{k}"] = t
                    for j in range(4):
                        x_tok[4 * g + j] = t

                def f0():
                    got["s"] = norm_in(X[:, bs, :], 4, xg(g))

                def f1():
                    t = norm_out(got["s"], lambda j: xf[:, 128 * j:128 * j + 128], (free["xf"],))
                    t = dve(lambda e: e.tensor_reduce(S[:, :, 0:1], b4(xf), AX.X, ALU.max, apply_absolute_value=True), t, free[sk])
                    t, ti = scale_of(S[:, :, 0:1], S[:, :, 1:2], t)
                    ti = dve(lambda e: e.tensor_scalar(S[:, :, 2:3], S[:, :, 1:2], ws[:, 12:13], 0.5, ALU.mult, ALU.mult), ti, tok["ws"])
                    ti = dve(lambda e: e.tensor_scalar(S[:, :, 3:4], S[:, :, 1:2], ws[:, 13:14], None, ALU.mult), ti)
                    got["sc"] = dve(lambda e: e.tensor_tensor(S[:, :, 3:4], S[:, :, 3:4], S[:, :, 2:3], ALU.mult), ti)
                    t = dve(lambda e: e.tensor_tensor(b4(xf), b4(xf), S[:, :, 0:1].broadcast_to([128, 4, 128]), ALU.mult), t)
                    got["q"] = dve(lambda e: e.tensor_scalar(xf, xf, MAGIC, MAGIC + 127.0, ALU.add, ALU.min), t)

                def f2():
                    got["q"] = free["xf"] = act(lambda e: e.activation(qn, xf, ACT.Identity, bias=magic[:, :]), got["q"], tok["magic"], free["qn"])

                def f3():
                    mb = misc()
                    for j in range(4):
                        t = pe(lambda e, j=j: e.transpose(PSB[mb].bitcast(BF16)[:, 128 * j:128 * j + 128], qn[:, 128 * j:128 * j + 128],
                                                          identb[:, :]), got["q"], bank_free[mb], inc=(j == 3))
                    free["qn"] = t
                    got["qT"] = bank_free[mb] = act(lambda e: e.activation(qT[:, k, :], PSB[mb].bitcast(BF16)[:, 0:512], ACT.Copy), t, free[qk])

                def up(j):
                    h, sl = 4 * k + j, f"sil{j % 2}"
                    ba, bb = misc(), misc()
                    ta = pe(lambda e: e.matmul(PSB[ba], qT[:, k, 128 * j:128 * j + 128], wt[:, 0, :], start=True, stop=True), got["qT"],
                            tok["wt"], bank_free[ba], inc=True)
                    tb = pe(lambda e: e.matmul(PSB[bb], qT[:, k, 128 * j:128 * j + 128], wt[:, 1, :], start=True, stop=True), bank_free[bb],
                            inc=True)
                    if j == 3:
                        free[qk] = tb
                    t = act(lambda e: e.activation(AT[:, j % 2, :], PSB[ba], ACT.Tanh, scale=S[:, j, 2:3]), ta, got["sc"], free[sl])
                    t = dve(lambda e: e.scalar_tensor_tensor(out=AT[:, j % 2, :], in0=AT[:, j % 2, :], scalar=1.0, in1=PSB[ba], op0=ALU.add,
                                                             op1=ALU.mult), t)
                    bank_free[ba] = t
                    t = dve(lambda e: e.scalar_tensor_tensor(out=H[h], in0=PSB[bb], scalar=S[:, j, 3:4], in1=AT[:, j % 2, :], op0=ALU.mult,
                                                             op1=ALU.mult), t, tb, h_free[h])
                    bank_free[bb] = free[sl] = t
                    got["m"] = dve(lambda e: e.tensor_reduce(S[:, j, 4:5], H[h], AX.X, ALU.max, apply_absolute_value=True), t)

                def scales():
                    t, ti = scale_of(S[:, :, 4:5], S[:, :, 5:6], got["m"])
                    got["qs"] = t
                    got["so"] = dve(lambda e: e.tensor_scalar(S[:, :, 6:7], S[:, :, 5:6], ws[:, 14:15], tg[:, 7:8], ALU.mult, ALU.mult), ti, t_tg)

                def quant(j):
                    h = 4 * k + j
                    t = act(lambda e: e.activation(H[h], H[h], ACT.Copy, scale=S[:, j, 4:5]), got["qs"])
                    t = dve(lambda e: e.tensor_scalar(H[h], H[h], MAGIC, MAGIC + 127.0, ALU.add, ALU.min), t)
                    got["q2", j] = h_free[h] = pool(lambda e: e.tensor_scalar(q2[:, j, :], H[h], -MAGIC, None, ALU.add), t, q2_free[j])

                def turn(j):
                    mb = misc()
                    for c in range(4):
                        t = pe(lambda e, c=c: e.transpose(PSB[mb].bitcast(BF16)[:, 128 * c:128 * c + 128], q2[:, j, 128 * c:128 * c + 128],
                                                          identb[:, :]), got["q2", j], bank_free[mb], inc=(c == 3))
                    q2_free[j] = t
                    got["T", j] = bank_free[mb] = act(lambda e: e.activation(q2T[:, j, :], PSB[mb].bitcast(BF16)[:, 0:512], ACT.Copy), t,
                                                      q2T_free[j])

                def down(j):
                    mb = misc()
                    b = 4 * g + j
                    for c in range(4):
                        t = pe(lambda e, c=c: e.matmul(PSB[mb][:, 0:128], q2T[:, j, 128 * c:128 * c + 128], wt[:, 2, 128 * c:128 * c + 128],
                                                       start=(c == 0), stop=(c == 3)), got["T", j], bank_free[mb], inc=(c == 3))
                    q2T_free[j] = t
                    t = dve(lambda e: e.scalar_tensor_tensor(out=X[:, b, :], in0=PSB[mb][:, 0:128], scalar=S[:, j, 6:7], in1=X[:, b, :],
                                                             op0=ALU.mult, op1=ALU.add), t, got["so"], x_tok[b])
                    bank_free[mb] = x_tok[b] = t
                    if j == 3:
                        free[sk] = t

                def step(f, j):
                    return lambda: f(j)

                fns = [(x0, 2), (x1, 2), (x2, 4), (x3, 3), (x4, 2)]
                if stop >= 8:
                    fns += [(f0, 2), (f1, 2), (f2, 4), (f3, 3), *((step(up, j), 2) for j in range(4)), scales,
                            *(step(quant, j) for j in range(4)), (step(turn, 0), 2), (step(turn, 1), 2), (step(down, 0), 2),
                            (step(turn, 2), 2), (step(down, 1), 2), (step(turn, 3), 2), (step(down, 2), 2), step(down, 3)]
                return fns

            return setup, context, own

        if stop >= 6:
            each, done = (lambda n: None), (lambda g: None)
            if stop >= 7:
                setup, context, own = layer3(t_gate)

                def each(n):
                    if n == 0:
                        chain(setup, 2)
                    if n % 8 == 2 and n // 8 < NG:
                        chain(context(n // 8), 2)

                def done(g):
                    chain(own(g), 1)

            moe(6, up2, lambda x, c: W2[:, 512 * x + 128 * c:512 * x + 128 * c + 128], init2, t_gate, each, done)

        t_o = Q.dma("out", out.rearrange("b t d -> t b d"), X[:, :, :], tuple(x_tok[b] for b in range(B)))
        Q.put("sp", lambda e: None, (t_o,), inc=False)

        blk = ctx.enter_context(nc.Block())
        blk.sync(lambda e: Q.emit("sp", e))
        blk.tensor(lambda e: Q.emit("pe", e))
        blk.vector(lambda e: Q.emit("dve", e))
        blk.scalar(lambda e: Q.emit("act", e))
        blk.gpsimd(lambda e: Q.emit("pool", e))


def layout(inputs):
    n = {k: np.asarray(v) for k, v in inputs.items()}
    c = np.ascontiguousarray

    def kT(w, k):
        return c(w.T.reshape(k, 128, w.shape[0]).transpose(1, 0, 2)).reshape(128, -1)

    def per_part(v):
        return c(v.reshape(-1, 128).T)

    a = {"x": c(n["x"]), "ctx_2048": c(n["ctx_2048"]), "seq": c(n["itok_Bx1_68_817"])}
    a["kT"] = c(n["ctx_2048"][:, :, :128].transpose(2, 0, 1)[by_place(16, 8)]).reshape(128, B * S)
    a["maskT"] = c(n["mask_BxS2_ik0"].T)
    a["lensT"] = c(n["mask_BxS2_if0"].T)
    a["g_xattn"], a["g_ffn"] = c(n["g_xattn"]), c(n["g_ffn"])
    a["L0_xattn_b"] = per_part(n["L0_xattn_b"])
    a["L2_b"] = c(np.broadcast_to(n["L2_xattn_b"].reshape(1, 1), (128, 1)))
    for k in ("w1_s", "w2_s", "h1_s", "h2_s"):
        a[k] = per_part(n["L0_ffn_" + k])
    a["w3_s"] = per_part(n["L0_ffn_w3_s"])
    a["w1T"], a["w2T"] = kT(n["L0_ffn_w1_w"], 1), kT(n["L0_ffn_w2_w"], 1)
    a["h1T"], a["h2T"], a["w3T"] = kT(n["L0_ffn_h1_w"], 4), kT(n["L0_ffn_h2_w"], 4), kT(n["L0_ffn_w3_w"], 4)
    rows = np.concatenate([by_place(16, 8), 128 + by_place(16, 8), 256 + np.arange(128)])
    a["w_qkvT"], a["w_projT"] = c(n["L1_xattn_w_qkv"][rows].T), c(n["L1_xattn_w_proj"].T)
    a["b_proj"] = c(n["L1_xattn_b_proj"])
    a["g1"], a["g2"] = per_part(n["L1_ffn_g1"]), per_part(n["L1_ffn_g2"])
    a["w_down"] = c(n["L1_ffn_w_down"])
    pl = by_place(16, 4)
    sw = pl ^ 1
    a["wqk"] = c(np.concatenate([n["L1_ffn_wq"][:, pl], n["L1_ffn_wk"][:, pl]], 1))
    a["wqk_sw"] = c(np.concatenate([n["L1_ffn_wq"][:, sw], n["L1_ffn_wk"][:, sw]], 1))
    a["wv"], a["w_up"], a["router_w"] = c(n["L1_ffn_wv"]), c(n["L1_ffn_w_up"]), c(n["L1_ffn_router_w"])
    a["m1"] = c(n["L1_ffn_w1"].transpose(1, 0, 2)).reshape(128, 2048)
    a["m3"] = c(n["L1_ffn_w3"].transpose(1, 0, 2)).reshape(128, 2048)
    a["m2"] = c(n["L1_ffn_w2"].reshape(16, 128, 128).transpose(1, 0, 2)).reshape(128, 2048)
    a["gamma"], a["beta"] = per_part(n["L2_ffn_gamma"]), per_part(n["L2_ffn_beta"])
    a["WgT"], a["bg"] = c(n["L2_ffn_Wg"].T), c(n["L2_ffn_bg"])
    a["W1T"] = c(n["L2_ffn_W1"].transpose(2, 0, 1)).reshape(128, 4096)
    a["b1"] = per_part(n["L2_ffn_b1"])
    a["W2T"] = c(n["L2_ffn_W2"].transpose(0, 2, 1).reshape(32, 128, 128).transpose(1, 0, 2)).reshape(128, 4096)
    a["b2"] = c(n["L2_ffn_b2"])
    a["W_inT"], a["b_in"] = c(n["L3_xattn_W_in"].T), c(n["L3_xattn_b_in"])
    a["g_res"], a["g_init"] = per_part(n["L3_xattn_g_res"]), c(n["L3_xattn_g_init"])
    a["qg"], a["qu"], a["qd"] = kT(n["L3_ffn_w_gate"], 1), kT(n["L3_ffn_w_up"], 1), kT(n["L3_ffn_w_down"], 4)
    a["cols"] = c(np.concatenate([a.pop(name) for name, _ in COLS], axis=1))
    return a


def kernel(**inputs):
    import concourse.bacc as _bacc
    from concourse.bass_utils import run_bass_kernel_spmd as _run

    nc = _bacc.Bacc("TRN2", target_bir_lowering=False, num_devices=1)
    block, cu = const_block()
    arrays = {f"in_{k}": v for k, v in {**layout(inputs), "cst": block}.items()}
    io = {k[3:]: nc.dram_tensor(k, v.shape, mybir.dt.from_np(v.dtype), kind="ExternalInput").ap() for k, v in arrays.items()}
    out = nc.dram_tensor("out", (B, S, D), F32, kind="ExternalOutput").ap()
    build(nc, io, out, cu)
    r = _run(nc, [arrays], core_ids=[0])
    return r.results[0]["out"]
```

```python
from contextlib import ExitStack

import numpy as np

import concourse.bass as bass
from concourse import mybir

F32 = mybir.dt.float32
BF16 = mybir.dt.bfloat16
I32 = mybir.dt.int32
F32R = mybir.dt.float32r
ALU = mybir.AluOpType
ACT = mybir.ActivationFunctionType
AX = mybir.AxisListType

B, S, D = 32, 128, 128
NP = B // 2
NG = B // 4
PVLAG = 2
EPS = 1e-5

COLS = (("L0_xattn_b", 1), ("L2_b", 1), ("w1_s", 4), ("w2_s", 4), ("h1_s", 4), ("h2_s", 4), ("w3_s", 1), ("g1", 1), ("g2", 1),
        ("gamma", 1), ("beta", 1), ("g_res", 1), ("b1", 32))
SMALL = (("w_qkvT", 128, 384), ("w_projT", 128, 128), ("w_down", 128, 64), ("wqk", 64, 128), ("wqk_sw", 64, 128), ("wv", 64, 64),
         ("w_up", 64, 128), ("router_w", 128, 8), ("WgT", 128, 8), ("W_inT", 128, 128))
CST = {}


def by_place(n, d):
    return np.arange(n * d).reshape(n, d).T.reshape(-1)


def const_block():
    f = np.float32
    j = np.arange(128)[:, None]
    t = np.arange(128)[None, :]
    parts = []

    def put(name, a):
        CST[name] = (sum(p.shape[1] for p in parts), a.shape[1])
        parts.append(np.ascontiguousarray(a, f))

    put("ident", (j == t).astype(f))
    put("tri", (j <= t).astype(f))
    logp = f(-0.001)
    dt = f(-np.log(-np.expm1(logp)))
    a = f(np.exp(-dt))
    put("toep", np.where(t >= j, np.power(np.float64(a), np.maximum(t - j, 0)), 0.0))
    put("iota_t", np.broadcast_to(t, (128, 128)))
    put("iota_p", j.astype(f))
    put("cneg", np.where(t > j, -1e30, 0.0))
    put("cnegT", np.where(j > t, -1e30, 0.0))
    put("selb", (np.arange(128)[:, None] % 32 == np.arange(32)[None, :]).astype(f))
    put("sel8", (np.arange(128)[:, None] % 8 == np.arange(8)[None, :]).astype(f))
    inv = (f(1.0) / np.power(f(10000.0), np.arange(0, 4, 2, dtype=f) / f(4))).astype(f)
    ang = np.arange(128, dtype=f)[None, :] * inv[(np.arange(128) % 4) // 2][:, None]
    half = np.where(np.arange(128) < 64, 0.5, 1.0).astype(f)[:, None]
    sign = np.where(np.arange(128) % 2 == 0, -1.0, 1.0).astype(f)[:, None]
    place = np.concatenate([by_place(16, 4), 64 + by_place(16, 4)])
    put("cos", (np.cos(ang).astype(f) * half)[place])
    put("sin", (np.sin(ang).astype(f) * sign * half)[place])
    i8 = np.arange(64)
    put("low", np.broadcast_to((i8 % 8 < i8 // 8).astype(f)[None, :], (128, 64)))
    put("ones", np.ones((128, 128), f))
    put("half", np.full((128, 32), -0.5, f))
    return np.concatenate(parts, axis=1), float(f(dt * f(np.exp(logp))) / dt)


def flat(waits):
    out = ()
    for w in waits:
        if w is not None:
            out += flat(w) if isinstance(w[0], tuple) else (w,)
    return out


class Queues:

    def __init__(self, nc, ctx):
        self.nc = nc
        self.names = ["pe", "dve", "act", "pool", "sp"]
        self.list = {n: [] for n in self.names}
        self.count = {n: 0 for n in self.names}
        self.sem = {n: ctx.enter_context(nc.semaphore("done_" + n)) for n in self.names}
        self.dsem = {}
        self.dcount = {}
        self.ctx = ctx

    def put(self, eng, fn, waits, inc=True):
        self.list[eng].append((fn, flat(waits), (self.sem[eng], 1) if inc else None))
        if inc:
            self.count[eng] += 1
        return (self.sem[eng], self.count[eng])

    def dma(self, name, out, in_, waits=(), eng="sp", **kw):
        if name not in self.dsem:
            self.dsem[name] = self.ctx.enter_context(self.nc.semaphore("dma_" + name))
            self.dcount[name] = 0
        self.dcount[name] += 16
        self.list[eng].append((lambda e: e.dma_start(out, in_, **kw), flat(waits), (self.dsem[name], 16)))
        return (self.dsem[name], self.dcount[name])

    def emit(self, eng, handle):
        seen = {}
        for fn, waits, inc in self.list[eng]:
            for s, v in waits:
                if seen.get(s.name, 0) < v:
                    handle.wait_ge(s, v)
                    seen[s.name] = v
            ins = fn(handle)
            if ins is not None and inc is not None:
                ins.then_inc(*inc)


def build(nc, io, out, cu, stop=99):
    ctx = ExitStack()
    with ctx:
        Q = Queues(nc, ctx)

        def sb(name, shape, dt=F32):
            return ctx.enter_context(nc.sbuf_tensor(name, shape, dt))

        def dve(fn, *w, inc=True):
            return Q.put("dve", fn, w, inc)

        def act(fn, *w):
            return Q.put("act", fn, w)

        def pool(fn, *w):
            return Q.put("pool", fn, (*w, (Q.sem["pool"], Q.count["pool"])))

        def pe(fn, *w, inc=False):
            return Q.put("pe", fn, w, inc)

        PSB = [ctx.enter_context(nc.psum_tensor(f"psb{i}", [128, 512], F32)) for i in (0, 1)]
        PSD = [ctx.enter_context(nc.psum_tensor(f"psd{i}", [128, 1024], F32)) for i in (0, 1)]
        PSB += [PSD[0][:, 0:512], PSD[0][:, 512:1024], PSD[1][:, 0:512], PSD[1][:, 512:1024]]
        PSB += [ctx.enter_context(nc.psum_tensor(f"psb{i}", [128, 512], F32)) for i in (6, 7)]
        PSB = [b[:, :] for b in PSB]
        bank_free = [None] * 8

        ncst = sum(w for _, w in CST.values())
        cst = sb("cst", [128, ncst])

        def C(name):
            o, w = CST[name]
            return cst[:, o:o + w]

        X = sb("X", [128, B, D])
        with (nc.sbuf_tensor("UFr", [128, 4096], F32R) as UFr, nc.sbuf_tensor("WBr", [128, 6144], F32R) as WBr,
              nc.sbuf_tensor("WSr", [128, 1216], F32), nc.sbuf_tensor("QFr", [128, 6144], F32R) as QFr,
              nc.sbuf_tensor("CFr", [128, 6144], F32R) as CFr, nc.sbuf_tensor("KFr", [128, 6144], F32R) as KFr,
              nc.sbuf_tensor("xnr", [128, 2, 512], F32R) as xnr, nc.sbuf_tensor("HBr", [128, 8, 512], F32R) as HBr,
              nc.sbuf_tensor("OEr", [128, 2, 512], F32R) as OEr):
            pass
        U = sb("U", [128, B, D])
        WB = sb("WB", [128, 6144])
        WS = sb("WS", [128, 1216])
        Q8 = sb("Q8", [128, 3, 4096], BF16)
        K8 = sb("K8", [128, 3, 4096], BF16)
        KS = sb("KS", [128, 3, 4096], BF16)
        xn = sb("xn", [128, 2, 512])
        HB = sb("HB", [128, 8, 512])
        OE = sb("OE", [128, 2, 512])
        AT = sb("AT", [128, 2, 512])
        TT = K8[:, :, :].rearrange("p a b -> p (a b)").bitcast(F32)
        tg = sb("tg", [128, 8])
        graw = sb("graw", [128, 8])
        cols = sb("cols", [128, sum(w for _, w in COLS)])
        rows = sb("rows", [128, 2, 128])
        identb = sb("identb", [128, 128], BF16)
        cnegb = sb("cnegb", [128, 2, 128], BF16)
        selbb = sb("selbb", [96, 32], BF16)
        sel8b = sb("sel8b", [24, 8], BF16)
        trib = sb("trib", [128, 128], BF16)
        bias = sb("bias", [128, 2, 32])
        biasc = sb("biasc", [128, 2, 96], BF16)
        biasT = sb("biasT", [96, 2, 128], BF16)
        btmp = sb("btmp", [128, 32])
        ints = sb("ints", [128, 3, 32], I32)
        st = sb("st", [128, 4, 4, 6])
        mv = sb("mv", [128, 4, 4, 2])
        rs = sb("rs", [128, 4, 4, 2])
        xT = sb("xT", [128, 2, 512])
        sp32 = sb("sp32", [128, 2, 256])
        r32 = sb("r32", [128, 2, 256])
        comp = sb("comp", [128, 4, 3 * 256], BF16)
        vraw = sb("vraw", [128, 3, 256])
        VA = sb("VA", [128, 4, 2 * 144])
        VS = sb("VS", [128, 4, 2 * 144])
        mneg = sb("mneg", [128, 4, 16])
        mres = sb("mres", [128, 16])
        mcb = sb("mcb", [128, 4, 48], BF16)
        mT = sb("mT", [48, 4, 128], BF16)
        rec = sb("rec", [128, 2, 16])
        otmp = sb("otmp", [128, 2, 128])
        oT = sb("oT", [128, 2, 128])
        LG = sb("LG", [128, B, 8])
        GT = sb("GT", [128, B, 8])

        def scratch(name, n=128):
            return nc.dram_tensor(name, [NP, 6, n, 256], BF16, kind="Internal").ap()

        sc_k = scratch("sc_k")
        sc_q = [scratch(f"sc_q{i}") for i in range(4)]
        sc_s = scratch("sc_s")
        sc_f = [scratch(f"sc_f{i}", 64) for i in range(2)]

        sp_free = [None, None]
        k_in = {}
        k_raw = {}

        def k_load(p):
            k_raw[p] = Q.dma(f"kin{p % 2}", sp32[:, p % 2, :], io["kT"][:, 256 * p:256 * p + 256], (sp_free[p % 2],))

        cut = (0, 4, 16, 32)
        t_x = []

        def x_load(i):
            t = Q.dma(f"x{i}", X[:, cut[i]:cut[i + 1], :], io["x"][cut[i]:cut[i + 1]].rearrange("b t d -> t b d"))
            t_x.extend([t] * (cut[i + 1] - cut[i]))

        k_load(0)
        x_load(0)
        t_cst = Q.dma("cst", cst[:, :], io["cst"])
        k_load(1)
        t_i = Q.dma("ints", ints[:, 0, :], io["seq"].rearrange("b a -> a b").broadcast_to([128, 32]))
        t_i = Q.dma("ints", ints[:, 1, :], io["maskT"])
        t_i = Q.dma("ints", ints[:, 2, :], io["lensT"])
        x_load(1)
        x_load(2)
        t_g = Q.dma("g", graw[:, 0:4], io["g_xattn"].rearrange("(a n) -> a n", a=1).broadcast_to([128, 4]))
        t_g = Q.dma("g", graw[:, 4:8], io["g_ffn"].rearrange("(a n) -> a n", a=1).broadcast_to([128, 4]))

        col_at = {}
        for name, n in COLS:
            col_at[name] = sum(w for nm, w in COLS[:len(col_at)])
        t_cols = Q.dma("cols", cols[:, 0:sum(w for _, w in COLS)], io["cols"])

        def col(name, i=0):
            return cols[:, col_at[name] + i:col_at[name] + i + 1]

        def row_bc(name, k, n=128):
            return io[name].rearrange("(a n) -> a n", a=1)[:, 0:n].broadcast_to([128, n])

        t_row1 = Q.dma("row1", rows[:, 1, :], row_bc("b_proj", 0))

        wb = {}
        wsm = {}
        t_wb = []
        t_ws = None
        at = 0
        for name, n in (("w1T", 512), ("w2T", 512), ("h1T", 2048), ("h2T", 2048), ("w3T", 512)):
            wb[name] = WB[:, at:at + n]
            at += n
        at = 0
        for name, p, n in SMALL:
            wsm[name] = WS[0:p, at:at + n]
            at += n

        def load_weights():
            nonlocal t_ws
            for name in wb:
                t_wb.append(Q.dma("wb", wb[name], io[name]))
            for name, _, _ in SMALL:
                t_ws = Q.dma("ws", wsm[name], io[name])
            del t_wb[:-1]

        def clear(put, tile, p, ones, *w):
            t = put(lambda e: e.memset(tile[0:96, p, :], 0.0), *w)
            return put(lambda e: e.memset(tile[96:128, p, :], 1.0), *w) if ones else t

        q8_free, k8_free, ks_free = [None] * 3, [None] * 3, [None] * 3
        q8_free[1] = clear(dve, Q8, 1, False)
        k8_free[1] = clear(dve, K8, 1, True)
        t_idb = dve(lambda e: e.tensor_copy(identb[:, :], C("ident")), t_cst)
        dve(lambda e: e.tensor_copy(cnegb[:, 0, :], C("cneg")), t_cst)
        dve(lambda e: e.tensor_copy(cnegb[:, 1, :], C("cnegT")), t_cst)
        dve(lambda e: e.tensor_copy(trib[:, :], C("tri")), t_cst)
        dve(lambda e: e.tensor_copy(sel8b[:, :], C("sel8")[0:24, :]), t_cst)
        t_cb = dve(lambda e: e.tensor_copy(selbb[:, :], C("selb")[0:96, :]), t_cst)
        t_tg = act(lambda e: e.activation(tg[:, :], graw[:, :], ACT.Tanh), t_g)

        q8_free[0] = clear(pool, Q8, 0, False)
        k8_free[0] = clear(pool, K8, 0, True)
        t_ones = pool(lambda e: e.memset(VA[:, :, :], 1.0))

        t = dve(lambda e: e.tensor_copy(btmp[:, :], ints[:, 0, :]), t_i)
        t = dve(lambda e: e.tensor_scalar(btmp[:, :], btmp[:, :], C("iota_p"), -1.0, ALU.is_gt, ALU.add), t, t_cst)
        t = dve(lambda e: e.tensor_scalar(bias[:, 0, :], btmp[:, :], 1e12, col("L0_xattn_b"), ALU.mult, ALU.add), t, t_cols)
        t = dve(lambda e: e.tensor_copy(btmp[:, :], ints[:, 1, :]), t)
        t = dve(lambda e: e.tensor_scalar(btmp[:, :], btmp[:, :], -1.0, 1e30, ALU.add, ALU.mult), t)
        t_bias = dve(lambda e: e.tensor_scalar(bias[:, 1, :], btmp[:, :], col("L2_b"), None, ALU.add), t, t_cols)
        t = t_bias
        for i in range(2):
            b3 = biasc[:, i, :].rearrange("p (c b) -> p c b", c=3)
            t = dve(lambda e, i=i, b3=b3: e.tensor_copy(b3[:, 0, :], bias[:, i, :]), t)
            t = dve(lambda e, i=i, b3=b3: e.tensor_tensor(btmp[:, :], bias[:, i, :], b3[:, 0, :], ALU.subtract), t)
            t = dve(lambda e, i=i, b3=b3: e.tensor_copy(b3[:, 1, :], btmp[:, :]), t)
            t = dve(lambda e, i=i, b3=b3: e.tensor_tensor(b3[:, 2, :], btmp[:, :], b3[:, 1, :], ALU.subtract), t)
            tp = pe(lambda e, i=i: e.transpose(PSB[7].bitcast(BF16)[0:96, 128 * i:128 * i + 128], biasc[:, i, :], identb[:, :]),
                    t, t_idb, bank_free[7], inc=True)
            t = dve(lambda e, i=i: e.tensor_copy(biasT[:, i, :], PSB[7].bitcast(BF16)[0:96, 128 * i:128 * i + 128]), tp)
            bank_free[7] = t
        t_biasT = t
        for tile, lo, hi, v in ((Q8, 0, 96, 0.0), (K8, 0, 96, 0.0), (K8, 96, 128, 1.0)):
            t = act(lambda e, tile=tile, lo=lo, hi=hi, v=v: e.activation(
                tile[lo:hi, 2, :].rearrange("p (a b) -> p a b", b=128), C("ones")[lo:hi, :].unsqueeze(1).broadcast_to([hi - lo, 32, 128]),
                ACT.Copy, scale=v), t_cst)
            (q8_free if tile is Q8 else k8_free)[2] = t

        st_free = [None] * 4
        turn = [0]

        def norm_in(src, n, waits, eps=EPS, rms=False):
            k = turn[0] % 4
            turn[0] += 1
            for j in range(n):
                t = dve(lambda e, j=j: e.bn_stats(st[:, k, j, :], src[:, j, :]), *waits, st_free[k])
            for j in range(n):
                t = dve(lambda e, j=j: e.bn_aggr(mv[:, k, j, :], st[:, k, j, :]), t)
            m, v = mv[:, k, 0:n, 0:1], mv[:, k, 0:n, 1:2]
            r0, r1 = rs[:, k, 0:n, 0:1], rs[:, k, 0:n, 1:2]
            if rms:
                t = pool(lambda e: e.tensor_tensor(r0, m, m, ALU.mult), t)
                t = pool(lambda e: e.tensor_tensor(r0, r0, v, ALU.add), t)
                t = pool(lambda e: e.tensor_scalar(r0, r0, eps, None, ALU.add), t)
            else:
                t = pool(lambda e: e.tensor_scalar(r0, v, eps, None, ALU.add), t)
            t = pool(lambda e: e.tensor_tensor(r1, r0, C("half")[:, 0:n].unsqueeze(2), ALU.pow), t, t_cst)
            return src, n, k, t, rms

        def norm_out(state, outs, waits=(), width=128, view=lambda a: a):
            src, n, k, t, rms = state
            for j in range(n):
                if rms:
                    t2 = dve(lambda e, j=j: e.tensor_scalar(outs(j), view(src[:, j, 0:width]), rs[:, k, j, 1:2], None, ALU.mult), t, *waits)
                else:
                    t2 = dve(lambda e, j=j: e.tensor_scalar(outs(j), view(src[:, j, :]), mv[:, k, j, 0:1], rs[:, k, j, 1:2],
                                                            ALU.subtract, ALU.mult), t, *waits)
            st_free[k] = t2
            return t2

        def norm(src, n, waits, outs, rms=False):
            return norm_out(norm_in(src, n, waits, rms=rms), outs)

        xn_free = [None, None]
        xT_free = [None, None]

        def turned(k, n, bank, t, scale=None, bcol=None, dst=None, dst_free=None):
            dst = xT[:, k, 0:128 * n] if dst is None else dst
            for j in range(n):
                tp = pe(lambda e, j=j: e.transpose(PSB[bank][:, 128 * j:128 * j + 128], xn[:, k, 128 * j:128 * j + 128],
                                                   C("ident")), t, bank_free[bank], t_cst, inc=(j == n - 1))
            xn_free[k] = tp
            s = 1.0 if scale is None else scale
            bz = 0.0 if bcol is None else bcol
            f = ACT.Identity if bcol is not None else ACT.Copy
            ta = act(lambda e: e.activation(dst, PSB[bank][:, 0:128 * n], f, bias=bz, scale=s), tp, xT_free[k], dst_free, t_cols)
            bank_free[bank] = ta
            return ta

        r32_free = [None, None]

        def split(src, dst, t, free, which):
            eng = (pool, dve)[which]
            r = r32[:, which, :]
            t = eng(lambda e: e.tensor_copy(dst[:, 0, :], src), t, free)
            t = eng(lambda e: e.tensor_tensor(r, src, dst[:, 0, :], ALU.subtract), t, r32_free[which])
            t_src = t
            t = eng(lambda e: e.tensor_copy(dst[:, 1, :], r), t)
            t = eng(lambda e: e.tensor_tensor(dst[:, 2, :], r, dst[:, 1, :], ALU.subtract), t)
            r32_free[which] = t
            return t_src, t

        comp_free = [None] * 4
        comp_turn = [0]

        def split_in(src, t, which=0):
            k = comp_turn[0] % 4
            comp_turn[0] += 1
            t_src, t = split(src, comp[:, k, :].rearrange("p (c t) -> p c t", c=3), t, comp_free[k], which)
            return t_src, (k, t)

        def store(parts, dests, p):
            k, t = parts
            dst = comp[:, k, :].rearrange("p (c t) -> p c t", c=3)
            for kind, lo, n, sc in dests:
                for c, (at_, m) in enumerate(((0, 3), (3, 2), (5, 1))):
                    if kind == "q":
                        a = dst[lo:lo + n, 0:m, :]
                    else:
                        a = dst[lo:lo + n, c:c + 1, :].broadcast_to([n, m, 256])
                    td = Q.dma(f"comp{k}", sc[p, at_:at_ + m].rearrange("c p t -> p c t"), a, (t,))
            comp_free[k] = td
            return td

        def load_rows(tile, name, sc, at_, dh, H, p, waits):
            dst = place(tile, at_, H)
            if dh == 16:
                for par in range(2):
                    src = sc[p].rearrange("c (d h e) t -> (c d) h e t", d=8, e=2)[:, :, par, :]
                    t = Q.dma(f"{name}{at_}", dst[48 * par:48 * par + 48, :].rearrange("r (h t) -> r h t", h=8), src, waits)
                return t
            return Q.dma(f"{name}{at_}", dst[0:6 * dh, :], sc[p].rearrange("c (d h) t -> (c d) (h t)", d=dh), waits)

        def place(tile, at_, H):
            w = 256 * H
            return tile[:, at_ * w // 4096, at_ * w % 4096:at_ * w % 4096 + w]

        def k_split(p):
            sp_free[p % 2], k_raw[p] = split_in(sp32[:, p % 2, :], k_raw[p], 1)

        def k_store(p):
            k_in[p] = store(k_raw[p], (("k", 0, 128, sc_k),), p)
            if p + 2 < NP:
                k_load(p + 2)

        x_tok = dict(enumerate(t_x))
        u_tok = {}

        va_free = [t_ones] * 4
        vs_free = [None] * 4
        vr_free = [None] * 3
        pt_free = [None] * 8
        mn_free = [None] * 4
        mcb_free = [None] * 4
        mres_free = [None]
        mT_free = [None] * 4
        rec_free = [None] * 2
        oe_free = [None] * 2
        side = []
        slot_no = [0]
        misc_turn = [0, 3]

        def soon(fn, delay, first=False):
            side.insert(0 if first else len(side), (slot_no[0] + delay, fn, first))

        def run_side(n):
            for _ in range(n):
                for i, (at_, fn, _) in enumerate(side):
                    if at_ <= slot_no[0]:
                        side.pop(i)
                        fn()
                        break

        def misc():
            misc_turn[0] += 1
            return 8 - misc_turn[1] + misc_turn[0] % misc_turn[1]

        def attention(H, dh, vd, ctx_kb, self_kb, prep, finish, bias_i=None, causal=False, base=0, may=lambda p, what: True):
            R = 48 // H
            LAG = 2 if H == 16 else 4
            nkb = len(ctx_kb) + len(self_kb)
            tiles = [K8] * len(ctx_kb) + [KS] * len(self_kb)
            vts = [VA] * len(ctx_kb) + [VS] * len(self_kb)
            RQ = 96
            at_ = lambda p: (p + base) % R
            per_s = 4 // nkb
            n_s = H // per_s
            n_st = (H // 4) * nkb
            prepped = {}
            ready_m = {}
            chain = {}
            pv_wait = []
            nst = [0]

            def vh(vt, p, b2):
                return vt[:, p % 4, 0:2 * H * (vd + 1)].rearrange("p (b h d) -> p b h d", b=2, h=H)[:, b2]

            def head(tile, p, b2, h, rows_):
                return place(tile, at_(p), H)[0:rows_, 256 * h + 128 * b2:256 * h + 128 * b2 + 128]

            def s_unit(b, i):
                p, b2 = divmod(b, 2)
                bank = i % 2
                w = [bank_free[bank], *prepped[p]["qk"]]
                extra = bias_i is not None or causal
                for hh in range(per_s):
                    h = i * per_s + hh
                    for kb in range(nkb):
                        o = PSB[bank][:, 128 * (hh * nkb + kb):128 * (hh * nkb + kb) + 128]
                        last = hh == per_s - 1 and kb == nkb - 1
                        t = pe(lambda e, o=o, h=h, kb=kb, st_=(hh == 0 and kb == 0), sp_=not extra: e.matmul(
                            o, head(Q8, p, b2, h, RQ), head(tiles[kb], p, b2, h, RQ), start=st_, stop=sp_,
                            skip_group_check=True), *w, inc=last and not extra)
                        w = []
                if bias_i is not None:
                    t = pe(lambda e: e.matmul(PSB[bank].rearrange("p (h k) -> p h k", h=4), selbb[:, b:b + 1].broadcast_to([96, 128]),
                                              biasT[:, bias_i, :].unsqueeze(1).broadcast_to([96, 4, 128]), start=False, stop=True,
                                              skip_group_check=True), t_biasT, t_cb, inc=True)
                if causal:
                    t = pe(lambda e: e.matmul(PSB[bank].rearrange("p (h k) -> p h k", h=4), identb[:, :],
                                              cnegb[:, 0, :].unsqueeze(1).broadcast_to([128, 4, 128]), start=False, stop=True,
                                              skip_group_check=True), t_cb, inc=True)
                tr = dve(lambda e: e.tensor_reduce(mneg[:, b % 4, i * per_s:(i + 1) * per_s],
                                                   PSB[bank].rearrange("p (h k) -> p h k", h=per_s), AX.X, ALU.max, negate=True),
                         t, mn_free[b % 4])
                bank_free[bank] = tr
                if i == n_s - 1:
                    k = b % 4
                    c3 = mcb[:, k, 0:3 * H].rearrange("p (c h) -> p c h", c=3)
                    mn = mneg[:, b % 4, 0:H]
                    t1 = dve(lambda e: e.tensor_copy(c3[:, 0, :], mn), tr, mcb_free[k])
                    t1 = dve(lambda e: e.tensor_tensor(mres[:, 0:H], mn, c3[:, 0, :], ALU.subtract), t1, mres_free[0])
                    mn_free[b % 4] = t1
                    t1 = dve(lambda e: e.tensor_copy(c3[:, 1, :], mres[:, 0:H]), t1)
                    t1 = dve(lambda e: e.tensor_tensor(c3[:, 2, :], mres[:, 0:H], c3[:, 1, :], ALU.subtract), t1)
                    mres_free[0] = t1
                    chain[b] = t1
                    soon(lambda: m_turn(b), {2: 5, 4: 4 if causal else 3, 8: 6}[n_st], True)

            def m_turn(b):
                p, b2 = divmod(b, 2)
                k = b % 4
                mb = misc()
                o = PSB[mb].bitcast(BF16)[0:3 * H, 0:128]
                t = pe(lambda e: e.transpose(o, mcb[:, k, 0:3 * H], identb[:, :]), chain[b], t_idb, bank_free[mb], inc=True)
                mcb_free[k] = t
                t = act(lambda e: e.activation(mT[0:3 * H, k, :], o, ACT.Copy), t, mT_free[k])
                bank_free[mb] = t
                dst = place(Q8, at_(p), H)[96:99, :].rearrange("c (h t) -> c h t", h=H)[:, :, 128 * b2:128 * b2 + 128]
                for c in range(3):
                    t2 = Q.dma(f"m{k}", dst[c:c + 1], mT[c * H:c * H + H, k, :], (t, *prepped[p]["qk"]))
                mT_free[k] = t2
                ready_m[b] = t2

            def st_unit(b, i):
                p, b2 = divmod(b, 2)
                G, kb = divmod(i, nkb)
                n = nst[0]
                nst[0] += 1
                bk = 2 + n % 2
                w = [bank_free[bk], ready_m[b]]
                for hh in range(4):
                    h = 4 * G + hh
                    o = PSB[bk][:, 128 * hh:128 * hh + 128]
                    t = pe(lambda e, o=o, h=h, hh=hh: e.matmul(o, head(tiles[kb], p, b2, h, 99), head(Q8, p, b2, h, 99),
                                                              start=(hh == 0), stop=not causal, skip_group_check=True),
                           *w, inc=(hh == 3 and not causal))
                    w = []
                if causal:
                    t = pe(lambda e: e.matmul(PSB[bk].rearrange("p (h k) -> p h k", h=4), identb[:, :],
                                              cnegb[:, 1, :].unsqueeze(1).broadcast_to([128, 4, 128]), start=False, stop=True,
                                              skip_group_check=True), t_cb, inc=True)
                bz = 0.0 if bias_i is None else bias[:, bias_i, b:b + 1]
                slot = n % 8
                te = act(lambda e: e.activation(HB[:, slot, :], PSB[bk], ACT.Exp, bias=bz), t, pt_free[slot], t_bias)
                bank_free[bk] = te
                if b2 == 1 and i == n_st - 1:
                    st_done.add(p)
                    q8_free[at_(p)] = t
                    if ctx_kb:
                        k8_free[at_(p)] = t
                    if self_kb:
                        ks_free[at_(p)] = t
                return (b, G, kb, slot, te)

            got = {}

            def pv_unit(u):
                b, G, kb, slot, te = u
                got.setdefault((b, G), []).append((kb, slot, te))
                if kb != nkb - 1:
                    return
                p, b2 = divmod(b, 2)
                k = b % 2
                bk = 4
                blocks = got.pop((b, G))
                w = [x[2] for x in blocks] + [*prepped[p]["v"]]
                if G == 0:
                    w.append(bank_free[bk])
                for kb_, slot_, _ in blocks:
                    for hh in range(4):
                        h = 4 * G + hh
                        o = PSB[bk][32 * hh:32 * hh + vd + 1, 128 * G:128 * G + 128]
                        t = pe(lambda e, o=o, h=h, hh=hh, kb_=kb_, slot_=slot_: e.matmul(
                            o, vh(vts[kb_], p, b2)[:, h, :], HB[:, slot_, 128 * hh:128 * hh + 128],
                            start=(kb_ == 0), stop=(kb_ == nkb - 1), skip_group_check=True), *w, inc=(hh == 3))
                        w = []
                    pt_free[slot_] = t
                if G == H // 4 - 1:
                    if b2 == 1:
                        pv_done.add(p)
                        if ctx_kb:
                            va_free[p % 4] = t
                        if self_kb:
                            vs_free[p % 4] = t
                    te = act(lambda e: e.activation(OE[:, k, 0:32 * H], PSB[bk][:, 0:32 * H], ACT.Copy), t, oe_free[k])
                    bank_free[bk] = te
                    soon(lambda: pv_turn(b, te), 4 if H == 16 else 3, True)

            def pv_turn(b, te):
                k = b % 2
                mb = misc()
                for G in range(H // 4):
                    t = pe(lambda e, G=G: e.transpose(PSB[mb][:, 128 * G:128 * G + 128], OE[:, k, 128 * G:128 * G + 128], C("ident")),
                           te, bank_free[mb], inc=(G == H // 4 - 1))
                oe_free[k] = t
                o3 = PSB[mb][:, 0:32 * H].rearrange("p (h d) -> p h d", h=H)
                t = dve(lambda e: e.reciprocal(rec[:, k, 0:H], o3[:, :, vd]), t, rec_free[k])
                t = dve(lambda e: e.tensor_tensor(otmp[:, k, 0:H * vd].rearrange("p (h d) -> p h d", h=H), o3[:, :, 0:vd],
                                                  rec[:, k, 0:H].unsqueeze(2).broadcast_to([128, H, vd]), ALU.mult), t)
                bank_free[mb] = t
                finish(b, k, t)

            coming = {}
            pv_done, st_done = set(), set()

            def stage(p):
                if len(coming.get(p, ())) > 1:
                    if coming[p][0].__name__ == "vv" and p >= 4 and p - 4 not in pv_done:
                        soon(lambda: stage(p), 1)
                    else:
                        coming[p].pop(0)()

            def copy(p):
                if p >= 4 and p - 4 not in pv_done:
                    soon(lambda: copy(p), 1)
                else:
                    prepped[p]["v"].append(prepped[p].pop("copy")())

            def loaded(p):
                for f in coming[p][:-1]:
                    f()
                prepped[p] = coming.pop(p)[-1]()
                if "copy" in prepped[p]:
                    soon(lambda: copy(p), n_s + n_st)

            load_step = {p: max(2 * (p - R) + 1 + LAG, 2 * p - 4) for p in range(NP)}
            ahead = [p for p in range(NP) if load_step[p] < 0]
            gap = 3 if n_st == 8 or n_st == 4 and not causal else 2

            def begin():
                def go(p, i):
                    fs = coming[p]
                    what = fs[i].__name__
                    if not may(p, what):
                        soon(lambda: go(p, i), 1)
                    elif i + 1 < len(fs):
                        fs[i]()
                        soon(lambda: go(p, i + 1), {"n1": 4, "n2": 4, "n3": 5, "parts": 4}.get(what, gap))
                    else:
                        prepped[p] = coming.pop(p)[-1]()
                        if "copy" in prepped[p]:
                            soon(lambda: copy(p), 6)
                for p in ahead:
                    coming[p] = prep(p, at_)
                    soon(lambda p=p: go(p, 0), 1 + 8 * p)

            def run(hook=lambda t: None):
                while any(p not in prepped for p in ahead):
                    slot_no[0] += 1
                    run_side(1)
                bank_free[4] = dve(lambda e: e.memset(PSB[4], 0.0), bank_free[4])
                misc_turn[1] = 3
                for tstep in range(B + LAG):
                    hook(tstep)
                    tasks = []
                    if tstep < B:
                        tasks.append([lambda i=i: s_unit(tstep, i) for i in range(n_s)])
                    if tstep >= LAG:
                        tasks.append([lambda i=i: ("st", st_unit(tstep - LAG, i)) for i in range(n_st)])
                    order = sorted(((i + 0.5) / len(g), gi, f) for gi, g in enumerate(tasks) for i, f in enumerate(g))
                    for pp in range(NP):
                        if pp not in ahead and max(0, load_step[pp] - {2: 5, 4: 3 if causal else 2, 8: 2}[n_st]) == tstep:
                            coming[pp] = prep(pp, at_)
                            n = 1
                            for f in coming[pp][:-1]:
                                soon(lambda pp=pp: stage(pp), n)
                                n += {"n1": 4, "n2": 4, "n3": 5, "parts": 4}.get(f.__name__, gap)
                    for _, _, f in order:
                        r = f()
                        if r is not None:
                            pv_wait.append(r[1])
                            if len(pv_wait) > PVLAG:
                                pv_unit(pv_wait.pop(0))
                        slot_no[0] += 1
                        run_side(2)
                    for pp in range(NP):
                        if load_step[pp] == tstep:
                            loaded(pp)
                while pv_wait:
                    slot_no[0] += 4
                    run_side(4)
                    pv_unit(pv_wait.pop(0))
                while any(own_ for _, _, own_ in side):
                    slot_no[0] += 2
                    run_side(2)

            return begin, run, st_done, pv_done

        def now():
            return tuple((Q.sem[n], Q.count[n]) for n in ("pe", "dve", "act", "pool"))

        def load_v(p):
            k = p % 3
            return Q.dma(f"vr{k}", vraw[:, k, :].rearrange("p (b d) -> p b d", b=2),
                         io["ctx_2048"][2 * p:2 * p + 2, :, 128:256].rearrange("b t d -> t b d"), (vr_free[k],))

        def copy_v(p, H, dh, tv):
            k = p % 3
            dst = VA[:, p % 4, 0:2 * H * (dh + 1)].rearrange("p (n d) -> p n d", d=dh + 1)
            t = dve(lambda e: e.tensor_copy(dst[:, :, 0:dh], vraw[:, k, :].rearrange("p (n d) -> p n d", d=dh)), tv, va_free[p % 4])
            vr_free[k] = t
            return t

        def heads_out(a):
            return a.rearrange("p (h d) -> p h d", h=16)

        def heads_in(a):
            return a.rearrange("p (d h) -> p h d", h=16)

        def prep_ctx(sc, dh, first):
            H = 128 // dh

            def prep(p, at_):
                k = p % 2
                got = {}

                def n1():
                    got["s"] = norm_in(X[:, 2 * p:2 * p + 2, :], 2, (x_tok[2 * p], x_tok[2 * p + 1]))

                def n2():
                    got["n"] = norm_out(got["s"], lambda j: heads_in(xn[:, k, 128 * j:128 * j + 128]), (xn_free[k],), view=heads_out)

                def qT():
                    got["T"] = turned(k, 2, misc(), got["n"], scale=float(np.float32(dh ** -0.5)))

                def parts():
                    xT_free[k], got["q"] = split_in(xT[:, k, 0:256], got["T"])

                def keep():
                    got["q"] = store(got["q"], (("q", 0, 128, sc),), p)
                    if first:
                        k_store(p)

                def loads():
                    tk = load_rows(K8, "k8", sc_k, at_(p), dh, H, p, (k_in[p], k8_free[at_(p)]))
                    tq = load_rows(Q8, "q8", sc, at_(p), dh, H, p, (got["q"], q8_free[at_(p)]))
                    tv = load_v(p)
                    return {"qk": [tq, tk], "v": [], "copy": lambda: copy_v(p, H, dh, tv)}
                return [n1, n2, *([lambda: k_split(p)] if first else []), qT, parts, keep, loads]
            return prep

        def finish_add(gi):
            def finish(b, k, t):
                t = dve(lambda e: e.scalar_tensor_tensor(out=X[:, b, :], in0=otmp[:, k, :], scalar=tg[:, gi:gi + 1], in1=X[:, b, :],
                                                         op0=ALU.mult, op1=ALU.add), t, t_tg, x_tok[b])
                x_tok[b] = t
                rec_free[k] = t
            return finish

        ring = [0, 8]

        def bank():
            ring[0] += 1
            return ring[0] % ring[1]

        def group_T(g, src, waits, rms=False, scale=None, bcol=None, dst=None, dst_free=None):
            k = g % 2
            t = norm(src, 4, (*waits, xn_free[k]), lambda j: xn[:, k, 128 * j:128 * j + 128], rms=rms)
            return turned(k, 4, bank(), t, scale=scale, bcol=bcol, dst=dst, dst_free=dst_free)

        def xg(g):
            return [x_tok[4 * g + j] for j in range(4)]

        soon(load_weights, 12)
        begin0, run0, *_ = attention(16, 8, 8, [0], [], prep_ctx(sc_q[0], 8, True), finish_add(0), bias_i=0)
        begin0()

        def clear_ks():
            for p in (0, 1):
                ks_free[p] = clear(pool, KS, p, True)
            vs_free[:] = [pool(lambda e: e.memset(VS[:, :, :], 1.0))] * 4

        run0(lambda t: clear_ks() if t == 8 else None)

        def y_turn(src, t, free, g):
            bt = bank()
            for j in range(4):
                t = pe(lambda e, j=j: e.transpose(PSB[bt][:, 128 * j:128 * j + 128], src[:, 128 * j:128 * j + 128], C("ident")), t,
                       bank_free[bt], inc=(j == 3))
            free[g % 2] = t
            return bt, PSB[bt].rearrange("p (b d) -> p b d", b=4), t

        def v_out(bank, p, H, dh, t):
            dst = VS[:, p % 4, 0:2 * H * (dh + 1)].rearrange("p (n d) -> p n d", d=dh + 1)
            t = act(lambda e: e.activation(dst[:, :, 0:dh], PSB[bank][:, 0:2 * H * dh].rearrange("p (n d) -> p n d", d=dh), ACT.Copy),
                    t, vs_free[p % 4])
            bank_free[bank] = t
            return t

        oT_free = [None] * 2

        def prep_x1(p, at_):
            k = p % 2
            got = {}

            def n1():
                got["s"] = norm_in(X[:, 2 * p:2 * p + 2, :], 2, (x_tok[2 * p], x_tok[2 * p + 1]))

            def n2():
                got["n"] = norm_out(got["s"], lambda j: xn[:, k, 128 * j:128 * j + 128], (xn_free[k],))

            def n3():
                got["T"] = turned(k, 2, misc(), got["n"])

            def qk():
                mb = misc()
                w = wsm["w_qkvT"]
                pe(lambda e: e.matmul(PSB[mb][:, 0:256], w[:, 0:128], xT[:, k, 0:256], start=True, stop=True), got["T"], t_ws, bank_free[mb])
                t = pe(lambda e: e.matmul(PSB[mb][:, 256:512], w[:, 128:256], xT[:, k, 0:256], start=True, stop=True), inc=True)
                got["ta"] = act(lambda e: e.activation(sp32[:, 0, :], PSB[mb][:, 0:256], ACT.Copy, scale=float(np.float32(8 ** -0.5))), t, sp_free[0])
                got["tb"] = act(lambda e: e.activation(sp32[:, 1, :], PSB[mb][:, 256:512], ACT.Copy), t, sp_free[1])
                bank_free[mb] = got["tb"]

            def parts():
                sp_free[0], got["q"] = split_in(sp32[:, 0, :], got["ta"])
                sp_free[1], got["k"] = split_in(sp32[:, 1, :], got["tb"])

            def keep():
                got["q"] = store(got["q"], (("q", 0, 128, sc_q[1]),), p)

            def keep2():
                got["k"] = store(got["k"], (("k", 0, 128, sc_s),), p)

            def vv():
                mb = misc()
                for j in range(2):
                    t = pe(lambda e, j=j: e.matmul(PSB[mb][:, 128 * j:128 * j + 128], xT[:, k, 128 * j:128 * j + 128],
                                                   wsm["w_qkvT"][:, 256:384], start=True, stop=True), got["T"], bank_free[mb], inc=(j == 1))
                xT_free[k] = t
                got["v"] = v_out(mb, p, 16, 8, t)

            def loads():
                tk = load_rows(K8, "k8", sc_k, at_(p), 8, 16, p, (k_in[p], k8_free[at_(p)]))
                tq = load_rows(Q8, "q8", sc_q[1], at_(p), 8, 16, p, (got["q"], q8_free[at_(p)]))
                t2 = load_rows(KS, "ks", sc_s, at_(p), 8, 16, p, (got["k"], ks_free[at_(p)]))
                tv = load_v(p)
                return {"qk": [tq, tk, t2], "v": [got["v"]], "copy": lambda: copy_v(p, 16, 8, tv)}
            return [n1, n2, n3, qk, parts, vv, keep, keep2, loads]

        def finish_mm(n, wname, end):
            def finish(b, k, t):
                def turn():
                    mb = misc()
                    tp = pe(lambda e: e.transpose(PSB[mb][0:n, 0:128], otmp[:, k, 0:n], C("ident")), t, bank_free[mb], inc=True)
                    rec_free[k] = tp
                    ta = act(lambda e: e.activation(oT[0:n, k, :], PSB[mb][0:n, 0:128], ACT.Copy), tp, oT_free[k])
                    bank_free[mb] = ta

                    def mul():
                        mb = misc()
                        tm = pe(lambda e: e.matmul(PSB[mb][:, 0:128], oT[0:n, k, :], wsm[wname], start=True, stop=True), ta, t_ws,
                                bank_free[mb], inc=True)
                        oT_free[k] = tm
                        end(b, k, tm, mb)
                    soon(mul, 3, True)
                soon(turn, 4, True)
            return finish

        ptmp_free = [None] * 2
        rope_free = [None]

        def end_x1(b, k, t, mb):
            t = dve(lambda e: e.tensor_tensor(AT[:, 0, 128 * k:128 * k + 128], PSB[mb][:, 0:128], rows[:, 1, :], ALU.add), t, t_row1,
                    ptmp_free[k])
            bank_free[mb] = t
            t = dve(lambda e: e.scalar_tensor_tensor(out=X[:, b, :], in0=AT[:, 0, 128 * k:128 * k + 128], scalar=tg[:, 1:2], in1=X[:, b, :],
                                                     op0=ALU.mult, op1=ALU.add), t, x_tok[b], t_tg)
            x_tok[b] = ptmp_free[k] = t

        begin_x1, run_x1, st_x1, pv_x1 = attention(16, 8, 8, [0], [0], prep_x1, finish_mm(128, "w_projT", end_x1))

        def halves(hi, lo, raw, *w):
            t = dve(lambda e: e.tensor_copy(hi, raw), *w)
            return dve(lambda e: e.tensor_tensor(lo, raw, hi.bitcast(F32), ALU.subtract), t)

        def product(out, wh, wl, xh, xl, *w):
            pe(lambda e: e.matmul(out, wh, xh, start=True, stop=False), *w)
            pe(lambda e: e.matmul(out, wh, xl, start=False, stop=False))
            return pe(lambda e: e.matmul(out, wl, xh, start=False, stop=True), inc=True)

        def ffn0():
            t_s3 = dve(lambda e: e.tensor_scalar(col("w3_s"), col("w3_s"), tg[:, 4:5], None, ALU.mult), t_cols, t_tg)
            UF = U[:, :, :].rearrange("p b d -> p (b d)").rearrange("p (n t) -> p n t", t=512)
            UR = UFr[:, :].rearrange("p (n t) -> p n t", t=512)
            space = [HB[:, 0:4, :], UF[:, 0:4, :]]
            hB = HB[:, 4:8, :]
            h1 = QFr[:, 4096:6144], WBr[:, 1024:3072]
            first = [KFr[:, 5120:5632], KFr[:, 5632:6144], WBr[:, 5632:6144], OEr[:, 1, :]]
            rest = [HBr[:, 0:4, :], UR[:, 0:4, :]]
            first_free = None
            h2 = CFr[:, 4096:6144], WBr[:, 3072:5120]
            now0 = now()
            start_w = [tuple(pt_free), ()]
            ring[1], misc_turn[1] = 6, 2
            at_free = [None, None]
            hA_free, hB_free = [None, None], None
            xt, nt, hid, yt = {}, {}, {}, {}
            K2 = KS[:, 2, :].bitcast(F32).rearrange("p (n t) -> p n t", t=512)
            nf, tf = K2[:, 0, :], K2[:, 1, :]
            nf_free, tf_free = None, None

            def n_(g):
                nt[g] = norm(X[:, 4 * g:4 * g + 4, :], 4, (*xg(g), nf_free), lambda j: nf[:, 128 * j:128 * j + 128])

            def t_(g):
                nonlocal nf_free
                bt = bank()
                for j in range(4):
                    t = pe(lambda e, j=j: e.transpose(PSB[bt][:, 128 * j:128 * j + 128], nf[:, 128 * j:128 * j + 128], C("ident")), nt[g],
                           bank_free[bt], inc=(j == 3))
                nf_free = t
                xt[g] = bank_free[bt] = act(lambda e: e.activation(tf, PSB[bt], ACT.Copy), t, tf_free)

            def up(g):
                nonlocal tf_free
                k = g % 2
                hA = space[k]
                hid[g] = []
                for m in range(4):
                    ba, bb = bank(), bank()
                    ta = pe(lambda e, m=m, ba=ba: e.matmul(PSB[ba], wb["w1T"][:, 128 * m:128 * m + 128], tf, start=True, stop=True),
                            xt[g], bank_free[ba], *t_wb, inc=True)
                    tb = pe(lambda e, m=m, bb=bb: e.matmul(PSB[bb], wb["w2T"][:, 128 * m:128 * m + 128], tf, start=True, stop=True),
                            bank_free[bb], inc=True)
                    a = m % 2
                    t = act(lambda e, m=m, ba=ba, a=a: e.activation(AT[:, a, :], PSB[ba], ACT.Silu, scale=col("w1_s", m)), ta, at_free[a], t_cols)
                    bank_free[ba] = t
                    t = dve(lambda e, m=m, bb=bb, a=a: e.scalar_tensor_tensor(out=hA[:, m, :], in0=PSB[bb], scalar=col("w2_s", m), in1=AT[:, a, :],
                                                                             op0=ALU.mult, op1=ALU.mult), t, tb, hA_free[k], *start_w[k])
                    bank_free[bb] = at_free[a] = t
                    hid[g].append(halves(first[m], rest[k][:, m, :], hA[:, m, :], t, first_free, *now0))
                tf_free = tb

            def product4(ba, m, w, xh, xl, *waits):
                for c in range(4):
                    o = slice(512 * c + 128 * m, 512 * c + 128 * m + 128)
                    pe(lambda e, c=c, o=o: e.matmul(PSB[ba], w[0][:, o], xh(c), start=(c == 0), stop=False), waits[0][c], *waits[1:])
                    pe(lambda e, c=c, o=o: e.matmul(PSB[ba], w[0][:, o], xl(c), start=False, stop=False))
                    t = pe(lambda e, c=c, o=o: e.matmul(PSB[ba], w[1][:, o], xh(c), start=False, stop=(c == 3)), inc=(c == 3))
                return t

            def mix1(g):
                nonlocal hB_free, first_free
                k = g % 2
                done, hid[g] = hid[g], []
                for m in range(4):
                    ba = bank()
                    t = product4(ba, m, h1, lambda c: first[c], lambda c: rest[k][:, c, :], done, bank_free[ba], t_h1)
                    t = act(lambda e, m=m, ba=ba: e.activation(hB[:, m, :], PSB[ba], ACT.Gelu, scale=col("h1_s", m)), t, hB_free, *start_w[0])
                    bank_free[ba] = t
                    hid[g].append(halves(UR[:, 4 + m, :], HBr[:, 4 + m, :], hB[:, m, :], t, hB_free))
                    slot_no[0] += 4
                    run_side(1)
                hA_free[k] = first_free = (Q.sem["pe"], Q.count["pe"])

            def mix2(g):
                nonlocal hB_free
                k = g % 2
                done, hid[g] = hid[g], []
                for m in range(4):
                    ba = bank()
                    t = product4(ba, m, h2, lambda c: UR[:, 4 + c, :], lambda c: HBr[:, 4 + c, :], done, bank_free[ba], t_h2)
                    t = act(lambda e, m=m, ba=ba: e.activation(space[k][:, m, :], PSB[ba], ACT.Gelu, scale=col("h2_s", m)), t, hA_free[k],
                            *start_w[k])
                    bank_free[ba] = t
                    hid[g].append(t)
                    slot_no[0] += 4
                    run_side(1)
                hB_free = (Q.sem["pe"], Q.count["pe"])

            def down(g):
                k = g % 2
                hA = space[k]
                by = bank()
                for c in range(4):
                    t = pe(lambda e, c=c: e.matmul(PSB[by], wb["w3T"][:, 128 * c:128 * c + 128], hA[:, c, :], start=(c == 0), stop=(c == 3)),
                           hid[g][c], bank_free[by], inc=(c == 3))
                hA_free[k] = t
                t = act(lambda e: e.activation(OE[:, 0, :], PSB[by], ACT.Copy, scale=col("w3_s")), t, oe_free[0], t_s3)
                bank_free[by] = t
                yt[g] = t

            def add(g):
                bt, P4, t = y_turn(OE[:, 0, :], yt[g], oe_free, 0)
                t = dve(lambda e: e.tensor_tensor(X[:, 4 * g:4 * g + 4, :], X[:, 4 * g:4 * g + 4, :], P4, ALU.add), t, *xg(g))
                bank_free[bt] = t
                for j in range(4):
                    x_tok[4 * g + j] = t

            n_(0)
            t_(0)
            t_h1 = halves(QFr[:, 4096:6144], WBr[:, 1024:3072], wb["h1T"], *now0, *t_wb)
            n_(1)
            up(0)
            t_(1)
            t_h2 = halves(CFr[:, 4096:6144], WBr[:, 3072:5120], wb["h2T"], *now0, *t_wb)
            mix1(0)
            for g in range(NG):
                if g + 2 < NG:
                    n_(g + 2)
                if g + 1 < NG:
                    up(g + 1)
                if g:
                    add(g - 1)
                if g == 1 and stop >= 3:
                    begin_x1()
                mix2(g)
                if g + 2 < NG:
                    t_(g + 2)
                if g + 1 < NG:
                    mix1(g + 1)
                down(g)
            add(NG - 1)
            t = (Q.sem["pe"], Q.count["pe"])
            for i in range(8):
                pt_free[i] = t
            q8_free[2] = clear(pool, Q8, 2, False, t, (Q.sem["dve"], Q.count["dve"]))
            k8_free[2] = clear(pool, K8, 2, True, t, (Q.sem["dve"], Q.count["dve"]))
            ks_free[2] = clear(pool, KS, 2, True, t, (Q.sem["act"], Q.count["act"]))

        if stop >= 2:
            ffn0()
        pe_after_ffn0 = (Q.sem["pe"], Q.count["pe"])

        t_m = None

        def load_moe1(t):
            for name, at in (("m1", 0), ("m3", 2048), ("m2", 4096)):
                tt = Q.dma("wb2", WB[:, at:at + 2048], io[name], (t,))
            return tt

        def prep_f1(p, at_):
            k = p % 2
            got = {}

            def n1():
                got["s"] = norm_in(X[:, 2 * p:2 * p + 2, :], 2, (x_tok[2 * p], x_tok[2 * p + 1]))

            def n2():
                t = norm_out(got["s"], lambda j: U[:, 2 * p + j, :])
                u_tok[2 * p] = u_tok[2 * p + 1] = t
                got["s"] = norm_in(U[:, 2 * p:2 * p + 2, :], 2, (t,), rms=True)

            def n3():
                got["n"] = norm_out(got["s"], lambda j: xn[:, k, 128 * j:128 * j + 128], (xn_free[k],))

            def n4():
                got["T"] = turned(k, 2, misc(), got["n"], scale=col("g1"))

            def cc():
                mb = misc()
                t = pe(lambda e: e.matmul(PSB[mb][0:64, 0:256], wsm["w_down"], xT[:, k, 0:256], start=True, stop=True), got["T"], t_ws,
                       bank_free[mb], inc=True)
                xT_free[k] = t
                got["c"] = bank_free[mb] = act(lambda e: e.activation(sp32[0:64, k, :], PSB[mb][0:64, 0:256], ACT.Copy), t, sp_free[k])

            def qk():
                mb = misc()
                c = sp32[0:64, k, :]
                pe(lambda e: e.matmul(PSB[mb][:, 0:256], wsm["wqk"], c, start=True, stop=True), got["c"], bank_free[mb])
                t = pe(lambda e: e.matmul(PSB[mb][:, 256:512], wsm["wqk_sw"], c, start=True, stop=True), inc=True)
                P = PSB[mb].rearrange("p (a b t) -> p a b t", a=2, b=2)
                o = [AT[:, 1, 256 * i:256 * i + 256] for i in range(2)]
                o3 = [x.rearrange("p (b t) -> p b t", b=2) for x in o]
                t1 = dve(lambda e: e.tensor_tensor(o3[0], P[:, 0], C("cos").unsqueeze(1).broadcast_to([128, 2, 128]), ALU.mult), t, rope_free[0])
                t1 = dve(lambda e: e.tensor_tensor(o3[1], P[:, 1], C("sin").unsqueeze(1).broadcast_to([128, 2, 128]), ALU.mult), t)
                bank_free[mb] = t1
                t1 = dve(lambda e: e.tensor_tensor(o[0], o[0], o[1], ALU.add), t1)
                got["r"] = t1

            def parts():
                rope_free[0], got["q"] = split_in(AT[:, 1, 0:256], got["r"])

            def keep():
                got["q"] = store(got["q"], (("q", 0, 64, sc_f[0]), ("k", 64, 64, sc_f[1])), p)

            def vv():
                if p < 4:
                    vs_free[p] = pool(lambda e: e.memset(VS[:, p, :], 1.0), vs_free[p])
                mb = misc()
                for j in range(2):
                    t = pe(lambda e, j=j: e.matmul(PSB[mb][:, 64 * j:64 * j + 64], sp32[0:64, k, 128 * j:128 * j + 128], wsm["wv"],
                                                   start=True, stop=True), bank_free[mb], inc=(j == 1))
                sp_free[k] = t
                got["v"] = v_out(mb, p, 16, 4, t)

            def loads():
                if p < 3:
                    Q.dma(f"ks{at_(p)}", place(KS, at_(p), 16)[24:48, :].bitcast(F32), io["zero"], (ks_free[at_(p)],))
                tq = load_rows(Q8, "q8", sc_f[0], at_(p), 4, 16, p, (got["q"], q8_free[at_(p)]))
                tk = load_rows(KS, "ks", sc_f[1], at_(p), 4, 16, p, (got["q"], ks_free[at_(p)]))
                return {"qk": [tq, tk], "v": [got["v"]]}
            return [n1, n2, n3, n4, cc, qk, parts, vv, keep, loads]

        def end_f1(b, k, t, mb):
            t = dve(lambda e: e.tensor_tensor(U[:, b, :], PSB[mb][:, 0:128], U[:, b, :], ALU.add), t, u_tok[b])
            bank_free[mb] = u_tok[b] = t

        def set_ones(d, vt, fr):
            for q in range(4):
                fr[q] = pool(lambda e, q=q: e.memset(vt[:, q, :], 1.0), fr[q])

        small = sb("small", [128, 3, 32])
        gate_tok, tt_tok, tt_read = {}, {}, {}

        def chain(fns, gap):
            def go(i):
                fn, n = fns[i] if isinstance(fns[i], tuple) else (fns[i], gap)
                fn()
                if i + 1 < len(fns):
                    soon(lambda: go(i + 1), n)
            soon(lambda: go(0), 1)

        def front(g, dst, xf, big, rms, wname, scale, bcol, plus, w, layer_norm):
            got = {}
            bs = slice(4 * g, 4 * g + 4)
            u_in = lambda: [u_tok[4 * g + j] for j in range(4)]
            big = [a.rearrange("p (b i j) -> p b i j", b=4, i=8) for a in big]
            L, T, s0, s1 = LG[:, bs, :], GT[:, bs, :], small[:, 0, bs], small[:, 1, bs]
            bc = lambda x: x.unsqueeze(2).broadcast_to([128, 4, 8])

            def n0():
                got["s"] = norm_in(X[:, bs, :], 4, xg(g))

            def n1():
                if layer_norm:
                    t = norm_out(got["s"], lambda j: U[:, 4 * g + j, :])
                    for j in range(4):
                        u_tok[4 * g + j] = t
                got["s"] = norm_in(U[:, bs, :], 4, u_in(), rms=rms)

            def n2():
                got["n"] = norm_out(got["s"], lambda j: xf[:, 128 * j:128 * j + 128], (fr["xf"], *w))

            def n3():
                mb = misc()
                for j in range(4):
                    t = pe(lambda e, j=j: e.transpose(PSB[mb][:, 128 * j:128 * j + 128], xf[:, 128 * j:128 * j + 128], C("ident")), got["n"],
                           bank_free[mb], inc=(j == 3))
                fr["xf"] = t
                f, bz = (ACT.Copy, 0.0) if bcol is None else (ACT.Identity, bcol)
                tt_tok[g] = bank_free[mb] = act(lambda e: e.activation(dst[:, 512 * g:512 * g + 512], PSB[mb], f, bias=bz, scale=scale), t, *w)

            def n4():
                mb = misc()
                for j in range(4):
                    t = pe(lambda e, j=j: e.matmul(PSB[mb][:, 8 * j:8 * j + 8], dst[:, 512 * g + 128 * j:512 * g + 128 * j + 128], wsm[wname],
                                                   start=True, stop=True), tt_tok[g], t_ws, bank_free[mb], inc=(j == 3))
                tt_read[g] = t
                P = PSB[mb][:, 0:32].rearrange("p (b e) -> p b e", b=4)
                if plus is None:
                    t = dve(lambda e: e.tensor_copy(L, P), t, fr["gate"])
                else:
                    t = dve(lambda e: e.tensor_tensor(L, P, rows2[:, :].unsqueeze(1).broadcast_to([128, 4, 8]), ALU.add), t, t_rows2, fr["gate"])
                bank_free[mb] = t
                t = dve(lambda e: e.tensor_reduce(s0, L, AX.X, ALU.max), t)
                got["t"] = dve(lambda e: e.tensor_tensor(L, L, bc(s0), ALU.subtract), t)

            def n5():
                got["t"] = act(lambda e: e.activation(L, L, ACT.Exp), got["t"])

            def n6():
                t = dve(lambda e: e.tensor_reduce(s0, L, AX.X, ALU.add), got["t"])
                t = dve(lambda e: e.reciprocal(s1, s0), t)
                t = dve(lambda e: e.tensor_tensor(L, L, bc(s1), ALU.mult), t)
                pj = L.unsqueeze(2).broadcast_to([128, 4, 8, 8])
                pi = L.unsqueeze(3).broadcast_to([128, 4, 8, 8])
                low = C("low").rearrange("p (i j) -> p i j", i=8).unsqueeze(1).broadcast_to([128, 4, 8, 8])
                t = dve(lambda e: e.tensor_tensor(big[0], pj, pi, ALU.is_gt), t, *w)
                t = dve(lambda e: e.tensor_tensor(big[1], pj, pi, ALU.is_equal), t)
                t = dve(lambda e: e.tensor_tensor(big[1], big[1], low, ALU.mult), t)
                got["t"] = dve(lambda e: e.tensor_tensor(big[0], big[0], big[1], ALU.add), t)

            def n7():
                t = dve(lambda e: e.tensor_reduce(T, big[0], AX.X, ALU.add), got["t"])
                t = dve(lambda e: e.scalar_tensor_tensor(out=T, in0=T, scalar=1.5, in1=L, op0=ALU.is_lt, op1=ALU.mult), t)
                t = dve(lambda e: e.tensor_reduce(s0, T, AX.X, ALU.add), t)
                if plus:
                    t = dve(lambda e: e.tensor_scalar(s0, s0, plus, None, ALU.add), t)
                t = dve(lambda e: e.reciprocal(s1, s0), t)
                t = dve(lambda e: e.tensor_tensor(T, T, bc(s1), ALU.mult), t)
                t = dve(lambda e: e.tensor_copy(G3[:, bs, 0, :], T), t)
                r = gr[:, 4 * (g % 2):4 * (g % 2) + 4, :]
                t = dve(lambda e: e.tensor_tensor(r, T, G3[:, bs, 0, :], ALU.subtract), t)
                t = dve(lambda e: e.tensor_copy(G3[:, bs, 1, :], r), t)
                gate_tok[g] = dve(lambda e: e.tensor_tensor(G3[:, bs, 2, :], r, G3[:, bs, 1, :], ALU.subtract), t)

            return [*([(n0, 3)] if layer_norm else []), (n1, 4), (n2, 7), (n3, 4), (n4, 4), n5, n6, n7]

        fr = {"xf": None, "gate": None}
        G3 = sb("G3", [128, 32, 3, 8], BF16)
        gS = comp[0:24, 0:2, 0:512]
        YT = [None, None]
        gr = sb("gr", [128, 8, 8])
        gs_tok = {}
        gS_free = [None, None]
        yt_free = [None, None]
        tmp_free = [None, None]
        tmp_turn = [0]

        def gate_rows(g):
            k = g % 2
            bt = bank()
            for j in range(4):
                t = pe(lambda e, j=j: e.transpose(PSB[bt].bitcast(BF16)[0:24, 128 * j:128 * j + 128],
                                                  G3[:, 4 * g + j].rearrange("p c e -> p (c e)"), identb[:, :]), gate_tok[g], bank_free[bt], inc=(j == 3))
            gs_tok[g] = bank_free[bt] = act(lambda e: e.activation(gS[:, k, :], PSB[bt].bitcast(BF16)[0:24, 0:512], ACT.Copy), t, gS_free[k])

        def moe_back(g, ex, hid, w2, t_hid, hid_free, y_tok):
            k = g % 2
            by, bg = bank(), bank()
            n = len(hid)
            for c in range(n):
                t = pe(lambda e, c=c: e.matmul(PSB[by], w2(ex, c), hid[c], start=(c == 0), stop=(c == n - 1)), t_hid[c], bank_free[by],
                       inc=(c == n - 1))
            hid_free(t)
            tg_ = pe(lambda e: e.matmul(PSB[bg], sel8b[:, ex:ex + 1].broadcast_to([24, 128]), gS[:, k, :], start=True, stop=True),
                     gs_tok[g], bank_free[bg], t_cb, inc=True)
            if ex == 7:
                gS_free[k] = tg_
            i = tmp_turn[0] % 2
            tmp_turn[0] += 1
            ta = act(lambda e: e.activation(OE[:, i, :], PSB[bg], ACT.Copy), tg_, tmp_free[i])
            bank_free[bg] = ta
            yt = YT[k]
            if y_tok is None:
                t = dve(lambda e: e.tensor_tensor(yt, PSB[by], OE[:, i, :], ALU.mult), t, ta, yt_free[k])
                bank_free[by] = tmp_free[i] = t
                return t
            t = dve(lambda e: e.tensor_tensor(OE[:, i, :], PSB[by], OE[:, i, :], ALU.mult), t, ta)
            bank_free[by] = t
            t = pool(lambda e: e.tensor_tensor(yt, yt, OE[:, i, :], ALU.add), t, y_tok)
            tmp_free[i] = t
            return t

        def moe_end(g, gi, t):
            b = 4 * g
            bt, P4, t = y_turn(YT[g % 2], t, yt_free, g)
            t = dve(lambda e: e.tensor_tensor(U[:, b:b + 4, :], P4, U[:, b:b + 4, :], ALU.add), t, *[u_tok[b + j] for j in range(4)])
            bank_free[bt] = t
            t = dve(lambda e: e.scalar_tensor_tensor(out=X[:, b:b + 4, :], in0=U[:, b:b + 4, :], scalar=tg[:, gi:gi + 1], in1=X[:, b:b + 4, :],
                                                     op0=ALU.mult, op1=ALU.add), t, t_tg, *xg(g))
            for j in range(4):
                x_tok[b + j] = u_tok[b + j] = t

        def tick():
            slot_no[0] += 1
            run_side(1)

        def moe(gi, up, w2, init, yts, each=lambda n: None, done=lambda g: None):
            YT[:] = yts
            for i in range(2):
                yt_free[i] = tmp_free[i] = now()
                gS_free[i] = (*now(), *comp_free[0:2])
            ring[1], misc_turn[1] = (6, 2) if gi == 5 else (5, 3)
            gate_rows(0)
            prev, end = None, None
            for n in range(8 * NG + 1):
                g, ex = divmod(n, 8)
                each(n)
                if n < 8 * NG:
                    cur = (g, ex, *up(g, ex))
                if end and (n % 8 == 2 or n == 8 * NG):
                    moe_end(end[0], gi, end[1])
                    done(end[0])
                    end = None
                if prev:
                    pg, pex, hid, th, freed = prev
                    if pex == 0:
                        y = init(pg) if init else None
                    y = moe_back(pg, pex, hid, w2, th, freed, y)
                    if pex == 7:
                        end = (pg, y)
                tick()
                tick()
                if n % 8 == 4 and g + 1 < NG:
                    gate_rows(g + 1)
                prev = cur
            moe_end(end[0], gi, end[1])
            done(end[0])

        at_free = [None, None]
        chunk_free = [None] * 8

        def front1(g, xf, big):
            chain(front(g, TT, xf, big, True, "router_w", col("g2"), None, None, w_f, False), 2)

        def front_f1(b):
            if b in (3, 7):
                front1(b // 4, vraw[:, 0:2, :].rearrange("p a b -> p (a b)"), [r32[:, 1, :], vraw[:, 2, :]])

        begin_f1, run_f1, *_ = attention(16, 4, 4, [], [0], prep_f1, finish_mm(64, "w_up", lambda *a: (end_f1(*a), front_f1(a[0]))), causal=True,
                                         base=1, may=lambda p, what: 13 + p in st_x1 if what == "loads" else what != "vv" or 12 + p in pv_x1)
        if stop >= 3:
            run_x1(lambda t: begin_f1() if stop >= 4 and t == 28 else None)

        rows2 = sb("rows2", [128, 8])
        b2 = sb("b2", [8, 128])
        KF = KS[:, :, :].rearrange("p a b -> p (a b)").bitcast(F32)
        QF = Q8[:, :, :].rearrange("p a b -> p (a b)").bitcast(F32)
        CF = K8[:, :, :].rearrange("p a b -> p (a b)").bitcast(F32)
        W2, T2 = KF[:, 0:4096], WB[:, 0:4096]
        t_w1 = []

        def finish2(b, k, t):
            finish_add(2)(b, k, t)
            if b in (3, 7):
                front2(b // 4, AT[:, 0, :], [AT[:, 1, 0:256], AT[:, 1, 256:512]])

        def front2(g, xf, big):
            chain(front(g, T2, xf, big, False, "WgT", col("gamma"), col("beta"), 1e-8, w2, True), 2)

        begin2, run2, *_ = attention(8, 16, 16, [0], [], prep_ctx(sc_q[3], 16, False), finish2, bias_i=1, base=4)

        def load2():
            nonlocal t_rows2, t_b2
            t_pe = (Q.sem["pe"], Q.count["pe"])
            t_rows2 = Q.dma("rows2", rows2[:, :], io["bg"].rearrange("(a n) -> a n", a=1).broadcast_to([128, 8]))
            t_b2 = Q.dma("b2", b2[:, :], io["b2"])
            q8_free[:] = [t_pe] * 6
            k8_free[:] = [t_pe] * 6
            set_ones(16, VA, va_free)
            vr_free[:] = [now()] * 3
            comp_turn[0] += -comp_turn[0] % 4 + 2
            begin2()

        t_ks = t_rows2 = t_b2 = None
        if stop >= 4:
            t_m = load_moe1((Q.sem["pe"], pe_after_ffn0[1]))
            w_f = now()
            run_f1()
            chunk_free = list(pt_free)
            at_free = [now(), now()]

            used1, half1 = {}, {}

            def up1(g, ex):
                hid, th = [], []
                for c in range(2):
                    slot = (2 * ex + c) % 8
                    ba, bb = bank(), bank()
                    o = 256 * ex + 128 * c
                    x = TT[:, 512 * g:512 * g + 512]
                    if g == 0:
                        ta = pe(lambda e, o=o, ba=ba: e.matmul(PSB[ba], WB[:, o:o + 128], x, start=True, stop=True), t_m, tt_tok[g],
                                bank_free[ba], inc=True)
                        tb = pe(lambda e, o=o, bb=bb: e.matmul(PSB[bb], WB[:, 2048 + o:2048 + o + 128], x, start=True, stop=True),
                                bank_free[bb], inc=True)
                        used1[ex] = tb
                    else:
                        xh, xl, o2 = KFr[:, 5120 + 512 * (g % 2):5632 + 512 * (g % 2)], CFr[:, 512 * g:512 * g + 512], 2048 + o
                        ta = product(PSB[ba], KFr[:, o:o + 128], WBr[:, o:o + 128], xh, xl, half1["x", g], half1["w", ex], bank_free[ba])
                        tb = product(PSB[bb], KFr[:, o2:o2 + 128], WBr[:, o2:o2 + 128], xh, xl, bank_free[bb])
                        if ex == 7 and c == 1:
                            half1["free", g % 2] = tb
                    t = act(lambda e, ba=ba, c=c: e.activation(AT[:, c, :], PSB[ba], ACT.Silu), ta, at_free[c])
                    bank_free[ba] = t
                    t = dve(lambda e, bb=bb, c=c, slot=slot: e.tensor_tensor(HB[:, slot, :], PSB[bb], AT[:, c, :], ALU.mult), t, tb,
                            chunk_free[slot])
                    bank_free[bb] = at_free[c] = t
                    hid.append(HB[:, slot, :])
                    th.append(t)
                    tick()

                def freed(tok):
                    for c in range(2):
                        chunk_free[(2 * ex + c) % 8] = tok
                return hid, th, freed

            VF = VS[:, :, :].rearrange("p a b -> p (a b)")
            fr["xf"] = fr["gate"] = (now(), *[x for x in (fr["xf"], fr["gate"]) if x])

            def each1(n):
                if 1 <= n <= 8:
                    for o in (256 * (n - 1), 2048 + 256 * (n - 1)):
                        half1["w", n - 1] = halves(KFr[:, o:o + 256], WBr[:, o:o + 256], WB[:, o:o + 256], used1[n - 1])
                if n % 8 == 5 and n // 8 + 1 < NG:
                    g = n // 8 + 1
                    half1["x", g] = halves(KFr[:, 5120 + 512 * (g % 2):5632 + 512 * (g % 2)], CFr[:, 512 * g:512 * g + 512],
                                           TT[:, 512 * g:512 * g + 512], tt_tok[g], tt_read[g], half1.get(("free", g % 2)))
                if n % 8 == 0 and n // 8 + 2 < NG:
                    front1(n // 8 + 2, KF[:, 4096:4608], [KF[:, 4608:4864], KF[:, 4864:5120]])

            moe(5, up1, lambda x, c: WB[:, 4096 + 256 * x + 128 * c:4096 + 256 * x + 128 * c + 128], None, [VF[:, 0:512], VF[:, 512:1024]],
                each=each1, done=lambda g: load2() if g == 0 and stop >= 5 else None)

        if stop >= 5:
            t_ks = Q.dma("w2", W2, io["W2T"], now())
            t_w1.append(Q.dma("w1a", KF[:, 4096:6144], io["W1T"][:, 0:2048], now()))
            k8_free[0:4] = [pool(lambda e: e.memset(K8[96:128, :, :].rearrange("p a b -> p (a b)")[:, 0:8192], 1.0), (Q.sem["pe"], Q.count["pe"]))] * 4
            comp_free[0:2] = [now()] * 2
            w2 = now()
            fr["xf"] = fr["gate"] = w2
            run2()

        if stop >= 6:
            t_w1.append(Q.dma("w1b", QF[:, 0:2048], io["W1T"][:, 2048:4096], ((Q.sem["pe"], Q.count["pe"]),)))

            def W1(o, kf=KF, qf=QF):
                return kf[:, 4096 + o:4096 + o + 128] if o < 2048 else qf[:, o - 2048:o - 2048 + 128]

            chunk_free = list(pt_free)
            gT = sp32[0:8, :, :].rearrange("p a b -> p (a b)")
            gT_free = [now()]

            gT_tok = {}

            def gates_T(g):
                bt = bank()
                for j in range(4):
                    t = pe(lambda e, j=j: e.transpose(PSB[bt][0:8, 128 * j:128 * j + 128], GT[:, 4 * g + j, :], C("ident")), gate_tok[g],
                           bank_free[bt], inc=(j == 3))
                t = act(lambda e: e.activation(gT, PSB[bt][0:8, :], ACT.Copy), t, gT_free[0])
                bank_free[bt] = gT_tok[g] = t

            def init2(g):
                by = bank()
                t = pe(lambda e: e.matmul(PSB[by], b2[:, :], gT, start=True, stop=True), gT_tok[g], t_b2, bank_free[by], inc=True)
                gT_free[0] = t
                yt = YT[g % 2]
                t = act(lambda e: e.activation(yt, PSB[by], ACT.Copy), t, yt_free[g % 2])
                bank_free[by] = t
                return t

            used2, half2 = {}, {}

            def hi2(ex):
                if ex < 4:
                    return QFr[:, 4096 + 512 * ex:4608 + 512 * ex]
                return CFr[:, 512 * (ex - 4):512 * (ex - 3)] if ex < 7 else CFr[:, 5376:5888]

            def halves2(ex):
                at = slice(4096 + 512 * ex, 4608 + 512 * ex) if ex < 4 else slice(512 * (ex - 4), 512 * (ex - 3))
                lo, raw = (KFr[:, at], KF[:, at]) if ex < 4 else (QFr[:, at], QF[:, at])
                half2["w", ex] = halves(hi2(ex), lo, raw, used2[ex], half2["now"], L3[3]["wt"] if 4 <= ex < 7 else None)

            def up2(g, ex):
                hid, th = [], []
                for c in range(4):
                    slot = (4 * ex + c) % 8
                    ba = bank()
                    o = 512 * ex + 128 * c
                    x = T2[:, 512 * g:512 * g + 512]
                    if g == 0 or stop < 7:
                        ta = pe(lambda e, o=o, ba=ba: e.matmul(PSB[ba], W1(o), x, start=True, stop=True), t_w1[ex // 4], tt_tok[g],
                                bank_free[ba], inc=True)
                        used2[ex] = ta
                    else:
                        ta = product(PSB[ba], hi2(ex)[:, 128 * c:128 * c + 128], W1(o, KFr, QFr), xnr[:, g % 2, :], WBr[:, 512 * g:512 * g + 512], half2["x", g], half2["w", ex],
                                     bank_free[ba])
                        if ex == 7 and c == 3:
                            half2["free", g % 2] = ta
                    t = act(lambda e, ba=ba, slot=slot, i=4 * ex + c: e.activation(HB[:, slot, :], PSB[ba], ACT.Gelu, bias=col("b1", i)),
                            ta, chunk_free[slot], t_cols)
                    bank_free[ba] = t
                    hid.append(HB[:, slot, :])
                    th.append(t)
                    tick()

                def freed(tok):
                    for c in range(4):
                        chunk_free[(4 * ex + c) % 8] = tok
                return hid, th, freed

            Q.put("pe", lambda e: None, (t_ks,), False)

        MAGIC = 12582912.0
        bidx = sb("bidx", [128, 32])
        bm = sb("bm", [128, 32], BF16)
        onesb = sb("onesb", [128, 1], BF16)
        magic = sb("magic", [128, 1])
        sc = sb("sc", [128, 2, 4, 8])

        def layer3(w):
            W3 = CF[:, 0:1536].rearrange("p (n w) -> p n w", n=3)
            wt = CF[:, 1536:2304].bitcast(BF16).rearrange("p (n w) -> p n w", n=3)
            CX = CF[:, 2304:3328].rearrange("p (b d) -> p b d", b=4)
            UP, DD, GM = (CF[:, 3328 + 512 * i:3840 + 512 * i] for i in range(3))
            RR = CF[:, 4864:5376]
            hT, xf = QF[:, 2048:2560], QF[:, 2560:3072]
            qn = QF[:, 3072:3328].bitcast(BF16)
            qT = QF[:, 3328:3840].bitcast(BF16).rearrange("p (k w) -> p k w", k=2)
            H = [WB[:, 4096 + 512 * i:4608 + 512 * i] for i in range(4)]
            q2 = VA[:, :, :].rearrange("p a b -> p (a b)").bitcast(BF16)[:, 0:2048].rearrange("p (k w) -> p k w", k=4)
            q2T = VS[:, :, :].rearrange("p a b -> p (a b)").bitcast(BF16)[:, 0:2048].rearrange("p (k w) -> p k w", k=4)
            EB = r32[:, :, :].rearrange("p a b -> p (a b)").bitcast(BF16)[:, 0:512].rearrange("p (k t) -> p k t", k=4)
            ws = small[:, 2, :]
            free = {n: w for n in ("cx", "up", "dd", "gm", "rr", "hT", "xf", "qn", "qT0", "qT1", "sil0", "sil1", "eb", "sc0", "sc1")}
            h_free, q2_free, q2T_free = [w] * 4, [w] * 4, [w] * 4
            tok = {}

            def b4(a):
                return a.rearrange("p (b d) -> p b d", b=4)

            def w0():
                for i, name in enumerate(("qg", "qu", "qd")):
                    tok["w"] = Q.dma("wb3", W3[:, i, :], io[name], (w,))
                tok["row0"] = Q.dma("row0", rows[:, 0, :], row_bc("b_in", 0), (w,))
                tok["row1"] = Q.dma("row1", rows[:, 1, :], row_bc("g_init", 1), (w,))
                tok["magic"] = dve(lambda e: e.memset(magic[:, :], -MAGIC))
                tok["ones"] = dve(lambda e: e.memset(onesb[:, :], 1.0))

            def m0():
                mb = misc()
                t = dve(lambda e: e.tensor_copy(btmp[:, :], ints[:, 2, :]), t_i)
                tp = pe(lambda e: e.matmul(PSB[mb][:, 0:32], C("tri"), btmp[:, :], start=True, stop=True), t, bank_free[mb], inc=True)
                t = dve(lambda e: e.tensor_scalar(bidx[:, :], PSB[mb][:, 0:32], -1.0, None, ALU.add), tp)
                bank_free[mb] = t
                t = dve(lambda e: e.tensor_scalar(btmp[:, :], bidx[:, :], 0.0, 128.0, ALU.is_lt, ALU.mult), t)
                tok["bidx"] = dve(lambda e: e.tensor_tensor(bidx[:, :], bidx[:, :], btmp[:, :], ALU.add), t)

            def w1():
                tok["w"] = dve(lambda e: e.tensor_reduce(ws[:, 0:3], W3, AX.X, ALU.add, apply_absolute_value=True), tok["w"])
                tok["row1"] = dve(lambda e: e.tensor_scalar(rows[:, 1, :], rows[:, 1, :], cu, None, ALU.mult), tok["row1"])

            def w2():
                mb = misc()
                tp = pe(lambda e: e.matmul(PSB[mb][:, 0:3], C("ones"), ws[:, 0:3], start=True, stop=True), tok["w"], bank_free[mb], inc=True)
                t = dve(lambda e: e.tensor_scalar(ws[:, 4:7], PSB[mb][:, 0:3], 1.0 / 65536.0, 1e-5, ALU.mult, ALU.max), tp)
                bank_free[mb] = t
                t = dve(lambda e: e.reciprocal(ws[:, 8:11], ws[:, 4:7]), t)
                tok["ws"] = dve(lambda e: e.reciprocal(ws[:, 12:15], ws[:, 8:11]), t)

            def w3(i):
                t = dve(lambda e: e.tensor_scalar(W3[:, i, :], W3[:, i, :], ws[:, 8 + i:9 + i], MAGIC, ALU.mult, ALU.add), tok["ws"])
                t = dve(lambda e: e.tensor_scalar(W3[:, i, :], W3[:, i, :], -MAGIC, 1.0, ALU.add, ALU.min), t)
                tok["wt"] = dve(lambda e: e.tensor_scalar(wt[:, i, :], W3[:, i, :], -1.0, None, ALU.max), t)

            setup = [w0, m0, w1, w2, lambda: w3(0), lambda: w3(1), lambda: w3(2)]

            def context(g):
                got = {}

                def c0():
                    got["c"] = Q.dma("cx", CX, io["ctx_2048"][4 * g:4 * g + 4].rearrange("b t d -> t b d"), (free["cx"],))

                def c1():
                    for j in range(4):
                        t = dve(lambda e, j=j: e.tensor_scalar(EB[:, j, :], C("iota_t"), bidx[:, 4 * g + j:4 * g + j + 1], None, ALU.is_equal),
                                tok["bidx"], free["eb"])
                    got["e"] = t

                def c2():
                    mb = misc()
                    for j in range(4):
                        t = pe(lambda e, j=j: e.matmul(PSB[mb][:, j:j + 1], EB[:, j, :], onesb[:, :], start=True, stop=True), got["e"],
                               tok["ones"], bank_free[mb], inc=(j == 3))
                    free["eb"] = t
                    got["bm"] = bank_free[mb] = dve(lambda e: e.tensor_scalar(bm[:, 4 * g:4 * g + 4], PSB[mb][:, 0:4], 1.0, None, ALU.min), t)

                def c3():
                    got["s"] = norm_in(CX, 4, (got["c"],), rms=True)

                def c4():
                    mb = misc()
                    for j in range(4):
                        t = pe(lambda e, j=j: e.matmul(PSB[mb][:, 128 * j:128 * j + 128], bm[:, 4 * g + j:4 * g + j + 1].broadcast_to([128, 128]),
                                                       trib[:, :], start=True, stop=True), got["bm"], t_cb, bank_free[mb], inc=(j == 3))
                    t = dve(lambda e: e.tensor_scalar(GM, PSB[mb], -1.0, 0.0, ALU.add, ALU.max), t, free["gm"])
                    bank_free[mb] = t
                    got["gm"] = dve(lambda e: e.tensor_scalar(GM, GM, 127.0, C("iota_p"), ALU.min, ALU.is_equal), t)

                def c5():
                    t = norm_out(got["s"], lambda j: UP[:, 128 * j:128 * j + 128], (free["up"],))
                    free["cx"] = t
                    got["u"] = dve(lambda e: e.tensor_tensor(b4(UP), b4(UP), rows[:, 1, :].unsqueeze(1).broadcast_to([128, 4, 128]), ALU.mult),
                                   t, tok["row1"])

                def c6():
                    mb = misc()
                    t = pe(lambda e: e.matmul(PSB[mb], C("toep"), UP, start=True, stop=True), got["u"], bank_free[mb], inc=True)
                    free["up"] = t
                    got["d"] = bank_free[mb] = act(lambda e: e.activation(DD, PSB[mb], ACT.Copy), t, free["dd"])

                def c7():
                    mb = misc()
                    for j in range(4):
                        o = slice(128 * j, 128 * j + 128)
                        t = pe(lambda e, o=o: e.matmul(PSB[mb][:, o], GM[:, o], DD[:, o], start=True, stop=True), got["gm"], got["d"],
                               bank_free[mb], inc=(j == 3))
                    free["dd"] = free["gm"] = t
                    tok["r", g] = bank_free[mb] = dve(lambda e: e.tensor_tensor(b4(RR), b4(PSB[mb]),
                                                                               rows[:, 0, :].unsqueeze(1).broadcast_to([128, 4, 128]), ALU.add),
                                                      t, free["rr"], tok["row0"])

                return [c0, (c1, 4), c2, c3, c4, (c5, 6), (c6, 4), c7]

            def scale_of(am, inv, t):
                t = dve(lambda e: e.tensor_scalar(am, am, 1e-5, None, ALU.max), t)
                t = dve(lambda e: e.reciprocal(inv, am), t)
                t = dve(lambda e: e.tensor_scalar(am, inv, 127.0, None, ALU.mult), t)
                return t, dve(lambda e: e.reciprocal(inv, am), t)

            def own(g):
                k = g % 2
                bs = slice(4 * g, 4 * g + 4)
                got = {}
                qk, sk = f"qT{k}", f"sc{k}"
                S = sc[:, k]

                def x0():
                    got["s"] = norm_in(X[:, bs, :], 4, xg(g))

                def x1():
                    t = norm_out(got["s"], lambda j: xf[:, 128 * j:128 * j + 128], (free["xf"],))
                    got["s"] = norm_in(b4(xf), 4, (t,), rms=True)

                def x2():
                    got["x"] = norm_out(got["s"], lambda j: xf[:, 128 * j:128 * j + 128])

                def x3():
                    mb = misc()
                    for j in range(4):
                        t = pe(lambda e, j=j: e.transpose(PSB[mb][:, 128 * j:128 * j + 128], xf[:, 128 * j:128 * j + 128], C("ident")), got["x"],
                               bank_free[mb], inc=(j == 3))
                    free["xf"] = t
                    got["h"] = bank_free[mb] = act(lambda e: e.activation(hT, PSB[mb], ACT.Copy, scale=col("g_res")), t, free["hT"])

                def x4():
                    mb = misc()
                    for j in range(4):
                        o = slice(128 * j, 128 * j + 128)
                        t = pe(lambda e, o=o: e.matmul(PSB[mb][:, o], hT[:, o], wsm["W_inT"], start=True, stop=True), got["h"], t_ws,
                               bank_free[mb], inc=(j == 3))
                    free["hT"] = t
                    R = RR
                    t = dve(lambda e: e.tensor_tensor(R, PSB[mb], R, ALU.add), t, tok["r", g])
                    bank_free[mb] = t
                    t = dve(lambda e: e.scalar_tensor_tensor(out=X[:, bs, :], in0=b4(R), scalar=tg[:, 3:4], in1=X[:, bs, :], op0=ALU.mult,
                                                             op1=ALU.add), t, t_tg, *xg(g))
                    free["rr"] = t
                    for j in range(4):
                        x_tok[4 * g + j] = t

                def f0():
                    got["s"] = norm_in(X[:, bs, :], 4, xg(g))

                def f1():
                    t = norm_out(got["s"], lambda j: xf[:, 128 * j:128 * j + 128], (free["xf"],))
                    t = dve(lambda e: e.tensor_reduce(S[:, :, 0:1], b4(xf), AX.X, ALU.max, apply_absolute_value=True), t, free[sk])
                    t, ti = scale_of(S[:, :, 0:1], S[:, :, 1:2], t)
                    ti = dve(lambda e: e.tensor_scalar(S[:, :, 2:3], S[:, :, 1:2], ws[:, 12:13], 0.5, ALU.mult, ALU.mult), ti, tok["ws"])
                    ti = dve(lambda e: e.tensor_scalar(S[:, :, 3:4], S[:, :, 1:2], ws[:, 13:14], None, ALU.mult), ti)
                    got["sc"] = dve(lambda e: e.tensor_tensor(S[:, :, 3:4], S[:, :, 3:4], S[:, :, 2:3], ALU.mult), ti)
                    t = dve(lambda e: e.tensor_tensor(b4(xf), b4(xf), S[:, :, 0:1].broadcast_to([128, 4, 128]), ALU.mult), t)
                    got["q"] = dve(lambda e: e.tensor_scalar(xf, xf, MAGIC, MAGIC + 127.0, ALU.add, ALU.min), t)

                def f2():
                    got["q"] = free["xf"] = act(lambda e: e.activation(qn, xf, ACT.Identity, bias=magic[:, :]), got["q"], tok["magic"], free["qn"])

                def f3():
                    mb = misc()
                    for j in range(4):
                        t = pe(lambda e, j=j: e.transpose(PSB[mb].bitcast(BF16)[:, 128 * j:128 * j + 128], qn[:, 128 * j:128 * j + 128],
                                                          identb[:, :]), got["q"], bank_free[mb], inc=(j == 3))
                    free["qn"] = t
                    got["qT"] = bank_free[mb] = act(lambda e: e.activation(qT[:, k, :], PSB[mb].bitcast(BF16)[:, 0:512], ACT.Copy), t, free[qk])

                def up(j):
                    h, sl = j, f"sil{j % 2}"
                    ba, bb = misc(), misc()
                    ta = pe(lambda e: e.matmul(PSB[ba], qT[:, k, 128 * j:128 * j + 128], wt[:, 0, :], start=True, stop=True), got["qT"],
                            tok["wt"], bank_free[ba], inc=True)
                    tb = pe(lambda e: e.matmul(PSB[bb], qT[:, k, 128 * j:128 * j + 128], wt[:, 1, :], start=True, stop=True), bank_free[bb],
                            inc=True)
                    if j == 3:
                        free[qk] = tb
                    t = act(lambda e: e.activation(AT[:, j % 2, :], PSB[ba], ACT.Tanh, scale=S[:, j, 2:3]), ta, got["sc"], free[sl])
                    t = dve(lambda e: e.scalar_tensor_tensor(out=AT[:, j % 2, :], in0=AT[:, j % 2, :], scalar=1.0, in1=PSB[ba], op0=ALU.add,
                                                             op1=ALU.mult), t)
                    bank_free[ba] = t
                    t = dve(lambda e: e.scalar_tensor_tensor(out=H[h], in0=PSB[bb], scalar=S[:, j, 3:4], in1=AT[:, j % 2, :], op0=ALU.mult,
                                                             op1=ALU.mult), t, tb, h_free[h])
                    bank_free[bb] = free[sl] = t
                    got["m"] = dve(lambda e: e.tensor_reduce(S[:, j, 4:5], H[h], AX.X, ALU.max, apply_absolute_value=True), t)

                def scales():
                    t, ti = scale_of(S[:, :, 4:5], S[:, :, 5:6], got["m"])
                    got["qs"] = t
                    got["so"] = dve(lambda e: e.tensor_scalar(S[:, :, 6:7], S[:, :, 5:6], ws[:, 14:15], tg[:, 7:8], ALU.mult, ALU.mult), ti, t_tg)

                def quant(j):
                    h = j
                    t = act(lambda e: e.activation(H[h], H[h], ACT.Copy, scale=S[:, j, 4:5]), got["qs"])
                    t = dve(lambda e: e.tensor_scalar(H[h], H[h], MAGIC, MAGIC + 127.0, ALU.add, ALU.min), t)
                    got["q2", j] = h_free[h] = pool(lambda e: e.tensor_scalar(q2[:, j, :], H[h], -MAGIC, None, ALU.add), t, q2_free[j])

                def turn(j):
                    mb = misc()
                    for c in range(4):
                        t = pe(lambda e, c=c: e.transpose(PSB[mb].bitcast(BF16)[:, 128 * c:128 * c + 128], q2[:, j, 128 * c:128 * c + 128],
                                                          identb[:, :]), got["q2", j], bank_free[mb], inc=(c == 3))
                    q2_free[j] = t
                    got["T", j] = bank_free[mb] = act(lambda e: e.activation(q2T[:, j, :], PSB[mb].bitcast(BF16)[:, 0:512], ACT.Copy), t,
                                                      q2T_free[j])

                def down(j):
                    mb = misc()
                    b = 4 * g + j
                    for c in range(4):
                        t = pe(lambda e, c=c: e.matmul(PSB[mb][:, 0:128], q2T[:, j, 128 * c:128 * c + 128], wt[:, 2, 128 * c:128 * c + 128],
                                                       start=(c == 0), stop=(c == 3)), got["T", j], bank_free[mb], inc=(c == 3))
                    q2T_free[j] = t
                    t = dve(lambda e: e.scalar_tensor_tensor(out=X[:, b, :], in0=PSB[mb][:, 0:128], scalar=S[:, j, 6:7], in1=X[:, b, :],
                                                             op0=ALU.mult, op1=ALU.add), t, got["so"], x_tok[b])
                    bank_free[mb] = x_tok[b] = t
                    if j == 3:
                        free[sk] = t

                def step(f, j):
                    return lambda: f(j)

                fns = [(x0, 2), (x1, 2), (x2, 4), (x3, 3), (x4, 2)]
                if stop >= 8:
                    fns += [(f0, 2), (f1, 2), (f2, 4), (f3, 3), *((step(up, j), 2) for j in range(4)), scales,
                            *(step(quant, j) for j in range(4)), (step(turn, 0), 2), (step(turn, 1), 2), (step(down, 0), 2),
                            (step(turn, 2), 2), (step(down, 1), 2), (step(turn, 3), 2), (step(down, 2), 2), step(down, 3)]
                return fns

            return setup, context, own, tok

        if stop >= 6:
            L3 = []
            fr["xf"] = fr["gate"] = now()
            half2["now"], half2["free", 0], half2["free", 1] = now(), now(), now()

            def each(n):
                if n == 0 or (n % 8 == 4 and n // 8 + 1 < NG):
                    gates_T((n + 4) // 8)
                if stop >= 7:
                    for ex, at_ in ((0, 2), (1, 3), (2, 4), (3, 5), (7, 9), (4, 10), (5, 11), (6, 12)):
                        if n == at_:
                            halves2(ex)
                    if n % 8 == 5 and n // 8 + 1 < NG:
                        g = n // 8 + 1
                        half2["x", g] = halves(xnr[:, g % 2, :], WBr[:, 512 * g:512 * g + 512], T2[:, 512 * g:512 * g + 512], tt_tok[g], tt_read[g], half2["free", g % 2])
                if n % 8 == 0 and n // 8 + 2 < NG:
                    front2(n // 8 + 2, vraw[:, 0:2, :].rearrange("p a b -> p (a b)"), [r32[:, 1, :], vraw[:, 2, :]])
                if stop >= 7 and n == 6:
                    L3[:] = layer3(now())
                    chain(L3[0], 2)
                if stop >= 7 and n % 8 == 6 and n // 8 < NG:
                    chain(L3[1](n // 8), 2)

            def done(g):
                if stop >= 7:
                    chain(L3[2](g), 1)

            moe(6, up2, lambda x, c: W2[:, 512 * x + 128 * c:512 * x + 128 * c + 128], init2, [xT[:, 0, :], xT[:, 1, :]], each, done)
            while side:
                slot_no[0] += 1
                run_side(1)

        t_o = Q.dma("out", out.rearrange("b t d -> t b d"), X[:, :, :], tuple(x_tok[b] for b in range(B)))
        Q.put("sp", lambda e: None, (t_o,), inc=False)

        blk = ctx.enter_context(nc.Block())
        blk.sync(lambda e: Q.emit("sp", e))
        blk.tensor(lambda e: Q.emit("pe", e))
        blk.vector(lambda e: Q.emit("dve", e))
        blk.scalar(lambda e: Q.emit("act", e))
        blk.gpsimd(lambda e: Q.emit("pool", e))


def layout(inputs):
    n = {k: np.asarray(v) for k, v in inputs.items()}
    c = np.ascontiguousarray

    def kT(w, k):
        return c(w.T.reshape(k, 128, w.shape[0]).transpose(1, 0, 2)).reshape(128, -1)

    def per_part(v):
        return c(v.reshape(-1, 128).T)

    a = {"x": c(n["x"]), "ctx_2048": c(n["ctx_2048"]), "seq": c(n["itok_Bx1_68_817"])}
    a["kT"] = c(n["ctx_2048"][:, :, :128].transpose(2, 0, 1)[by_place(16, 8)]).reshape(128, B * S)
    a["maskT"] = c(n["mask_BxS2_ik0"].T)
    a["lensT"] = c(n["mask_BxS2_if0"].T)
    a["g_xattn"], a["g_ffn"] = c(n["g_xattn"]), c(n["g_ffn"])
    a["L0_xattn_b"] = per_part(n["L0_xattn_b"])
    a["L2_b"] = c(np.broadcast_to(n["L2_xattn_b"].reshape(1, 1), (128, 1)))
    for k in ("w1_s", "w2_s", "h1_s", "h2_s"):
        a[k] = per_part(n["L0_ffn_" + k])
    a["w3_s"] = per_part(n["L0_ffn_w3_s"])
    a["w1T"], a["w2T"] = kT(n["L0_ffn_w1_w"], 1), kT(n["L0_ffn_w2_w"], 1)
    a["h1T"], a["h2T"], a["w3T"] = kT(n["L0_ffn_h1_w"], 4), kT(n["L0_ffn_h2_w"], 4), kT(n["L0_ffn_w3_w"], 4)
    rows = np.concatenate([by_place(16, 8), 128 + by_place(16, 8), 256 + np.arange(128)])
    a["w_qkvT"], a["w_projT"] = c(n["L1_xattn_w_qkv"][rows].T), c(n["L1_xattn_w_proj"].T)
    a["b_proj"] = c(n["L1_xattn_b_proj"])
    a["g1"], a["g2"] = per_part(n["L1_ffn_g1"]), per_part(n["L1_ffn_g2"])
    a["w_down"] = c(n["L1_ffn_w_down"])
    pl = by_place(16, 4)
    sw = pl ^ 1
    a["wqk"] = c(np.concatenate([n["L1_ffn_wq"][:, pl], n["L1_ffn_wk"][:, pl]], 1))
    a["wqk_sw"] = c(np.concatenate([n["L1_ffn_wq"][:, sw], n["L1_ffn_wk"][:, sw]], 1))
    a["wv"], a["w_up"], a["router_w"] = c(n["L1_ffn_wv"]), c(n["L1_ffn_w_up"]), c(n["L1_ffn_router_w"])
    a["m1"] = c(n["L1_ffn_w1"].transpose(1, 0, 2)).reshape(128, 2048)
    a["m3"] = c(n["L1_ffn_w3"].transpose(1, 0, 2)).reshape(128, 2048)
    a["m2"] = c(n["L1_ffn_w2"].reshape(16, 128, 128).transpose(1, 0, 2)).reshape(128, 2048)
    a["gamma"], a["beta"] = per_part(n["L2_ffn_gamma"]), per_part(n["L2_ffn_beta"])
    a["WgT"], a["bg"] = c(n["L2_ffn_Wg"].T), c(n["L2_ffn_bg"])
    a["W1T"] = c(n["L2_ffn_W1"].transpose(2, 0, 1)).reshape(128, 4096)
    a["b1"] = per_part(n["L2_ffn_b1"])
    a["W2T"] = c(n["L2_ffn_W2"].transpose(0, 2, 1).reshape(32, 128, 128).transpose(1, 0, 2)).reshape(128, 4096)
    a["b2"] = c(n["L2_ffn_b2"])
    a["W_inT"], a["b_in"] = c(n["L3_xattn_W_in"].T), c(n["L3_xattn_b_in"])
    a["g_res"], a["g_init"] = per_part(n["L3_xattn_g_res"]), c(n["L3_xattn_g_init"])
    a["qg"], a["qu"], a["qd"] = kT(n["L3_ffn_w_gate"], 1), kT(n["L3_ffn_w_up"], 1), kT(n["L3_ffn_w_down"], 4)
    a["zero"] = np.zeros((24, 2048), np.float32)
    a["cols"] = c(np.concatenate([a.pop(name) for name, _ in COLS], axis=1))
    return a


def kernel(**inputs):
    import concourse.bacc as _bacc
    from concourse.bass_utils import run_bass_kernel_spmd as _run

    nc = _bacc.Bacc("TRN2", target_bir_lowering=False, num_devices=1)
    block, cu = const_block()
    arrays = {f"in_{k}": v for k, v in {**layout(inputs), "cst": block}.items()}
    io = {k[3:]: nc.dram_tensor(k, v.shape, mybir.dt.from_np(v.dtype), kind="ExternalInput").ap() for k, v in arrays.items()}
    out = nc.dram_tensor("out", (B, S, D), F32, kind="ExternalOutput").ap()
    build(nc, io, out, cu)
    r = _run(nc, [arrays], core_ids=[0])
    return r.results[0]["out"]
```
